# Optimizing a Trainium2 kernel written in Bass

```python
import numpy as np
import jax
import jax.numpy as jnp

def _softmax(x, axis=-1):
    return jax.nn.softmax(x, axis=axis)

def _gelu(x):
    return jax.nn.gelu(x, approximate=True)

def _silu(x):
    return jax.nn.silu(x)

def _sigmoid(x):
    return jax.nn.sigmoid(x)

def _layernorm(x, axis=-1, eps=1e-05):
    m = jnp.mean(x, axis=axis, keepdims=True)
    v = jnp.var(x, axis=axis, keepdims=True)
    return (x - m) / jnp.sqrt(v + eps)

def _scatter_add(tgt, idx, src, axis=0):
    return tgt.at[idx].add(src)

def _segment_sum(src, seg, n):
    return jax.ops.segment_sum(src, seg, n)
kernel_name = 'mk_adj_resnorm_d2_adj_r2_fd344b'

def setup_inputs(seed: int=0):
    np.random.seed(seed)
    _w = jnp.asarray

    def _rec_inputs():
        import jax
        import jax.numpy as jnp
        _gk = jax.random.key(seed)
        x = -0.0005207 + 1.001 * jax.random.normal(jax.random.fold_in(_gk, 1), (4096, 128), jnp.float32)
        _a = jax.random.bernoulli(jax.random.fold_in(_gk, 2), 0.000488281, (4096, 4096))
        _a = jnp.logical_or(_a, jnp.swapaxes(_a, -1, -2))
        _a = jnp.logical_or(_a, jnp.eye(4096, dtype=bool))
        _af = _a.astype(jnp.float32)
        _af = _af * jax.random.uniform(jax.random.fold_in(_gk, 3), (4096, 4096), jnp.float32, 0.05, 2.05)
        adj = _af
        return (x, adj)
    x, adj = _rec_inputs()

    def _L0_gnn_setup():
        import jax, jax.numpy as jnp
        import numpy as np
        N = 4096
        D = 128
        CUTOFF = 1.0
        MU = 1.0
        SIGMA = 0.5

        def sensitivity(r, mu, sigma):
            return jnp.exp(-(1.0 / r - 1.0 / mu) ** 2 / (2.0 * sigma * sigma))
        key = jax.random.key(seed)
        k_z, k_d, k_w = jax.random.split(key, 3)
        z = jax.random.normal(k_z, (N, D), dtype=jnp.float32)
        dist_matrix = jax.random.uniform(k_d, (N, N), dtype=jnp.float32) * 2.0 + 0.05
        W = jax.random.normal(k_w, (D, D), dtype=jnp.float32)
        B = jnp.zeros((D,), dtype=jnp.float32)
        return {'z': z, 'dist_matrix': dist_matrix, 'W': W, 'B': B}
    _L0_gnn_all = _L0_gnn_setup()
    _L0_gnn_in = {k: v for k, v in _L0_gnn_all.items() if k in ('W', 'B')}
    del _L0_gnn_all

    def _L1_gnn_setup():
        import jax, jax.numpy as jnp
        import numpy as np
        N, H, HEADS = (2048, 128, 3)
        ALPHA = 0.2
        NEG_INF = -9000000000000000.0

        def _sign_adj(key, n, density):
            k1, k2 = jax.random.split(key)
            mask = jax.random.uniform(k1, (n, n)) < density
            sign = jnp.where(jax.random.uniform(k2, (n, n)) < 0.5, -1.0, 1.0)
            adj = jnp.where(mask, sign, 0.0).astype(jnp.float32)
            idx = jnp.arange(n)
            return adj.at[idx, idx].set(1.0)

        def _gru_cell(x, hstate, Wih, Whh, bih, bhh):
            gi = x @ Wih.T + bih
            gh = hstate @ Whh.T + bhh
            ir, iz, inn = jnp.split(gi, 3, axis=1)
            hr, hz, hn = jnp.split(gh, 3, axis=1)
            r = jax.nn.sigmoid(ir + hr)
            z = jax.nn.sigmoid(iz + hz)
            n = jnp.tanh(inn + r * hn)
            return (1.0 - z) * n + z * hstate

        def _gat_head(h, node_adj, edge_adj, W, a):
            hW = h @ W
            hp = (node_adj > 0).astype(hW.dtype) @ hW
            hm = (node_adj < 0).astype(hW.dtype) @ hW
            e_plus = jax.nn.leaky_relu(jnp.concatenate([hp, hm], axis=1) @ a, ALPHA)[:, 0]
            e_minus = jax.nn.leaky_relu(jnp.concatenate([hm, hp], axis=1) @ a, ALPHA)[:, 0]
            att = jnp.where(edge_adj > 0, e_plus[None, :], NEG_INF)
            att = jnp.where(edge_adj < 0, e_minus[None, :], att)
            att = jax.nn.softmax(att, axis=1)
            return att * edge_adj @ hW
        key = jax.random.key(seed)
        ks = jax.random.split(key, 16)
        std = 0.01
        gain = 1.414
        return {'h': jax.random.normal(ks[0], (N, H), jnp.float32), 'node_adj': _sign_adj(ks[1], N, 0.005), 'edge_adj': _sign_adj(ks[2], N, 0.005), 'gat_W': jax.random.normal(ks[3], (HEADS, H, H), jnp.float32) * (gain / np.sqrt(H, dtype=np.float32)), 'gat_a': jax.random.normal(ks[4], (HEADS, 2 * H, 1), jnp.float32) * 0.1, 'edge_Wih': jax.random.normal(ks[5], (3 * H, H), jnp.float32) * std, 'edge_Whh': jax.random.normal(ks[6], (3 * H, H), jnp.float32) * std, 'edge_bih': jnp.zeros((3 * H,), jnp.float32), 'edge_bhh': jnp.zeros((3 * H,), jnp.float32), 'node_Wih': jax.random.normal(ks[7], (3 * H, H), jnp.float32) * std, 'node_Whh': jax.random.normal(ks[8], (3 * H, H), jnp.float32) * std, 'node_bih': jnp.zeros((3 * H,), jnp.float32), 'node_bhh': jnp.zeros((3 * H,), jnp.float32)}
    _L1_gnn_all = _L1_gnn_setup()
    _L1_gnn_in = {k: v for k, v in _L1_gnn_all.items() if k in ('gat_W', 'gat_a', 'edge_Wih', 'edge_Whh', 'edge_bih', 'edge_bhh', 'node_Wih', 'node_Whh', 'node_bih', 'node_bhh')}
    del _L1_gnn_all
    return {'x': x, 'adj': adj, 'L0_gnn_W': _L0_gnn_in['W'], 'L0_gnn_B': _L0_gnn_in['B'], 'L1_gnn_gat_W': _L1_gnn_in['gat_W'], 'L1_gnn_gat_a': _L1_gnn_in['gat_a'], 'L1_gnn_edge_Wih': _L1_gnn_in['edge_Wih'], 'L1_gnn_edge_Whh': _L1_gnn_in['edge_Whh'], 'L1_gnn_edge_bih': _L1_gnn_in['edge_bih'], 'L1_gnn_edge_bhh': _L1_gnn_in['edge_bhh'], 'L1_gnn_node_Wih': _L1_gnn_in['node_Wih'], 'L1_gnn_node_Whh': _L1_gnn_in['node_Whh'], 'L1_gnn_node_bih': _L1_gnn_in['node_bih'], 'L1_gnn_node_bhh': _L1_gnn_in['node_bhh']}

def reference(x, adj, L0_gnn_W, L0_gnn_B, L1_gnn_gat_W, L1_gnn_gat_a, L1_gnn_edge_Wih, L1_gnn_edge_Whh, L1_gnn_edge_bih, L1_gnn_edge_bhh, L1_gnn_node_Wih, L1_gnn_node_Whh, L1_gnn_node_bih, L1_gnn_node_bhh):
    import jax
    import jax.numpy as jnp

    def _L0_gnn_ref(z, dist_matrix, W, B):
        import jax, jax.numpy as jnp
        import numpy as np
        N = 4096
        D = 128
        CUTOFF = 1.0
        MU = 1.0
        SIGMA = 0.5

        def sensitivity(r, mu, sigma):
            return jnp.exp(-(1.0 / r - 1.0 / mu) ** 2 / (2.0 * sigma * sigma))
        msg = z @ W + B
        sens = sensitivity(dist_matrix, MU, SIGMA)
        weights = jnp.where(dist_matrix < CUTOFF, sens, 0.0)
        return weights @ msg

    def _L1_gnn_ref(h, node_adj, edge_adj, gat_W, gat_a, edge_Wih, edge_Whh, edge_bih, edge_bhh, node_Wih, node_Whh, node_bih, node_bhh):
        import jax, jax.numpy as jnp
        import numpy as np
        N, H, HEADS = (2048, 128, 3)
        ALPHA = 0.2
        NEG_INF = -9000000000000000.0

        def _sign_adj(key, n, density):
            k1, k2 = jax.random.split(key)
            mask = jax.random.uniform(k1, (n, n)) < density
            sign = jnp.where(jax.random.uniform(k2, (n, n)) < 0.5, -1.0, 1.0)
            adj = jnp.where(mask, sign, 0.0).astype(jnp.float32)
            idx = jnp.arange(n)
            return adj.at[idx, idx].set(1.0)

        def _gru_cell(x, hstate, Wih, Whh, bih, bhh):
            gi = x @ Wih.T + bih
            gh = hstate @ Whh.T + bhh
            ir, iz, inn = jnp.split(gi, 3, axis=1)
            hr, hz, hn = jnp.split(gh, 3, axis=1)
            r = jax.nn.sigmoid(ir + hr)
            z = jax.nn.sigmoid(iz + hz)
            n = jnp.tanh(inn + r * hn)
            return (1.0 - z) * n + z * hstate

        def _gat_head(h, node_adj, edge_adj, W, a):
            hW = h @ W
            hp = (node_adj > 0).astype(hW.dtype) @ hW
            hm = (node_adj < 0).astype(hW.dtype) @ hW
            e_plus = jax.nn.leaky_relu(jnp.concatenate([hp, hm], axis=1) @ a, ALPHA)[:, 0]
            e_minus = jax.nn.leaky_relu(jnp.concatenate([hm, hp], axis=1) @ a, ALPHA)[:, 0]
            att = jnp.where(edge_adj > 0, e_plus[None, :], NEG_INF)
            att = jnp.where(edge_adj < 0, e_minus[None, :], att)
            att = jax.nn.softmax(att, axis=1)
            return att * edge_adj @ hW
        dn = jnp.diag(node_adj)
        de = jnp.diag(edge_adj)
        idx = jnp.arange(node_adj.shape[0])
        node_adj_norm = node_adj.at[idx, idx].add(-dn)
        edge_adj_norm = edge_adj.at[idx, idx].add(-de)
        node_support = node_adj_norm @ h
        edge_output = _gru_cell(node_support, h, edge_Wih, edge_Whh, edge_bih, edge_bhh)
        edge_support = _gat_head(h, node_adj_norm, edge_adj_norm, gat_W[0], gat_a[0])
        for i in range(1, HEADS):
            edge_support = edge_support + _gat_head(h, node_adj_norm, edge_adj_norm, gat_W[i], gat_a[i])
        edge_support = edge_support / HEADS
        node_output = _gru_cell(edge_support, h, node_Wih, node_Whh, node_bih, node_bhh)
        return de[:, None] * edge_output + dn[:, None] * node_output
    x = _layernorm(x + _L0_gnn_ref(x, adj, L0_gnn_W, L0_gnn_B), axis=-1)
    x = _layernorm(x + _L1_gnn_ref(x, adj, adj, L1_gnn_gat_W, L1_gnn_gat_a, L1_gnn_edge_Wih, L1_gnn_edge_Whh, L1_gnn_edge_bih, L1_gnn_edge_bhh, L1_gnn_node_Wih, L1_gnn_node_Whh, L1_gnn_node_bih, L1_gnn_node_bhh), axis=-1)
    return x

_drawn_inputs = setup_inputs


def setup_inputs(seed=0):
    import zlib

    import numpy as np

    out = dict(_drawn_inputs(seed))
    spreads = {'L0_gnn_B': (0.0, 0.8),
     'L1_gnn_edge_bih': (0.0, 0.302),
     'L1_gnn_edge_bhh': (0.0, 0.516),
     'L1_gnn_node_bih': (0.0, 0.293),
     'L1_gnn_node_bhh': (0.0, 0.448)}
    factors = {'L1_gnn_gat_a': 26.998, 'L1_gnn_edge_Whh': 2.992, 'L1_gnn_node_Whh': 2.899}
    for name, (base, spread) in spreads.items():
        noise = np.random.default_rng([zlib.crc32(name.encode()), seed]).standard_normal(out[name].shape)
        drawn = base * np.exp(spread * noise) if base else spread * noise
        out[name] = jnp.asarray(drawn.astype(out[name].dtype))
    for name, factor in factors.items():
        out[name] = (out[name] * factor).astype(out[name].dtype)
    return out
```

```python
from contextlib import ExitStack

import concourse.bass as bass
from concourse import mybir

F32 = mybir.dt.float32
BF16 = mybir.dt.bfloat16
FP8 = mybir.dt.float8e4
U32 = mybir.dt.uint32
I32 = mybir.dt.int32
U8 = mybir.dt.uint8
U16 = mybir.dt.uint16
ALU = mybir.AluOpType
ACT = mybir.ActivationFunctionType
AX = mybir.AxisListType.X

P = 128
N = 4096
NT = N // P
SEG = 4
SEGW = N // SEG
CAND = 8 * SEG
SLOTS = 16
HEADS = 3
ROW = P + 3
EPS = 1e-5
BIG = 9e15
FP8_ONE = 56


class Chain:

    def __init__(self, eng, sem):
        self.eng, self.sem, self.n = eng, sem, 0

    def restart(self):
        self.eng.sem_clear(self.sem)
        self.n = 0

    def link(self, ins):
        self.n += 1
        ins.then_inc(self.sem, 1)
        self.eng.wait_ge(self.sem, self.n)


def two_phases(eng, first, second):
    first(0, 0, 0)
    first(1, 1, 0)
    second(0, 0, 0)
    first(2, 0, 1)
    second(1, 1, 0)
    with eng.Fori(1, NT // 2 - 1) as i:
        first(2 * i + 1, 1, i)
        second(2 * i, 0, i)
        first(2 * i + 2, 0, i + 1)
        second(2 * i + 1, 1, i)
    first(NT - 1, 1, NT // 2 - 1)
    second(NT - 2, 0, NT // 2 - 1)
    second(NT - 1, 1, NT // 2 - 1)


def all_tiles(eng, step):
    step(0, 0, 0)
    step(1, 1, 0)
    with eng.Fori(1, NT // 2) as i:
        step(2 * i, 0, i)
        step(2 * i + 1, 1, i)


def spread(ap, axis, shape):
    return ap.unsqueeze(axis).broadcast_to(shape)


def build(nc, d, out):
    x_d, adj_d = d["x"], d["adj"]
    table_d = nc.dram_tensor("node_table", (N, ROW), F32).ap()
    logit_d = nc.dram_tensor("logit_rows", (2 * HEADS, N), F32).ap()
    root = ExitStack()

    with root:
        def sb(name, shape, dt, ctx=root):
            return ctx.enter_context(nc.sbuf_tensor(name, shape, dt))

        def ps(name, shape, dt, ctx=root):
            return ctx.enter_context(nc.psum_tensor(name, shape, dt))

        def sem(name, ctx):
            return root.enter_context(nc.semaphore(name))

        m = {}
        m["ident"] = sb("ident", [P, P], F32)
        m["identb"] = sb("identb", [P, P], BF16)
        m["offdiag"] = sb("offdiag", [P, P], BF16)
        m["ones"] = sb("ones", [P, P], F32)
        m["rowid"] = sb("rowid", [P, NT], F32)
        m["segoff"] = sb("segoff", [P, CAND], F32)
        m["idx_all"] = sb("idx_all", [P, NT, SLOTS], U16)
        m["val_all"] = sb("val_all", [P, NT, SLOTS], F32)
        m["diag"] = sb("diag", [P, NT], F32)
        m["wsum"] = sb("wsum", [P, NT], F32)
        m["cnt"] = sb("cnt", [P, NT], F32)
        m["full"] = sb("full", [P, NT], F32)
        m["signs"] = sb("signs", [P, NT, SEG], F32)
        m["flag"] = sb("flag", [1, 1], I32)
        m["yT"] = sb("yT", [P, NT, P], F32)
        m["maskT"] = sb("maskT", [P, NT, N], U8)
        with ExitStack() as ctx:
            constants(nc, ctx, sb, sem, m)
        with ExitStack() as ctx:
            extract(nc, ctx, sb, ps, sem, m, x_d, adj_d)
        unfit = nc.values_load(m["flag"][0:1, 0:1], min_val=0, max_val=1)
        with nc.If(unfit != 0):
            with ExitStack() as ctx:
                weights_dense(nc, ctx, sb, ps, sem, m, x_d, adj_d)
        with ExitStack() as ctx:
            w = load_weights(nc, root, ctx, sb, ps, sem, m, d)
        with ExitStack() as ctx:
            first_norm(nc, ctx, sb, ps, sem, m, w, x_d, table_d)
        unfit = nc.values_load(m["flag"][0:1, 0:1], min_val=0, max_val=1)
        with nc.If(unfit != 0):
            with ExitStack() as ctx:
                logits_dense(nc, ctx, sb, ps, sem, m, w, adj_d, logit_d)
            with ExitStack() as ctx:
                attention_dense(nc, ctx, sb, ps, sem, m, w, adj_d, table_d, logit_d)
        with nc.Else():
            with ExitStack() as ctx:
                logits(nc, ctx, sb, ps, sem, m, w, table_d)
            with ExitStack() as ctx:
                attention(nc, ctx, sb, ps, sem, m, w, table_d)
        with ExitStack() as ctx:
            last_norm(nc, ctx, sb, ps, sem, m, w, out)


def constants(nc, ctx, sb, sem, m):
    ri = sb("rowid_i", [P, NT], I32, ctx)
    si = sb("segoff_i", [P, CAND], I32, ctx)
    s_iota = sem("s_iota", ctx)
    s_fill = sem("s_fill", ctx)
    block = ctx.enter_context(nc.Block())

    @block.gpsimd
    def _(pool):
        pool.iota(ri[:, :], pattern=[[P, NT]], base=1, channel_multiplier=1)
        pool.iota(si[:, :].rearrange("p (g e) -> p g e", e=8), pattern=[[SEGW, SEG], [0, 8]], base=1,
                  channel_multiplier=0).then_inc(s_iota, 1)
        pool.memset(m["ones"][:, :], 1.0)
        pool.memset(m["offdiag"][:, :], 1.0)
        pool.memset(m["identb"][:, :], 0.0)
        pool.memset(m["ident"][:, :], 0.0).then_inc(s_fill, 1)
        pool.wait_ge(s_fill, 1)
        for t, op, fill in (("ident", ALU.not_equal, 1.0), ("identb", ALU.not_equal, 1.0),
                            ("offdiag", ALU.not_equal, 0.0)):
            pool.affine_select(out=m[t][:, :], in_=m[t][:, :], compare_op=op, fill=fill, base=0,
                               pattern=[[-1, P]], channel_multiplier=1)

    @block.vector
    def _(dve):
        dve.wait_ge(s_iota, 1)
        dve.tensor_copy(m["rowid"][:, :], ri[:, :])
        dve.tensor_copy(m["segoff"][:, :], si[:, :])


def extract(nc, ctx, sb, ps, sem, m, x_d, adj_d):
    A = sb("A", [P, 2, N], F32, ctx)
    sg = sb("sg", [P, 2, SEGW], BF16, ctx)
    G = sb("G", [P, 2, SLOTS, P], F32, ctx)
    xt = sb("xt", [P, 2, P], F32, ctx)
    top = sb("top", [P, CAND], F32, ctx)
    pos = sb("pos", [P, CAND], U32, ctx)
    posf = sb("posf", [P, CAND], F32, ctx)
    there = sb("there", [P, CAND], F32, ctx)
    key = sb("key", [P, CAND], F32, ctx)
    key2 = sb("key2", [P, CAND], F32, ctx)
    skey = sb("skey", [P, SLOTS], F32, ctx)
    own = sb("own", [P, SLOTS], F32, ctx)
    eq = sb("eq", [P, SLOTS, CAND], F32, ctx)
    dtmp = sb("dtmp", [P, P], F32, ctx)
    idx = sb("idx", [P, 2, SLOTS], U32, ctx)
    r = sb("r", [P, 2, SLOTS + 1], F32, ctx)
    z = sb("z", [P, 2, SLOTS + 1], F32, ctx)
    q = sb("q", [P, 2, SLOTS + 1], F32, ctx)
    e = sb("e", [P, 2, SLOTS + 1], F32, ctx)
    wt = sb("wt", [P, SLOTS + 1], F32, ctx)
    bad = sb("bad", [P, 3, NT], F32, ctx)
    sgs = sb("sgs", [P, NT], F32, ctx)
    badrow = sb("badrow", [P, 1], F32, ctx)
    psT = ps("psT", [P, 2, SEGW], BF16, ctx)
    psY = ps("psY", [P, 2, 512], F32, ctx)
    psF = ps("psF", [P, 512], F32, ctx)

    s_adj = [sem(f"s_adj{b}", ctx) for b in range(2)]
    s_x = [sem(f"s_x{b}", ctx) for b in range(2)]
    s_gath = [sem(f"s_gath{b}", ctx) for b in range(2)]
    s_off = sem("s_off", ctx)
    s_scan = sem("s_scan", ctx)
    s_sign = sem("s_sign", ctx)
    s_turn = sem("s_turn", ctx)
    s_mask = sem("s_mask", ctx)
    s_idx = sem("s_idx", ctx)
    s_q = sem("s_q", ctx)
    s_exp = sem("s_exp", ctx)
    s_prod = sem("s_prod", ctx)
    s_sum = sem("s_sum", ctx)
    s_y = sem("s_y", ctx)
    s_v = sem("s_v", ctx)
    s_gv, s_gp, s_ga = sem("s_gate_v", ctx), sem("s_gate_p", ctx), sem("s_gate_a", ctx)
    s_gt, s_gs = sem("s_gate_t", ctx), sem("s_gate_s", ctx)
    s_bad, s_cntd, s_w = sem("s_bad", ctx), sem("s_cntd", ctx), sem("s_w", ctx)
    block = ctx.enter_context(nc.Block())

    @block.sync
    def _(sp):
        def load(t, b, h):
            if not (isinstance(t, int) and t < 2):
                sp.wait_ge(s_scan, t - 1)
                sp.sem_inc(s_gs, 1)
                sp.wait_ge(s_sign, SEG * (t - 1))
                sp.sem_inc(s_gs, 1)
            sp.dma_start(A[:, b, :], adj_d[bass.ds(t * P, P), :]).then_inc(s_adj[b], 16)
            if not (isinstance(t, int) and t < 2):
                sp.wait_ge(s_sum, t - 1)
                sp.sem_inc(s_gs, 1)
            sp.dma_start(xt[:, b, :], x_d[bass.ds(t * P, P), :]).then_inc(s_x[b], 16)
        all_tiles(sp, load)

    @block.gpsimd
    def _(pool):
        def gather(t, b, h):
            pool.wait_ge(s_idx, t + 1)
            if not (isinstance(t, int) and t < 2):
                pool.wait_ge(s_sum, t - 1)
            pool.sem_inc(s_gp, 1)
            for s in range(SLOTS):
                pool.indirect_dma_start(G[:, b, s, :], None, x_d[:, :],
                                        bass.IndirectOffsetOnAxis(ap=idx[:, b, s:s + 1], axis=0))\
                    .then_inc(s_gath[b], 16)
        all_tiles(pool, gather)

    @block.vector
    def _(dve):
        ch = Chain(dve, s_v)

        def scan(t, b, h):
            ch.restart()
            dve.wait_ge(s_adj[b], 16 * (h + 1))
            dve.sem_inc(s_gv, 1)
            blk = A[:, b, bass.ds(t * P, P)]
            ch.link(dve.tensor_tensor(dtmp[:, :], blk, m["ident"][:, :], ALU.mult))
            dve.tensor_reduce(r[:, b, SLOTS:SLOTS + 1], dtmp[:, :], AX, ALU.add)
            ch.link(dve.tensor_tensor(blk, blk, m["offdiag"][:, :], ALU.mult))
            dve.sem_inc(s_off, 1)
            for g in range(SEG):
                last = dve.max(top[:, 8 * g:8 * g + 8], A[:, b, g * SEGW:(g + 1) * SEGW])
            ch.link(last)
            for g in range(SEG):
                last = dve.max_index(pos[:, 8 * g:8 * g + 8], top[:, 8 * g:8 * g + 8],
                                     A[:, b, g * SEGW:(g + 1) * SEGW])
            ch.link(last)
            dve.sem_inc(s_scan, 1)
            dve.tensor_scalar(there[:, :], top[:, :], 0.0, None, ALU.is_gt)
            ch.link(dve.tensor_tensor(posf[:, :], pos[:, :], m["segoff"][:, :], ALU.add))
            dve.tensor_reduce(m["cnt"][:, bass.ds(t, 1)], there[:, :], AX, ALU.add)
            dve.tensor_reduce(m["full"][:, bass.ds(t, 1)], top[:, 7::8], AX, ALU.max)
            ch.link(dve.tensor_tensor(key[:, :], posf[:, :], there[:, :], ALU.mult))
            ch.link(dve.max(skey[:, 0:8], key[:, :]))
            ch.link(dve.match_replace(key2[:, :], skey[:, 0:8], key[:, :], 0.0))
            ch.link(dve.max(skey[:, 8:16], key2[:, :]))
            shape = [P, SLOTS, CAND]
            dve.tensor_scalar(own[:, :], skey[:, :], 0.0, m["rowid"][:, bass.ds(t, 1)], ALU.is_equal, ALU.mult)
            ch.link(dve.tensor_tensor(eq[:, :, :], spread(skey[:, :], 2, shape), spread(key[:, :], 1, shape),
                                      ALU.is_equal))
            dve.scalar_tensor_tensor(idx[:, b, :], skey[:, :], -1.0, own[:, :], ALU.add, ALU.add)\
                .then_inc(s_idx, 1)
            ch.link(dve.tensor_tensor(eq[:, :, :], eq[:, :, :], spread(top[:, :], 1, shape), ALU.mult))
            ch.link(dve.tensor_reduce(r[:, b, 0:SLOTS], eq[:, :, :], AX, ALU.add))
            dve.tensor_copy(m["idx_all"][:, t, :], idx[:, b, :])
            dve.tensor_copy(m["val_all"][:, t, :], r[:, b, 0:SLOTS])
            dve.tensor_copy(m["diag"][:, bass.ds(t, 1)], r[:, b, SLOTS:SLOTS + 1])
            ch.link(dve.tensor_scalar(z[:, b, :], r[:, b, :], 0.0, 2.0, ALU.is_equal, ALU.mult))
            ch.link(dve.tensor_tensor(z[:, b, :], z[:, b, :], r[:, b, :], ALU.add))
            ch.link(dve.reciprocal(q[:, b, :], z[:, b, :]))
            ch.link(dve.tensor_scalar(q[:, b, :], q[:, b, :], -1.0, None, ALU.add))
            dve.tensor_tensor(q[:, b, :], q[:, b, :], q[:, b, :], ALU.mult).then_inc(s_q, 1)

        def weigh(t, b, h):
            dve.wait_ge(s_exp, t + 1)
            dve.wait_ge(s_gath[b], 16 * SLOTS * (h + 1))
            dve.wait_ge(s_x[b], 16 * (h + 1))
            dve.sem_inc(s_gv, 1)
            ch.link(dve.scalar_tensor_tensor(wt[:, :], z[:, b, :], 1.0, e[:, b, :], ALU.is_lt, ALU.mult))
            dve.tensor_reduce(m["wsum"][:, bass.ds(t, 1)], wt[:, :], AX, ALU.add)
            dve.tensor_scalar(xt[:, b, :], xt[:, b, :], wt[:, SLOTS:SLOTS + 1], None, ALU.mult)
            dve.tensor_tensor(G[:, b, :, :], G[:, b, :, :], spread(wt[:, 0:SLOTS], 2, [P, SLOTS, P]),
                              ALU.mult).then_inc(s_prod, 1)

        two_phases(dve, scan, weigh)
        ch.restart()
        dve.wait_ge(s_mask, NT * SEG)
        ch.link(dve.tensor_reduce(sgs[:, :], m["signs"][:, :, :], AX, ALU.add))
        dve.tensor_tensor(bad[:, 0, :], sgs[:, :], m["cnt"][:, :], ALU.not_equal)
        dve.tensor_scalar(bad[:, 1, :], m["cnt"][:, :], float(SLOTS), None, ALU.is_gt)
        ch.link(dve.tensor_scalar(bad[:, 2, :], m["full"][:, :], 0.0, None, ALU.is_gt))
        dve.tensor_reduce(badrow[:, :], bad[:, :, :].rearrange("p a t -> p (a t)"), AX, ALU.add)\
            .then_inc(s_bad, 1)
        dve.wait_ge(s_cntd, 1)
        dve.tensor_scalar(m["flag"][:, :], psF[0:1, 0:1], 1.0, None, ALU.min)

    @block.scalar
    def _(act):
        def signs(t, b, h):
            for g in range(SEG):
                if g == 0:
                    act.wait_ge(s_off, t + 1)
                if not (isinstance(t, int) and t == 0 and g < 2):
                    act.wait_ge(s_turn, SEG * t + g - 1)
                act.sem_inc(s_ga, 1)
                act.activation(sg[:, g % 2, :], A[:, b, g * SEGW:(g + 1) * SEGW], ACT.Sign,
                               accum_out=m["signs"][:, t, g:g + 1]).then_inc(s_sign, 1)
                if not (isinstance(t, int) and t == 0 and g < 1):
                    keep(t, g - 1)
            
        def keep(t, g):
            if g < 0:
                t, g = t - 1, SEG - 1
            act.wait_ge(s_turn, SEG * t + g + 1)
            act.sem_inc(s_ga, 1)
            act.activation(m["maskT"][:, 8 * g:8 * g + 8, bass.ds(t * P, P)],
                           psT[:, g % 2, :].rearrange("p (j i) -> p j i", i=P), ACT.Copy,
                           scale=float(FP8_ONE)).then_inc(s_mask, 1)

        def expo(t, b, h):
            act.wait_ge(s_q, t + 1)
            act.sem_inc(s_ga, 1)
            act.activation(e[:, b, :], q[:, b, :], ACT.Exp, scale=-2.0).then_inc(s_exp, 1)
            act.wait_ge(s_sum, t + 1)
            act.sem_inc(s_ga, 1)
            act.activation(m["yT"][:, t, :], psY[:, b, 0:P], ACT.Copy).then_inc(s_y, 1)

        two_phases(act, signs, expo)
        keep(NT - 1, SEG - 1)

    @block.tensor
    def _(pe):
        def turn(t, b, h):
            for g in range(SEG):
                pe.wait_ge(s_sign, SEG * t + g + 1)
                if not (isinstance(t, int) and t == 0 and g < 2):
                    pe.wait_ge(s_mask, SEG * t + g - 1)
                pe.sem_inc(s_gt, 1)
                for j in range(8):
                    last = pe.transpose(psT[:, g % 2, j * P:(j + 1) * P], sg[:, g % 2, j * P:(j + 1) * P],
                                        m["identb"][:, :])
                last.then_inc(s_turn, 1)

        def total(t, b, h):
            pe.wait_ge(s_prod, t + 1)
            if not (isinstance(t, int) and t < 2):
                pe.wait_ge(s_y, t - 1)
            pe.sem_inc(s_gt, 1)
            for s in range(SLOTS):
                pe.matmul(psY[:, b, 0:P], G[:, b, s, :], m["ident"][:, :], start=(s == 0), stop=False)
            pe.matmul(psY[:, b, 0:P], xt[:, b, :], m["ident"][:, :], start=False, stop=True)\
                .then_inc(s_sum, 1)

        two_phases(pe, turn, total)
        pe.wait_ge(s_bad, 1)
        pe.matmul(psF[0:1, 0:1], badrow[:, :], m["ones"][:, 0:1], start=True, stop=True).then_inc(s_cntd, 1)


def load_weights(nc, root, ctx, sb, ps, sem, m, d):
    w = {}
    w["W0"] = sb("W0", [P, P], F32, root)
    w["B0"] = sb("B0", [P, P], F32, root)
    w["gatW"] = sb("gatW", [P, HEADS, P], F32, root)
    w["ih"] = sb("ihT", [P, 2, 3 * P], F32, root)
    w["hh"] = sb("hhT", [P, 2, 3 * P], F32, root)
    w["bias"] = sb("bias", [1, 2, 4 * P], F32, root)
    w["WA"] = sb("WA", [P, 2 * HEADS], F32, root)
    w["V"] = sb("V", [P, NT, 2 * HEADS], F32, root)
    w["H"] = sb("H", [P, NT, P], F32, root)
    w["mv"] = sb("mv_all", [P, NT, 2], F32, root)
    w["rstd"] = sb("rstd", [P, NT], F32, root)
    a6 = sb("a6", [2 * HEADS, P], F32, ctx)
    a6T = sb("a6T", [P, 2 * HEADS], F32, ctx)
    gwT = sb("gwT", [P, HEADS, P], F32, ctx)
    raw = sb("raw", [P, 4, 3, P], F32, ctx)
    bi = sb("bi", [1, 2, 3 * P], F32, ctx)
    bh = sb("bh", [1, 2, 3 * P], F32, ctx)
    pw = ps("pw", [P, 4, 512], F32, ctx)
    pa = ps("pa", [P, 512], F32, ctx)
    pg = ps("pg", [P, 512], F32, ctx)
    pwa = ps("pwa", [P, 512], F32, ctx)
    s_w, s_t, s_c, s_o = sem("s_load", ctx), sem("s_turned", ctx), sem("s_copied", ctx), sem("s_wa", ctx)
    s_b = sem("s_biascopy", ctx)
    block = ctx.enter_context(nc.Block())
    names = [("L1_gnn_edge_Wih", "ih", 0), ("L1_gnn_node_Wih", "ih", 1),
             ("L1_gnn_edge_Whh", "hh", 0), ("L1_gnn_node_Whh", "hh", 1)]
    loads = [(w["W0"][:, :], d["L0_gnn_W"]), (w["B0"][:, :], d["L0_gnn_B"].partition_broadcast(P)),
             (w["gatW"][:, :, :], d["L1_gnn_gat_W"].rearrange("k c e -> c k e")),
             (a6[:, :], d["L1_gnn_gat_a"].rearrange("k (g e) o -> (k g) (e o)", g=2)),
             (bi[:, 0, :], d["L1_gnn_edge_bih"].rearrange("(o n) -> o n", o=1)),
             (bi[:, 1, :], d["L1_gnn_node_bih"].rearrange("(o n) -> o n", o=1)),
             (bh[:, 0, :], d["L1_gnn_edge_bhh"].rearrange("(o n) -> o n", o=1)),
             (bh[:, 1, :], d["L1_gnn_node_bhh"].rearrange("(o n) -> o n", o=1))]
    loads += [(raw[:, i, :, :], d[n].rearrange("(g p) c -> p g c", p=P)) for i, (n, _, _) in enumerate(names)]

    @block.sync
    def _(sp):
        for dst, src in loads:
            sp.dma_start(dst, src).then_inc(s_w, 16)

    @block.tensor
    def _(pe):
        pe.wait_ge(s_w, 16 * len(loads))
        for i in range(4):
            for g in range(3):
                pe.transpose(pw[:, i, g * P:(g + 1) * P], raw[:, i, g, :], m["ident"][:, :])
        for k in range(HEADS):
            pe.transpose(pg[:, k * P:(k + 1) * P], w["gatW"][:, k, :], m["ident"][:, :])
        pe.transpose(pa[:, 0:2 * HEADS], a6[:, :], m["ident"][0:2 * HEADS, 0:2 * HEADS]).then_inc(s_t, 1)
        pe.wait_ge(s_c, 1)
        for k in range(HEADS):
            last = pe.matmul(pwa[:, 2 * k:2 * k + 2], gwT[:, k, :], a6T[:, 2 * k:2 * k + 2],
                             start=True, stop=True)
        last.then_inc(s_o, 1)

    @block.vector
    def _(dve):
        dve.wait_ge(s_t, 1)
        dve.tensor_copy(a6T[:, :], pa[:, 0:2 * HEADS])
        dve.tensor_copy(gwT[:, :, :], pg[:, 0:3 * P].rearrange("p (k c) -> p k c", k=HEADS)).then_inc(s_c, 1)
        for i, (_, key, j) in enumerate(names):
            dve.tensor_copy(w[key][:, j, :], pw[:, i, 0:3 * P])
        dve.tensor_tensor(w["bias"][:, :, 0:2 * P], bi[:, :, 0:2 * P], bh[:, :, 0:2 * P], ALU.add)
        dve.tensor_copy(w["bias"][:, :, 2 * P:3 * P], bi[:, :, 2 * P:3 * P])
        dve.tensor_copy(w["bias"][:, :, 3 * P:4 * P], bh[:, :, 2 * P:3 * P])
        dve.wait_ge(s_o, 1)
        dve.tensor_copy(w["WA"][:, :].rearrange("p (g k) -> p k g", g=2),
                        pwa[:, 0:2 * HEADS].rearrange("p (k g) -> p k g", g=2))
    return w


def finish_stats(dve, act, w, ch, s_var, s_sd):
    ch.link(dve.tensor_scalar(w["rstd"][:, :], w["mv"][:, :, 1], EPS, None, ALU.add))
    dve.sem_inc(s_var, 1)
    dve.wait_ge(s_sd, 1)
    ch.link(dve.reciprocal(w["rstd"][:, :], w["rstd"][:, :]))


def first_norm(nc, ctx, sb, ps, sem, m, w, x_d, table_d):
    hb = sb("h_row", [P, 2, P], F32, ctx)
    yb = sb("yb", [P, 2, P], F32, ctx)
    xb = sb("xb", [P, 2, P], F32, ctx)
    hT = sb("hT", [P, 2, P], F32, ctx)
    st = sb("st", [P, 6], F32, ctx)
    mv = sb("mv", [P, 2], F32, ctx)
    psM = ps("psM", [P, 2, 512], F32, ctx)
    psH = ps("psH", [P, 2, 512], F32, ctx)
    psV = ps("psV", [P, 2, 512], F32, ctx)
    s_x = [sem(f"s_x2{b}", ctx) for b in range(2)]
    s_yb = sem("s_yb", ctx)
    s_mm = sem("s_mm", ctx)
    s_pre = sem("s_pre", ctx)
    s_var, s_sd = sem("s_var", ctx), sem("s_sd", ctx)
    s_h = sem("s_h", ctx)
    s_ht = sem("s_ht", ctx)
    s_htc = sem("s_htc", ctx)
    s_v = sem("s_v2", ctx)
    s_vc = sem("s_vc", ctx)
    s_tab = [sem(f"s_tab{b}", ctx) for b in range(2)]
    s_ch = sem("s_ch2", ctx)
    s_gv, s_gt, s_ga, s_gs = (sem(n, ctx) for n in ("s_gv2", "s_gt2", "s_ga2", "s_gs2"))
    block = ctx.enter_context(nc.Block())

    @block.sync
    def _(sp):
        def load(t, b, h):
            if not (isinstance(t, int) and t < 2):
                sp.wait_ge(s_pre, t - 1)
                sp.sem_inc(s_gs, 1)
            sp.dma_start(xb[:, b, :], x_d[bass.ds(t * P, P), :]).then_inc(s_x[b], 16)

        def store(t, b, h):
            sp.wait_ge(s_h, t + 1)
            sp.sem_inc(s_gs, 1)
            sp.dma_start(table_d[bass.ds(t * P, P), 0:P], hb[:, b, :]).then_inc(s_tab[b], 16)
        all_tiles(sp, load)
        all_tiles(sp, store)
        for b in range(2):
            sp.wait_ge(s_tab[b], 16 * NT // 2)

    @block.scalar
    def _(act):
        def fetch(t, b, h):
            if not (isinstance(t, int) and t < 2):
                act.wait_ge(s_mm, t - 1)
                act.sem_inc(s_ga, 1)
            act.activation(yb[:, b, :], m["yT"][:, t, :], ACT.Copy).then_inc(s_yb, 1)
        all_tiles(act, fetch)
        act.wait_ge(s_var, 1)
        act.activation(w["rstd"][:, :], w["rstd"][:, :], ACT.Sqrt).then_inc(s_sd, 1)

        def copy(t, b, h):
            act.wait_ge(s_ht, t + 1)
            if not (isinstance(t, int) and t < 2):
                act.wait_ge(s_v, t - 1)
            act.sem_inc(s_ga, 1)
            act.activation(hT[:, b, :], psH[:, b, 0:P], ACT.Copy).then_inc(s_htc, 1)
        all_tiles(act, copy)

    @block.tensor
    def _(pe):
        def product(t, b, h):
            pe.wait_ge(s_yb, t + 1)
            if not (isinstance(t, int) and t < 2):
                pe.wait_ge(s_pre, t - 1)
            pe.sem_inc(s_gt, 1)
            pe.matmul(psM[:, b, 0:P], yb[:, b, :], w["W0"][:, :], start=True, stop=True).then_inc(s_mm, 1)
        all_tiles(pe, product)

        def turn(t, b, h):
            pe.wait_ge(s_h, t + 1)
            if not (isinstance(t, int) and t < 2):
                pe.wait_ge(s_htc, t - 1)
            pe.sem_inc(s_gt, 1)
            pe.transpose(psH[:, b, 0:P], hb[:, b, :], m["ident"][:, :]).then_inc(s_ht, 1)
            pe.wait_ge(s_htc, t + 1)
            if not (isinstance(t, int) and t < 2):
                pe.wait_ge(s_vc, t - 1)
            pe.sem_inc(s_gt, 1)
            pe.matmul(psV[:, b, 0:2 * HEADS], hT[:, b, :], w["WA"][:, :], start=True, stop=True)\
                .then_inc(s_v, 1)
        all_tiles(pe, turn)

    @block.vector
    def _(dve):
        ch = Chain(dve, s_ch)

        def rows(t, b, h):
            ch.restart()
            dve.wait_ge(s_x[b], 16 * (h + 1))
            dve.sem_inc(s_gv, 1)
            ch.link(dve.scalar_tensor_tensor(xb[:, b, :], w["B0"][:, :], m["wsum"][:, bass.ds(t, 1)],
                                             xb[:, b, :], ALU.mult, ALU.add))
            dve.wait_ge(s_mm, t + 1)
            dve.sem_inc(s_gv, 1)
            ch.link(dve.tensor_tensor(w["H"][:, t, :], psM[:, b, 0:P], xb[:, b, :], ALU.add))
            dve.sem_inc(s_pre, 1)
            ch.link(dve.bn_stats(st[:, :], w["H"][:, t, :]))
            ch.link(dve.bn_aggr(mv[:, :], st[:, :]))
            ch.link(dve.tensor_copy(w["mv"][:, t, :], mv[:, :]))
        all_tiles(dve, rows)
        finish_stats(dve, None, w, ch, s_var, s_sd)

        def normalise(t, b, h):
            if not (isinstance(t, int) and t < 2):
                dve.wait_ge(s_tab[b], 16 * h)
                dve.wait_ge(s_ht, t - 1)
                dve.sem_inc(s_gv, 1)
            dve.tensor_scalar(hb[:, b, :], w["H"][:, t, :], w["mv"][:, t, 0:1],
                              w["rstd"][:, bass.ds(t, 1)], ALU.subtract, ALU.mult).then_inc(s_h, 1)

        def values(t, b, h):
            dve.wait_ge(s_v, t + 1)
            dve.sem_inc(s_gv, 1)
            dve.tensor_copy(w["V"][:, t, :], psV[:, b, 0:2 * HEADS]).then_inc(s_vc, 1)
        two_phases(dve, normalise, values)


def logits(nc, ctx, sb, ps, sem, m, w, table_d):
    M9 = 3 * HEADS
    W = 512
    rest = sb("rest", [P, NT, HEADS], F32, ctx)
    parts = sb("parts", [P, NT, M9], BF16, ctx)
    U = sb("U", [M9, N], F32, ctx)
    comb = sb("comb", [M9, HEADS], F32, ctx)
    lg = sb("lg", [P, NT, HEADS], F32, ctx)
    lk = sb("lk", [P, NT, HEADS], F32, ctx)
    psU = ps("psU", [P, 2, W], F32, ctx)
    psL = ps("psL", [P, NT, HEADS], F32, ctx)
    s_comb, s_c3 = sem("s_comb", ctx), sem("s_ch3", ctx)
    s_parts, s_u, s_uc, s_l, s_e, s_out = (sem(n, ctx) for n in
                                           ("s_parts", "s_u", "s_uc", "s_l", "s_e", "s_logit"))
    block = ctx.enter_context(nc.Block())

    @block.gpsimd
    def _(pool):
        pool.memset(comb[:, :], 0.0).then_inc(s_comb, 1)
        for j in range(3):
            pool.wait_ge(s_comb, j + 1)
            pool.affine_select(out=comb[:, :], in_=comb[:, :], compare_op=ALU.not_equal, fill=1.0,
                               base=-HEADS * j, pattern=[[-1, HEADS]], channel_multiplier=1).then_inc(s_comb, 1)

    @block.vector
    def _(dve):
        ch = Chain(dve, s_c3)
        ch.link(dve.tensor_copy(rest[:, :, :], w["V"][:, :, 0:HEADS]))
        for j in range(3):
            part = parts[:, :, j * HEADS:(j + 1) * HEADS]
            ch.link(dve.tensor_copy(part, rest[:, :, :]))
            if j < 2:
                ch.link(dve.tensor_tensor(rest[:, :, :], rest[:, :, :], part, ALU.subtract))
        dve.sem_inc(s_parts, 1)
        dve.wait_ge(s_l, 1)
        ch.link(dve.tensor_copy(lg[:, :, :], psL[:, :, :]))
        dve.scalar_tensor_tensor(lk[:, :, :], lg[:, :, :], 0.2, lg[:, :, :], ALU.mult, ALU.max).then_inc(s_e, 1)

    @block.tensor
    def _(pe):
        pe.wait_ge(s_parts, 1)
        for c in range(N // W):
            if c >= 2:
                pe.wait_ge(s_uc, c - 1)
            for j in range(NT):
                last = pe.matmul(psU[0:M9, c % 2, :], parts[:, j, :],
                                 m["maskT"][:, j, c * W:(c + 1) * W].bitcast(FP8),
                                 start=(j == 0), stop=(j == NT - 1))
            last.then_inc(s_u, 1)
        pe.wait_ge(s_comb, 4)
        pe.wait_ge(s_uc, N // W)
        for t in range(NT):
            last = pe.matmul(psL[:, t, :], U[:, t * P:(t + 1) * P], comb[:, :], start=True, stop=True)
        last.then_inc(s_l, 1)

    @block.scalar
    def _(act):
        for c in range(N // W):
            act.wait_ge(s_u, c + 1)
            act.activation(U[:, c * W:(c + 1) * W], psU[0:M9, c % 2, :], ACT.Copy).then_inc(s_uc, 1)

    @block.sync
    def _(sp):
        sp.wait_ge(s_e, 1)
        sp.dma_start(table_d.rearrange("(t p) c -> p t c", p=P)[:, :, P:P + HEADS], lk[:, :, :],
                     allow_slow_non_contiguous=True).then_inc(s_out, 16)
        sp.wait_ge(s_out, 16)


def carve(region):
    at = [0]

    def place(*shape, dt=F32):
        n = 4
        for x in shape:
            n *= x
        ap = region[:, at[0]:at[0] + n].bitcast(dt)
        at[0] += n
        assert at[0] <= region.shape[1]
        if len(shape) == 2:
            return ap.rearrange("p (a b) -> p a b", b=shape[1])
        if len(shape) == 3:
            return ap.rearrange("p (a b c) -> p a b c", b=shape[1], c=shape[2])
        if len(shape) == 4:
            return ap.rearrange("p (a b c e) -> p a b c e", b=shape[1], c=shape[2], e=shape[3])
        return ap
    return place


class Gru:

    def __init__(self, tag, ctx, place, ps, sem, m, w, hb, supT, s_h, s_supc, s_gv, s_ga, s_gt):
        self.m, self.w, self.hb, self.supT = m, w, hb, supT
        self.s_h, self.s_supc, self.s_gv, self.s_ga, self.s_gt = s_h, s_supc, s_gv, s_ga, s_gt
        self.hT = place(2, P)
        self.nsT = place(2, P)
        self.g1 = place(2, 2 * P)
        self.nn = place(2, P)
        self.nt = place(2, P)
        self.df = place(2, P)
        self.oo = place(P)
        self.st = place(6)
        self.mv = place(2)
        self.psH = ps("psH3" + tag, [P, 512], F32, ctx)
        self.psN = ps("psN3" + tag, [P, 512], F32, ctx)
        self.psG = ps("psG" + tag, [P, 2, 4 * P], F32, ctx)
        self.s_ht = sem("s_ht3" + tag, ctx)
        self.s_htc = sem("s_htc3" + tag, ctx)
        self.s_ns = sem("s_ns" + tag, ctx)
        self.s_nsc = sem("s_nsc" + tag, ctx)
        self.s_gru = sem("s_gru" + tag, ctx)
        self.s_g1 = sem("s_g1" + tag, ctx)
        self.s_nn = sem("s_nn" + tag, ctx)
        self.s_nt = sem("s_nt" + tag, ctx)
        self.s_res = sem("s_res" + tag, ctx)

    def turn_h(self, pe, t, b, landed):
        pe.wait_ge(self.s_h[b], landed)
        if not (isinstance(t, int) and t < 1):
            pe.wait_ge(self.s_htc, t)
        pe.sem_inc(self.s_gt, 1)
        pe.transpose(self.psH[:, 0:P], self.hb[:, b, :], self.m["ident"][:, :]).then_inc(self.s_ht, 1)

    def copy_h(self, act, t, b):
        act.wait_ge(self.s_ht, t + 1)
        act.sem_inc(self.s_ga, 1)
        act.activation(self.hT[:, b, :], self.psH[:, 0:P], ACT.Copy).then_inc(self.s_htc, 1)

    def products(self, pe, t, b):
        w, supT, psG = self.w, self.supT, self.psG
        pe.wait_ge(self.s_supc, t + 1)
        pe.sem_inc(self.s_gt, 1)
        for k in range(HEADS):
            last = pe.matmul(self.psN[:, 0:P], w["gatW"][:, k, :], supT[:, b, k + 1, :],
                             start=(k == 0), stop=(k == HEADS - 1))
        last.then_inc(self.s_ns, 1)
        if not (isinstance(t, int) and t < 1):
            pe.wait_ge(self.s_res, t)
        pe.wait_ge(self.s_htc, t + 1)
        pe.sem_inc(self.s_gt, 1)
        for j in range(2):
            pe.matmul(psG[:, j, :], self.m["ones"][0:1, :], w["bias"][:, j, :], start=True, stop=False)
            pe.matmul(psG[:, j, 0:2 * P], self.hT[:, b, :], w["hh"][:, j, 0:2 * P], start=False, stop=False)
            pe.matmul(psG[:, j, 3 * P:4 * P], self.hT[:, b, :], w["hh"][:, j, 2 * P:3 * P],
                      start=False, stop=False)
            if j == 1:
                pe.wait_ge(self.s_nsc, t + 1)
                pe.sem_inc(self.s_gt, 1)
            last = pe.matmul(psG[:, j, 0:3 * P], self.nsT[:, b, :] if j else supT[:, b, 0, :],
                             w["ih"][:, j, :], start=False, stop=True)
        last.then_inc(self.s_gru, 1)

    def tanhs(self, act, t, b):
        act.wait_ge(self.s_ns, t + 1)
        act.sem_inc(self.s_ga, 1)
        act.activation(self.nsT[:, b, :], self.psN[:, 0:P], ACT.Copy, scale=1.0 / HEADS).then_inc(self.s_nsc, 1)
        act.wait_ge(self.s_gru, t + 1)
        act.sem_inc(self.s_ga, 1)
        act.activation(self.g1[:, :, :], self.psG[:, :, 0:2 * P], ACT.Tanh, scale=0.5).then_inc(self.s_g1, 1)
        act.wait_ge(self.s_nn, t + 1)
        act.sem_inc(self.s_ga, 1)
        act.activation(self.nt[:, :, :], self.nn[:, :, :], ACT.Tanh).then_inc(self.s_nt, 1)

    def gates(self, dve, ch, t, b, landed):
        m, w, hb, psG = self.m, self.w, self.hb, self.psG
        g1, nn, nt, df, oo, st, mv = self.g1, self.nn, self.nt, self.df, self.oo, self.st, self.mv
        dve.wait_ge(self.s_g1, t + 1)
        dve.wait_ge(self.s_h[b], landed)
        dve.sem_inc(self.s_gv, 1)
        ch.link(dve.scalar_tensor_tensor(nn[:, :, :], g1[:, :, 0:P], 1.0, psG[:, :, 3 * P:4 * P],
                                         ALU.add, ALU.mult))
        ch.link(dve.scalar_tensor_tensor(nn[:, :, :], nn[:, :, :], 0.5, psG[:, :, 2 * P:3 * P],
                                         ALU.mult, ALU.add))
        dve.sem_inc(self.s_nn, 1)
        dve.wait_ge(self.s_nt, t + 1)
        dve.sem_inc(self.s_gv, 1)
        ch.link(dve.tensor_tensor(df[:, :, :], spread(hb[:, b, :], 1, [P, 2, P]), nt[:, :, :], ALU.subtract))
        ch.link(dve.scalar_tensor_tensor(df[:, :, :], g1[:, :, P:2 * P], 1.0, df[:, :, :], ALU.add, ALU.mult))
        ch.link(dve.scalar_tensor_tensor(df[:, :, :], df[:, :, :], 0.5, nt[:, :, :], ALU.mult, ALU.add))
        ch.link(dve.tensor_tensor(oo[:, :], df[:, 0, :], df[:, 1, :], ALU.add))
        ch.link(dve.scalar_tensor_tensor(w["H"][:, t, :], oo[:, :], m["diag"][:, bass.ds(t, 1)], hb[:, b, :],
                                         ALU.mult, ALU.add))
        dve.sem_inc(self.s_res, 1)
        ch.link(dve.bn_stats(st[:, :], w["H"][:, t, :]))
        ch.link(dve.bn_aggr(mv[:, :], st[:, :]))
        ch.link(dve.tensor_copy(w["mv"][:, t, :], mv[:, :]))


def attention(nc, ctx, sb, ps, sem, m, w, table_d):
    place = carve(m["maskT"][:, :, :].rearrange("p a b -> p (a b)"))
    K4 = HEADS + 1
    G = place(2, SLOTS, ROW)
    prod = place(2, K4 * SLOTS, P)
    idx = place(2, SLOTS, dt=U32)
    coef = place(2, K4, SLOTS)
    L = place(2, HEADS, SLOTS)
    E = place(2, HEADS, SLOTS)
    mk = place(SLOTS)
    nb = place(SLOTS)
    mx = place(HEADS)
    den = place(HEADS)
    hb = place(2, P)
    supT = place(2, K4, P)
    psS = ps("psS", [P, 2, K4, P], F32, ctx)

    s_h = [sem(f"s_h3{b}", ctx) for b in range(2)]
    s_gath = [sem(f"s_gath3{b}", ctx) for b in range(2)]
    names = ("s_idx3", "s_lgt", "s_p", "s_coef", "s_prodv", "s_proda", "s_sup", "s_supc", "s_ch4",
             "s_gv4", "s_gp4", "s_ga4", "s_gt4", "s_gs4")
    (s_idx, s_lgt, s_p, s_coef, s_prodv, s_proda, s_sup, s_supc, s_ch,
     s_gv, s_gp, s_ga, s_gt, s_gs) = (sem(n, ctx) for n in names)
    gru = Gru("", ctx, place, ps, sem, m, w, hb, supT, s_h, s_supc, s_gv, s_ga, s_gt)
    s_res = gru.s_res
    block = ctx.enter_context(nc.Block())

    @block.sync
    def _(sp):
        def load(t, b, h):
            if not (isinstance(t, int) and t < 2):
                sp.wait_ge(s_res, t - 1)
                sp.sem_inc(s_gs, 1)
            sp.dma_start(hb[:, b, :], table_d[bass.ds(t * P, P), 0:P]).then_inc(s_h[b], 16)
        all_tiles(sp, load)

    @block.gpsimd
    def _(pool):
        def gather(t, b, h):
            pool.wait_ge(s_idx, t + 1)
            if not (isinstance(t, int) and t < 2):
                pool.wait_ge(s_prodv, t - 1)
                pool.wait_ge(s_proda, t - 1)
            pool.sem_inc(s_gp, 1)
            for s in range(SLOTS):
                pool.indirect_dma_start(G[:, b, s, :], None, table_d[:, :],
                                        bass.IndirectOffsetOnAxis(ap=idx[:, b, s:s + 1], axis=0))\
                    .then_inc(s_gath[b], 16)
        all_tiles(pool, gather)

    @block.vector
    def _(dve):
        ch = Chain(dve, s_ch)

        def columns(t, b):
            dve.tensor_copy(idx[:, b, :], m["idx_all"][:, t, :]).then_inc(s_idx, 1)

        def attend(t, b, h):
            ch.restart()
            if not (isinstance(t, int) and t == NT - 1):
                columns(t + 1, 1 - b)
            V = coef[:, b, 0, :]
            shape = [P, HEADS, SLOTS]
            ch.link(dve.tensor_copy(V, m["val_all"][:, t, :]))
            ch.link(dve.tensor_scalar(mk[:, :], V, 0.0, None, ALU.is_gt))
            ch.link(dve.tensor_scalar(nb[:, :], mk[:, :], -1.0, BIG, ALU.add, ALU.mult))
            dve.wait_ge(s_gath[b], 16 * SLOTS * (h + 1))
            dve.sem_inc(s_gv, 1)
            lb = L[:, b, :, :]
            gl = G[:, b, :, P:P + HEADS].rearrange("p s k -> p k s")
            ch.link(dve.tensor_tensor(lb, gl, spread(mk[:, :], 1, shape), ALU.mult))
            ch.link(dve.tensor_tensor(lb, lb, spread(nb[:, :], 1, shape), ALU.add))
            ch.link(dve.tensor_reduce(mx[:, :], lb, AX, ALU.max))
            ch.link(dve.tensor_tensor(lb, lb, spread(mx[:, :], 2, shape), ALU.subtract))
            dve.sem_inc(s_lgt, 1)
            dve.wait_ge(s_p, t + 1)
            dve.sem_inc(s_gv, 1)
            eb = E[:, b, :, :]
            ch.link(dve.tensor_reduce(den[:, :], eb, AX, ALU.add))
            ch.link(dve.reciprocal(den[:, :], den[:, :]))
            ch.link(dve.tensor_tensor(eb, eb, spread(den[:, :], 2, shape), ALU.mult))
            ch.link(dve.tensor_tensor(coef[:, b, 1:K4, :], eb, spread(V, 1, shape), ALU.mult))
            dve.sem_inc(s_coef, 1)
            if not (isinstance(t, int) and t < 2):
                dve.wait_ge(s_sup, t - 1)
                dve.sem_inc(s_gv, 1)
            for k in range(1, K4):
                last = dve.tensor_tensor(prod[:, b, k * SLOTS:(k + 1) * SLOTS, :], G[:, b, :, 0:P],
                                         spread(coef[:, b, k, :], 2, [P, SLOTS, P]), ALU.mult)
            last.then_inc(s_prodv, 1)

        def recur(t, b, h):
            gru.gates(dve, ch, t, b, 16 * (h + 1))

        columns(0, 0)
        two_phases(dve, attend, recur)

    @block.scalar
    def _(act):
        def weigh(t, b, h):
            act.wait_ge(s_lgt, t + 1)
            act.sem_inc(s_ga, 1)
            act.activation(E[:, b, :, :], L[:, b, :, :], ACT.Exp).then_inc(s_p, 1)
            if not (isinstance(t, int) and t < 2):
                act.wait_ge(s_sup, t - 1)
            act.wait_ge(s_coef, t + 1)
            act.sem_inc(s_ga, 1)
            for s in range(SLOTS):
                last = act.activation(prod[:, b, s, :], G[:, b, s, 0:P], ACT.Copy, scale=coef[:, b, 0, s:s + 1])
            last.then_inc(s_proda, 1)

        def move(t, b, h):
            gru.copy_h(act, t, b)
            act.wait_ge(s_sup, t + 1)
            act.sem_inc(s_ga, 1)
            act.activation(supT[:, b, :, :], psS[:, b, :, :], ACT.Copy).then_inc(s_supc, 1)
            gru.tanhs(act, t, b)

        two_phases(act, weigh, move)

    @block.tensor
    def _(pe):
        def tile(t, b, h):
            gru.turn_h(pe, t, b, 16 * (h + 1))
            pe.wait_ge(s_proda, t + 1)
            pe.wait_ge(s_prodv, t + 1)
            pe.sem_inc(s_gt, 1)
            for k in range(K4):
                for s in range(SLOTS):
                    last = pe.matmul(psS[:, b, k, :], prod[:, b, k * SLOTS + s, :], m["ident"][:, :],
                                     start=(s == 0), stop=(s == SLOTS - 1))
            last.then_inc(s_sup, 1)
            gru.products(pe, t, b)
        all_tiles(pe, tile)


def tile_by_tile(eng, step):
    step(0)
    with eng.Fori(1, NT) as t:
        step(t)


class DenseSum:

    def __init__(self, tag, ctx, place, ps, sem, m, s_ga, s_gt):
        self.m, self.s_ga, self.s_gt = m, s_ga, s_gt
        self.T = place(4, P)
        self.psT = ps("psT_" + tag, [P, 4, P], F32, ctx)
        self.s_turned = sem("s_turned_" + tag, ctx)
        self.s_copied = sem("s_copied_" + tag, ctx)

    def turn(self, pe, src, n, multiply):
        for c in range(NT // 4):
            for j in range(4):
                at = (4 * c + j) * P
                last = pe.transpose(self.psT[:, j, :], src[:, at:at + P], self.m["ident"][:, :])
            last.then_inc(self.s_turned, 1)
            pe.wait_ge(self.s_copied, n * (NT // 4) + c + 1)
            pe.sem_inc(self.s_gt, 1)
            for j in range(4):
                last = multiply(4 * c + j, self.T[:, j, :], c + j == 0, 4 * c + j == NT - 1)
        return last

    def copy(self, act, n):
        for c in range(NT // 4):
            act.wait_ge(self.s_turned, n * (NT // 4) + c + 1)
            act.sem_inc(self.s_ga, 1)
            act.activation(self.T[:, :, :], self.psT[:, :, :], ACT.Copy).then_inc(self.s_copied, 1)


def weights_dense(nc, ctx, sb, ps, sem, m, x_d, adj_d):
    place = carve(m["maskT"][:, :, :].rearrange("p a b -> p (a b)"))
    A, B, X = place(N), place(N), place(NT, P)
    s_x, s_a, s_q, s_e, s_wt, s_sum, s_y, s_ch, s_gs, s_gv, s_ga, s_gt = (
        sem(n + "_wd", ctx) for n in ("x", "a", "q", "e", "wt", "sum", "y", "ch", "gs", "gv", "ga", "gt"))
    ds = DenseSum("wd", ctx, place, ps, sem, m, s_ga, s_gt)
    psY = ps("psY_d", [P, 512], F32, ctx)
    block = ctx.enter_context(nc.Block())

    @block.gpsimd
    def _(pool):
        pool.dma_start(X[:, :, :], x_d.rearrange("(t p) c -> p t c", p=P)).then_inc(s_x, 16)

    @block.sync
    def _(sp):
        def load(t):
            if not isinstance(t, int):
                sp.wait_ge(s_y, t)
                sp.sem_inc(s_gs, 1)
            sp.dma_start(A[:, :], adj_d[bass.ds(t * P, P), :]).then_inc(s_a, 16)
        tile_by_tile(sp, load)

    @block.vector
    def _(dve):
        ch = Chain(dve, s_ch)

        def weigh(t):
            ch.restart()
            dve.wait_ge(s_a, 16 * (t + 1))
            dve.sem_inc(s_gv, 1)
            ch.link(dve.tensor_scalar(B[:, :], A[:, :], 0.0, 2.0, ALU.is_equal, ALU.mult))
            ch.link(dve.tensor_tensor(A[:, :], A[:, :], B[:, :], ALU.add))
            ch.link(dve.reciprocal(B[:, :], A[:, :]))
            ch.link(dve.tensor_scalar(B[:, :], B[:, :], -1.0, None, ALU.add))
            dve.tensor_tensor(B[:, :], B[:, :], B[:, :], ALU.mult).then_inc(s_q, 1)
            dve.wait_ge(s_e, t + 1)
            dve.sem_inc(s_gv, 1)
            ch.link(dve.scalar_tensor_tensor(A[:, :], A[:, :], 1.0, B[:, :], ALU.is_lt, ALU.mult))
            ch.link(dve.tensor_reduce(m["wsum"][:, bass.ds(t, 1)], A[:, :], AX, ALU.add))
            dve.sem_inc(s_wt, 1)
        tile_by_tile(dve, weigh)

    @block.scalar
    def _(act):
        def step(t):
            act.wait_ge(s_q, t + 1)
            act.sem_inc(s_ga, 1)
            act.activation(B[:, :], B[:, :], ACT.Exp, scale=-2.0).then_inc(s_e, 1)
            ds.copy(act, t)
            act.wait_ge(s_sum, t + 1)
            act.sem_inc(s_ga, 1)
            act.activation(m["yT"][:, t, :], psY[:, 0:P], ACT.Copy).then_inc(s_y, 1)
        tile_by_tile(act, step)

    @block.tensor
    def _(pe):
        pe.wait_ge(s_x, 16)

        def step(t):
            pe.wait_ge(s_wt, t + 1)
            if not isinstance(t, int):
                pe.wait_ge(s_y, t)
            pe.sem_inc(s_gt, 1)
            ds.turn(pe, A, t, lambda j, block_t, first, last: pe.matmul(
                psY[:, 0:P], X[:, j, :], block_t, start=first, stop=last)).then_inc(s_sum, 1)
        tile_by_tile(pe, step)


def logits_dense(nc, ctx, sb, ps, sem, m, w, adj_d, logit_d):
    place = carve(m["maskT"][:, :, :].rearrange("p a b -> p (a b)"))
    A, Mp, Mm = place(N), place(N), place(N)
    K2 = 2 * HEADS
    up, e6, l6 = place(2, K2), place(K2), place(K2)
    rows = place(N)
    s_a, s_m, s_u, s_e6, s_t, s_tc, s_out, s_ch, s_gs, s_gv, s_ga, s_gt = (
        sem(n + "_ld", ctx) for n in ("a", "m", "u", "e6", "t", "tc", "out", "ch", "gs", "gv", "ga", "gt"))
    ds = DenseSum("ld", ctx, place, ps, sem, m, s_ga, s_gt)
    psU = ps("psU_d", [P, 2, 512], F32, ctx)
    psR = ps("psR_d", [P, 512], F32, ctx)
    block = ctx.enter_context(nc.Block())

    @block.sync
    def _(sp):
        def load(t):
            if not isinstance(t, int):
                sp.wait_ge(s_tc, t)
                sp.sem_inc(s_gs, 1)
            sp.dma_start(A[:, :], adj_d[bass.ds(t * P, P), :]).then_inc(s_a, 16)
        tile_by_tile(sp, load)
        sp.wait_ge(s_tc, NT)
        sp.dma_start(logit_d, rows[0:K2, :]).then_inc(s_out, 16)
        sp.wait_ge(s_out, 16)

    @block.vector
    def _(dve):
        ch = Chain(dve, s_ch)

        def step(t):
            ch.restart()
            dve.wait_ge(s_a, 16 * (t + 1))
            dve.sem_inc(s_gv, 1)
            blk = A[:, bass.ds(t * P, P)]
            ch.link(dve.tensor_tensor(blk, blk, m["offdiag"][:, :], ALU.mult))
            dve.tensor_scalar(Mp[:, :], A[:, :], 0.0, None, ALU.is_gt)
            dve.tensor_scalar(Mm[:, :], A[:, :], 0.0, None, ALU.is_lt).then_inc(s_m, 1)
            dve.wait_ge(s_u, t + 1)
            dve.sem_inc(s_gv, 1)
            ch.link(dve.tensor_copy(up[:, :, :], psU[:, :, 0:K2]))
            ch.link(dve.tensor_tensor(e6[:, 0:HEADS], up[:, 0, 0:HEADS], up[:, 1, HEADS:K2], ALU.add))
            ch.link(dve.tensor_tensor(e6[:, HEADS:K2], up[:, 1, 0:HEADS], up[:, 0, HEADS:K2], ALU.add))
            dve.scalar_tensor_tensor(l6[:, :], e6[:, :], 0.2, e6[:, :], ALU.mult, ALU.max).then_inc(s_e6, 1)
        tile_by_tile(dve, step)

    @block.scalar
    def _(act):
        def step(t):
            ds.copy(act, 2 * t)
            ds.copy(act, 2 * t + 1)
            act.wait_ge(s_t, t + 1)
            act.sem_inc(s_ga, 1)
            act.activation(rows[0:K2, bass.ds(t * P, P)], psR[0:K2, 0:P], ACT.Copy).then_inc(s_tc, 1)
        tile_by_tile(act, step)

    @block.tensor
    def _(pe):
        def step(t):
            pe.wait_ge(s_m, t + 1)
            pe.sem_inc(s_gt, 1)
            for n, mask in ((0, Mp), (1, Mm)):
                last = ds.turn(pe, mask, 2 * t + n, lambda j, block_t, first, last, n=n: pe.matmul(
                    psU[:, n, 0:K2], block_t, w["V"][:, j, :], start=first, stop=last))
            last.then_inc(s_u, 1)
            pe.wait_ge(s_e6, t + 1)
            if not isinstance(t, int):
                pe.wait_ge(s_tc, t)
            pe.sem_inc(s_gt, 1)
            pe.transpose(psR[0:K2, 0:P], l6[:, :], m["ident"][:, :]).then_inc(s_t, 1)
        tile_by_tile(pe, step)


def attention_dense(nc, ctx, sb, ps, sem, m, w, adj_d, table_d, logit_d):
    place = carve(m["maskT"][:, :, :].rearrange("p a b -> p (a b)"))
    K4 = HEADS + 1
    A, Mp, L, Ep, Em = (place(N) for _ in range(5))
    Mm = place(N)
    hall = place(NT, P)
    place = carve(m["yT"][:, :, :].rearrange("p a b -> p (a b)").bitcast(U8))
    hb = place(2, P)
    supT = place(2, K4, P)
    mx, den = place(1), place(1)
    psS = ps("psS_d", [P, K4, P], F32, ctx)
    s_all, s_h0, s_a, s_el, s_m, s_lk, s_lg, s_ex, s_s, s_sum, s_supc, s_ch, s_gs, s_gv, s_ga, s_gt = (
        sem(n + "_ad", ctx) for n in ("all", "h0", "a", "el", "m", "lk", "lg", "ex", "s", "sum", "supc", "ch",
                                      "gs", "gv", "ga", "gt"))
    ds = DenseSum("ad", ctx, place, ps, sem, m, s_ga, s_gt)
    gru = Gru("d", ctx, place, ps, sem, m, w, hb, supT, [s_h0], s_supc, s_gv, s_ga, s_gt)
    block = ctx.enter_context(nc.Block())

    @block.sync
    def _(sp):
        sp.dma_start(hall[:, :, :], table_d.rearrange("(t p) c -> p t c", p=P)[:, :, 0:P]).then_inc(s_all, 16)

        def load(t):
            if not isinstance(t, int):
                sp.wait_ge(gru.s_res, t)
                sp.sem_inc(s_gs, 1)
            sp.dma_start(A[:, :], adj_d[bass.ds(t * P, P), :]).then_inc(s_a, 16)
            sp.dma_start(hb[:, 0, :], table_d[bass.ds(t * P, P), 0:P]).then_inc(s_h0, 16)
            for k in range(HEADS):
                if not (isinstance(t, int) and k == 0):
                    sp.wait_ge(s_lk, HEADS * t + k)
                    sp.sem_inc(s_gs, 1)
                sp.dma_start(Ep[:, :], logit_d[k, :].partition_broadcast(P)).then_inc(s_el, 16)
                sp.dma_start(Em[:, :], logit_d[HEADS + k, :].partition_broadcast(P)).then_inc(s_el, 16)
        tile_by_tile(sp, load)

    @block.vector
    def _(dve):
        ch = Chain(dve, s_ch)

        def step(t):
            ch.restart()
            dve.wait_ge(s_a, 16 * (t + 1))
            dve.sem_inc(s_gv, 1)
            blk = A[:, bass.ds(t * P, P)]
            ch.link(dve.tensor_tensor(blk, blk, m["offdiag"][:, :], ALU.mult))
            dve.tensor_scalar(Mp[:, :], A[:, :], 0.0, None, ALU.is_gt)
            ch.link(dve.tensor_scalar(Mm[:, :], A[:, :], 0.0, None, ALU.is_lt))
            dve.sem_inc(s_m, 1)
            for k in range(HEADS):
                if k:
                    dve.wait_ge(s_sum, K4 * t + k + 1)
                dve.wait_ge(s_el, 32 * (HEADS * t + k + 1))
                dve.sem_inc(s_gv, 1)
                ch.link(dve.memset(L[:, :], -BIG))
                ch.link(dve.copy_predicated(L[:, :], Mp[:, :].bitcast(I32), Ep[:, :]))
                ch.link(dve.copy_predicated(L[:, :], Mm[:, :].bitcast(I32), Em[:, :]))
                dve.sem_inc(s_lk, 1)
                ch.link(dve.tensor_reduce(mx[:, :], L[:, :], AX, ALU.max))
                ch.link(dve.tensor_scalar(L[:, :], L[:, :], mx[:, :], None, ALU.subtract))
                dve.sem_inc(s_lg, 1)
                dve.wait_ge(s_ex, HEADS * t + k + 1)
                dve.sem_inc(s_gv, 1)
                ch.link(dve.reciprocal(den[:, :], den[:, :]))
                ch.link(dve.scalar_tensor_tensor(L[:, :], L[:, :], den[:, :], A[:, :], ALU.mult, ALU.mult))
                dve.sem_inc(s_s, 1)
            gru.gates(dve, ch, t, 0, 16 * (t + 1))
        tile_by_tile(dve, step)

    @block.scalar
    def _(act):
        def step(t):
            gru.copy_h(act, t, 0)
            ds.copy(act, K4 * t)
            for k in range(HEADS):
                act.wait_ge(s_lg, HEADS * t + k + 1)
                act.sem_inc(s_ga, 1)
                act.activation(L[:, :], L[:, :], ACT.Exp, accum_out=den[:, :]).then_inc(s_ex, 1)
                ds.copy(act, K4 * t + k + 1)
            act.wait_ge(s_sum, K4 * (t + 1))
            act.sem_inc(s_ga, 1)
            act.activation(supT[:, 0, :, :], psS[:, :, :], ACT.Copy).then_inc(s_supc, 1)
            gru.tanhs(act, t, 0)
        tile_by_tile(act, step)

    @block.tensor
    def _(pe):
        pe.wait_ge(s_all, 16)

        def step(t):
            gru.turn_h(pe, t, 0, 16 * (t + 1))
            for k in range(K4):
                if k == 0:
                    pe.wait_ge(s_m, t + 1)
                else:
                    pe.wait_ge(s_s, HEADS * t + k)
                pe.sem_inc(s_gt, 1)
                ds.turn(pe, L if k else A, K4 * t + k, lambda j, block_t, first, last, k=k: pe.matmul(
                    psS[:, k, :], hall[:, j, :], block_t, start=first, stop=last)).then_inc(s_sum, 1)
            gru.products(pe, t, 0)
        tile_by_tile(pe, step)


def last_norm(nc, ctx, sb, ps, sem, m, w, out):
    s_ch, s_var, s_sd, s_n, s_out = (sem(n, ctx) for n in ("s_ch5", "s_var5", "s_sd5", "s_n5", "s_out"))
    CH = 8
    block = ctx.enter_context(nc.Block())

    @block.scalar
    def _(act):
        act.wait_ge(s_var, 1)
        act.activation(w["rstd"][:, :], w["rstd"][:, :], ACT.Sqrt).then_inc(s_sd, 1)

    @block.vector
    def _(dve):
        ch = Chain(dve, s_ch)
        finish_stats(dve, None, w, ch, s_var, s_sd)
        with dve.Fori(0, NT) as t:
            dve.tensor_scalar(w["H"][:, t, :], w["H"][:, t, :], w["mv"][:, t, 0:1],
                              w["rstd"][:, bass.ds(t, 1)], ALU.subtract, ALU.mult).then_inc(s_n, 1)

    @block.sync
    def _(sp):
        rows = out.rearrange("(t p) c -> p t c", p=P)
        for g in range(NT // CH):
            sp.wait_ge(s_n, CH * (g + 1))
            sp.dma_start(rows[:, CH * g:CH * (g + 1), :], w["H"][:, CH * g:CH * (g + 1), :]).then_inc(s_out, 16)
        sp.wait_ge(s_out, 16 * (NT // CH))


NAMES = ["x", "adj", "L0_gnn_W", "L0_gnn_B", "L1_gnn_gat_W", "L1_gnn_gat_a", "L1_gnn_edge_Wih", "L1_gnn_edge_Whh",
         "L1_gnn_edge_bih", "L1_gnn_edge_bhh", "L1_gnn_node_Wih", "L1_gnn_node_Whh", "L1_gnn_node_bih",
         "L1_gnn_node_bhh"]


def kernel(**inputs):
    import numpy as _np
    import concourse.bacc as _bacc
    from concourse.bass_utils import run_bass_kernel_spmd as _run

    nc = _bacc.Bacc("TRN2", target_bir_lowering=False, num_devices=1)
    arrays, tensors = {}, {}
    for name in NAMES:
        a = _np.ascontiguousarray(inputs[name])
        arrays[f"in_{name}"] = a
        tensors[name] = nc.dram_tensor(f"in_{name}", a.shape, mybir.dt.from_np(a.dtype), kind="ExternalInput").ap()
    out = nc.dram_tensor("out", (N, P), F32, kind="ExternalOutput").ap()
    build(nc, tensors, out)
    result = _run(nc, [arrays], core_ids=[0])
    return result.results[0]["out"]
```

```python
from contextlib import ExitStack

import concourse.bass as bass
from concourse import mybir

F32 = mybir.dt.float32
BF16 = mybir.dt.bfloat16
FP8 = mybir.dt.float8e4
U32 = mybir.dt.uint32
I32 = mybir.dt.int32
U8 = mybir.dt.uint8
ALU = mybir.AluOpType
ACT = mybir.ActivationFunctionType
AX = mybir.AxisListType.X

P = 128
N = 4096
NT = N // P
SEG = 4
SEGW = N // SEG
CAND = 8 * SEG
SLOTS = 16
CHUNKS = 5
EDGES = CHUNKS * P
RANK, KEY, VAL, BASE, OWN = 0, CAND, 2 * CAND, 3 * CAND, 3 * CAND + 1
PAY = OWN + 1
RKEY, RROW, RSLOT, RVAL = 0, 1, 2, 3
REC = 4
RECS = REC * CHUNKS + 1
HEADS = 3
ROW = P + 3
EPS = 1e-5
BIG = 9e15
FP8_ONE = 56


class Chain:

    def __init__(self, eng, sem):
        self.eng, self.sem, self.n = eng, sem, 0

    def restart(self):
        self.eng.sem_clear(self.sem)
        self.n = 0

    def mark(self, ins):
        self.n += 1
        ins.then_inc(self.sem, 1)

    def wait(self):
        self.eng.wait_ge(self.sem, self.n)

    def link(self, ins):
        self.mark(ins)
        self.wait()


def two_phases(eng, first, second):
    first(0, 0, 0)
    first(1, 1, 0)
    second(0, 0, 0)
    first(2, 0, 1)
    second(1, 1, 0)
    with eng.Fori(1, NT // 2 - 1) as i:
        first(2 * i + 1, 1, i)
        second(2 * i, 0, i)
        first(2 * i + 2, 0, i + 1)
        second(2 * i + 1, 1, i)
    first(NT - 1, 1, NT // 2 - 1)
    second(NT - 2, 0, NT // 2 - 1)
    second(NT - 1, 1, NT // 2 - 1)


def all_tiles(eng, step):
    step(0, 0, 0)
    step(1, 1, 0)
    with eng.Fori(1, NT // 2) as i:
        step(2 * i, 0, i)
        step(2 * i + 1, 1, i)


def early(t, n):
    return isinstance(t, int) and t < n


def over(t, n):
    return isinstance(t, int) and t >= n


def all_steps(eng, step):
    for t in range(4):
        step(t, t % 2, t // 2)
    with eng.Fori(2, NT // 2) as i:
        step(2 * i, 0, i)
        step(2 * i + 1, 1, i)
    step(NT, 0, NT // 2)
    step(NT + 1, 1, NT // 2)


def all_steps_of_four(eng, step, before_last=0):
    for t in range(4):
        step(t, t, 0)
    with eng.Fori(1, (NT - before_last) // 4) as i:
        for j in range(4):
            step(4 * i + j, j, i)
    for t in range(NT - before_last, NT + 2):
        step(t, t % 4, t // 4)


def spread(ap, axis, shape):
    return ap.unsqueeze(axis).broadcast_to(shape)


def build(nc, d, out):
    x_d, adj_d = d["x"], d["adj"]
    table_d = nc.dram_tensor("node_table", (N, ROW), F32).ap()
    logit_d = nc.dram_tensor("logit_rows", (2 * HEADS, N), F32).ap()
    root = ExitStack()

    with root:
        def sb(name, shape, dt, ctx=root):
            return ctx.enter_context(nc.sbuf_tensor(name, shape, dt))

        def ps(name, shape, dt, ctx=root):
            return ctx.enter_context(nc.psum_tensor(name, shape, dt))

        def sem(name, ctx):
            return root.enter_context(nc.semaphore(name))

        m = {}
        m["gates"] = [sem("gate_" + e, root) for e in ("vector", "pool", "scalar", "tensor", "sync")]
        m["ident"] = sb("ident", [P, P], F32)
        m["identb"] = sb("identb", [P, P], BF16)
        m["offdiag"] = sb("offdiag", [P, P], BF16)
        m["ones"] = sb("ones", [P, 1], F32)
        m["segoff"] = sb("segoff", [P, CAND], F32)
        m["iota"] = sb("iota", [P, EDGES], F32)
        m["edge1"] = sb("edge1", [P, CHUNKS], F32)
        m["before"] = sb("before", [P, P], F32)
        m["own"] = sb("own", [P, 1], F32)
        m["rec_all"] = sb("rec_all", [P, NT, RECS], F32)
        m["ends"] = sb("ends", [P, NT], F32)
        m["wsum"] = sb("wsum", [P, NT], F32)
        m["cnt"] = sb("cnt", [P, NT], F32)
        m["full"] = sb("full", [P, NT], F32)
        m["signs"] = sb("signs", [P, NT, SEG], F32)
        m["flag"] = sb("flag", [1, 1], I32)
        m["yT"] = sb("yT", [P, NT, P], F32)
        m["maskT"] = sb("maskT", [P, NT, N], U8)
        with ExitStack() as ctx:
            constants(nc, ctx, sb, sem, m)
        with ExitStack() as ctx:
            extract(nc, ctx, sb, ps, sem, m, x_d, adj_d)
        unfit = nc.values_load(m["flag"][0:1, 0:1], min_val=0, max_val=1)
        with nc.If(unfit != 0):
            with ExitStack() as ctx:
                weights_dense(nc, ctx, sb, ps, sem, m, x_d, adj_d)
        with ExitStack() as ctx:
            w = load_weights(nc, root, ctx, sb, ps, sem, m, d)
        with ExitStack() as ctx:
            first_norm(nc, ctx, sb, ps, sem, m, w, x_d, table_d)
        unfit = nc.values_load(m["flag"][0:1, 0:1], min_val=0, max_val=1)
        with nc.If(unfit != 0):
            with ExitStack() as ctx:
                logits_dense(nc, ctx, sb, ps, sem, m, w, adj_d, logit_d)
            with ExitStack() as ctx:
                attention_dense(nc, ctx, sb, ps, sem, m, w, adj_d, table_d, logit_d)
        with nc.Else():
            with ExitStack() as ctx:
                logits(nc, ctx, sb, ps, sem, m, w, table_d)
            with ExitStack() as ctx:
                attention(nc, ctx, sb, ps, sem, m, w, table_d)
        with ExitStack() as ctx:
            last_norm(nc, ctx, sb, ps, sem, m, w, out)


def constants(nc, ctx, sb, sem, m):
    oi = sb("own_i", [P, 1], I32, ctx)
    si = sb("segoff_i", [P, CAND], I32, ctx)
    ii = sb("iota_i", [P, EDGES], I32, ctx)
    ei = sb("edge_i", [P, CHUNKS], I32, ctx)
    s_iota = sem("s_iota", ctx)
    s_fill = sem("s_fill", ctx)
    block = ctx.enter_context(nc.Block())

    @block.gpsimd
    def _(pool):
        pool.iota(oi[:, :], pattern=[[0, 1]], base=0, channel_multiplier=1)
        pool.iota(ii[:, :], pattern=[[1, EDGES]], base=0, channel_multiplier=0)
        pool.iota(ei[:, :], pattern=[[P, CHUNKS]], base=1, channel_multiplier=1)
        pool.iota(si[:, :].rearrange("p (g e) -> p g e", e=8), pattern=[[SEGW, SEG], [0, 8]], base=1,
                  channel_multiplier=0).then_inc(s_iota, 1)
        pool.memset(m["ones"][:, :], 1.0)
        pool.memset(m["before"][:, :], 1.0)
        pool.memset(m["offdiag"][:, :], 1.0)
        pool.memset(m["identb"][:, :], 0.0)
        pool.memset(m["ident"][:, :], 0.0).then_inc(s_fill, 1)
        pool.wait_ge(s_fill, 1)
        for t, op, fill in (("ident", ALU.not_equal, 1.0), ("identb", ALU.not_equal, 1.0),
                            ("offdiag", ALU.not_equal, 0.0)):
            pool.affine_select(out=m[t][:, :], in_=m[t][:, :], compare_op=op, fill=fill, base=0,
                               pattern=[[-1, P]], channel_multiplier=1)
        pool.affine_select(out=m["before"][:, :], in_=m["before"][:, :], compare_op=ALU.is_gt, fill=0.0,
                           base=0, pattern=[[1, P]], channel_multiplier=-1)

    @block.vector
    def _(dve):
        dve.wait_ge(s_iota, 1)
        dve.tensor_copy(m["own"][:, :], oi[:, :])
        dve.tensor_copy(m["iota"][:, :], ii[:, :])
        dve.tensor_copy(m["edge1"][:, :], ei[:, :])
        dve.tensor_copy(m["segoff"][:, :], si[:, :])


def extract(nc, ctx, sb, ps, sem, m, x_d, adj_d):
    A = sb("A", [P, 2, N], F32, ctx)
    sg = sb("sg", [P, 2, SEGW], BF16, ctx)
    G = sb("G", [P, 2, CHUNKS, P], F32, ctx)
    S = sb("S", [P, 2, CHUNKS + 1, P], F32, ctx)
    xt = sb("xt", [P, 2, P], F32, ctx)
    pos = sb("pos", [P, CAND], U32, ctx)
    posf = sb("posf", [P, CAND], F32, ctx)
    there = sb("there", [P, CAND], F32, ctx)
    zero = sb("zero", [P, CAND], F32, ctx)
    pay = sb("pay", [P, 2, PAY], F32, ctx)
    cnt = sb("cnt1", [P, 1], F32, ctx)
    end = sb("end1", [P, 1], F32, ctx)
    Q = sb("Q", [P, EDGES], F32, ctx)
    dtmp = sb("dtmp", [P, 2, P], F32, ctx)
    eo = sb("eo", [P, CHUNKS, CAND], F32, ctx)
    kv = sb("kv", [P, CHUNKS, 2, CAND], F32, ctx)
    rec = sb("rec", [P, 2, RECS], F32, ctx)
    idx = sb("idx", [P, 2, CHUNKS], U32, ctx)
    z = sb("z", [P, 2, CHUNKS + 1], F32, ctx)
    q = sb("q", [P, 2, CHUNKS + 1], F32, ctx)
    e = sb("e", [P, 2, CHUNKS + 1], F32, ctx)
    wt = sb("wt", [P, 2, CHUNKS + 1], F32, ctx)
    bad = sb("bad", [P, 4, NT], F32, ctx)
    sgs = sb("sgs", [P, NT], F32, ctx)
    badrow = sb("badrow", [P, 1], F32, ctx)
    psT = ps("psT", [P, 2, SEGW], BF16, ctx)
    psE = ps("psE", [P, 2, 512], F32, ctx)
    psB = ps("psB", [P, 512], F32, ctx)
    psY = ps("psY", [P, 2, 512], F32, ctx)
    dsum = ps("dsum", [P, P], F32, ctx)

    s_adj = [sem(f"s_adj{b}", ctx) for b in range(2)]
    s_x = [sem(f"s_x{b}", ctx) for b in range(2)]
    s_gath = [sem(f"s_gath{b}", ctx) for b in range(2)]
    s_off = sem("s_off", ctx)
    s_diag = sem("s_diag", ctx)
    s_wt = sem("s_wt", ctx)
    s_scan = sem("s_scan", ctx)
    s_sign = sem("s_sign", ctx)
    s_turn = sem("s_turn", ctx)
    s_mask = sem("s_mask", ctx)
    s_cnt = sem("s_cnt", ctx)
    s_base = sem("s_base", ctx)
    s_pay = sem("s_pay", ctx)
    s_edge = sem("s_edge", ctx)
    s_idx = sem("s_idx", ctx)
    s_q = sem("s_q", ctx)
    s_exp = sem("s_exp", ctx)
    s_prod = sem("s_prod", ctx)
    s_sum = sem("s_sum", ctx)
    s_y = sem("s_y", ctx)
    s_v = sem("s_v", ctx)
    s_gv, s_gp, s_ga, s_gt, s_gs = m["gates"]
    s_bad, s_cntd = sem("s_bad", ctx), sem("s_cntd", ctx)
    block = ctx.enter_context(nc.Block())

    @block.sync
    def _(sp):
        def load(t, b, h):
            if not over(t, NT):
                if not early(t, 2):
                    sp.wait_ge(s_scan, t - 1)
                    sp.sem_inc(s_gs, 1)
                    sp.wait_ge(s_sign, SEG * (t - 1))
                    sp.sem_inc(s_gs, 1)
                sp.dma_start(A[:, b, :], adj_d[bass.ds(t * P, P), :]).then_inc(s_adj[b], 16)
            if not early(t, 2):
                if not early(t, 4):
                    sp.wait_ge(s_sum, t - 3)
                    sp.sem_inc(s_gs, 1)
                sp.dma_start(xt[:, b, :], x_d[bass.ds((t - 2) * P, P), :]).then_inc(s_x[b], 16)
        all_steps(sp, load)

    @block.gpsimd
    def _(pool):
        def clear(t, b, h):
            pool.wait_ge(s_adj[b], 16 * (h + 1))
            if not early(t, 2):
                pool.wait_ge(s_diag, t - 1)
            pool.sem_inc(s_gp, 1)
            blk = A[:, b, bass.ds(t * P, P)]
            pool.tensor_tensor(dtmp[:, b, :], blk, m["ident"][:, :], ALU.mult)
            pool.tensor_tensor(blk, blk, m["offdiag"][:, :], ALU.mult).then_inc(s_off, 1)

        def step(t, b, h):
            if not early(t, 2):
                pool.wait_ge(s_wt, t - 1)
                if not early(t, 4):
                    pool.wait_ge(s_sum, t - 3)
                pool.sem_inc(s_gp, 1)
                pool.tensor_scalar(S[:, b, CHUNKS, :], m["ident"][:, :], wt[:, b, CHUNKS:CHUNKS + 1], None, ALU.mult)
                for c in range(CHUNKS):
                    at = RROW * CHUNKS + c
                    last = pool.tensor_scalar(S[:, b, c, :], m["iota"][:, 0:P], rec[:, b, at:at + 1],
                                              wt[:, b, c:c + 1], ALU.is_equal, ALU.mult)
                last.then_inc(s_prod, 1)
            if not (early(t, 1) or over(t, NT + 1)):
                pool.wait_ge(s_idx, t)
                if not early(t, 3):
                    pool.wait_ge(s_sum, t - 2)
                pool.sem_inc(s_gp, 1)
                for c in range(CHUNKS):
                    pool.indirect_dma_start(G[:, 1 - b, c, :], None, x_d[:, :],
                                            bass.IndirectOffsetOnAxis(ap=idx[:, 1 - b, c:c + 1], axis=0))\
                        .then_inc(s_gath[1 - b], 16)
            if not over(t, NT):
                return lambda: clear(t + 1, 1 - b, h + b)

        clear(0, 0, 0)
        for t in range(4):
            step(t, t % 2, t // 2)()
        with pool.Fori(2, NT // 2 - 1) as i:
            step(2 * i, 0, i)()
            step(2 * i + 1, 1, i)()
        step(NT - 2, 0, NT // 2 - 1)()
        step(NT - 1, 1, NT // 2 - 1)
        step(NT, 0, NT // 2)
        step(NT + 1, 1, NT // 2)

    @block.vector
    def _(dve):
        ch = Chain(dve, s_v)

        def step(t, b, h):
            a = 1 - b
            scanned, packed, weighed = not over(t, NT), not (early(t, 1) or over(t, NT + 1)), not early(t, 2)
            ch.restart()
            top, key, rank = (pay[:, b, at:at + CAND] for at in (VAL, KEY, RANK))
            ed = psE[:, a, 0:CHUNKS * PAY].rearrange("p (c y) -> p c y", y=PAY)
            recs = rec[:, a, 0:REC * CHUNKS].rearrange("p (g c) -> p g c", c=CHUNKS)
            values = rec[:, a, RVAL * CHUNKS:RECS]
            shape = [P, CHUNKS, CAND]
            seg = lambda g: A[:, b, g * SEGW:(g + 1) * SEGW]
            best = lambda g: pay[:, b, VAL + 8 * g:VAL + 8 * g + 8]
            find = lambda g: dve.max_index(pos[:, 8 * g:8 * g + 8], best(g), seg(g))
            if scanned:
                dve.wait_ge(s_off, t + 1)
                dve.sem_inc(s_gv, 1)
                dve.max(best(0), seg(0))
            if weighed:
                dve.wait_ge(s_exp, t - 1)
                if not early(t, 4):
                    dve.wait_ge(s_prod, t - 3)
                dve.sem_inc(s_gv, 1)
                dve.scalar_tensor_tensor(wt[:, b, :], z[:, b, :], 1.0, e[:, b, :], ALU.is_lt, ALU.mult)\
                    .then_inc(s_wt, 1)
            if scanned:
                dve.max(best(1), seg(1))
                dve.max(best(2), seg(2))
            if packed:
                dve.wait_ge(s_edge, t)
                dve.wait_ge(s_diag, t)
                if not early(t, 3):
                    dve.wait_ge(s_prod, t - 2)
                dve.sem_inc(s_gv, 1)
                ch.mark(dve.tensor_tensor(recs[:, RSLOT, :], m["edge1"][:, :], ed[:, :, BASE], ALU.subtract))
                dve.tensor_copy(recs[:, RROW, :], ed[:, :, OWN])
            if scanned:
                ch.mark(dve.max(best(3), seg(3)))
            if scanned or packed:
                ch.wait()
            if packed:
                ch.mark(dve.tensor_tensor(eo[:, :, :], ed[:, :, RANK:RANK + CAND],
                                          spread(recs[:, RSLOT, :], 2, shape), ALU.is_equal))
            if scanned:
                ch.link(dve.tensor_scalar(there[:, :], top, 0.0, None, ALU.is_gt))
                ch.mark(dve.tensor_reduce(cnt[:, :], there[:, :], AX, ALU.add))
                find(0)
                ch.wait()
                dve.sem_inc(s_cnt, 1)
            if packed:
                ch.wait()
                ch.link(dve.tensor_tensor(kv[:, :, :, :], ed[:, :, KEY:KEY + 2 * CAND].rearrange(
                    "p c (g q) -> p c g q", g=2), spread(eo[:, :, :], 2, [P, CHUNKS, 2, CAND]), ALU.mult))
                ch.mark(dve.tensor_reduce(recs[:, RKEY:RVAL + 1:RVAL, :].rearrange("p g c -> p c g"),
                                          kv[:, :, :, :], AX, ALU.add))
            if scanned:
                find(1)
                ch.mark(dve.tensor_tensor_scan(posf[:, :], there[:, :], zero[:, :], 0.0, ALU.add, ALU.add))
            ch.wait()
            if packed:
                dve.tensor_scalar(idx[:, a, :], recs[:, RKEY, :], -1.0, 0.0, ALU.add, ALU.max).then_inc(s_idx, 1)
                ch.mark(dve.tensor_scalar(z[:, a, :], values, 0.0, 2.0, ALU.is_equal, ALU.mult))
                dve.tensor_copy(m["rec_all"][:, t - 1, :], rec[:, a, :])
            if scanned:
                dve.tensor_tensor(rank, posf[:, :], there[:, :], ALU.mult)
                find(2)
            if packed:
                ch.wait()
                ch.mark(dve.tensor_tensor(z[:, a, :], z[:, a, :], values, ALU.add))
            if scanned:
                dve.wait_ge(s_base, t + 1)
                dve.sem_inc(s_gv, 1)
                ch.mark(dve.tensor_copy(pay[:, b, BASE:BASE + 1], psB[:, 0:1]))
                dve.tensor_copy(m["cnt"][:, bass.ds(t, 1)], cnt[:, :])
                ch.mark(find(3))
                ch.wait()
                dve.sem_inc(s_scan, 1)
                dve.tensor_tensor(end[:, :], pay[:, b, BASE:BASE + 1], cnt[:, :], ALU.add)
                ch.mark(dve.tensor_tensor(posf[:, :], pos[:, :], m["segoff"][:, :], ALU.add))
                dve.tensor_scalar(Q[:, :], m["iota"][:, :], pay[:, b, BASE:BASE + 1], None, ALU.is_ge)
            ch.wait()
            if packed:
                ch.mark(dve.reciprocal(q[:, a, :], z[:, a, :]))
            if scanned:
                dve.tensor_tensor(key, posf[:, :], there[:, :], ALU.mult)
                ch.mark(dve.tensor_copy(m["ends"][:, bass.ds(t, 1)], end[:, :]))
                ch.wait()
                ch.mark(dve.scalar_tensor_tensor(Q[:, :], m["iota"][:, :], end[:, :], Q[:, :],
                                                 ALU.is_lt, ALU.mult))
            ch.wait()
            if scanned:
                dve.sem_inc(s_pay, 1)
            if packed:
                ch.mark(dve.tensor_scalar(q[:, a, :], q[:, a, :], -1.0, None, ALU.add))
            if scanned:
                dve.tensor_reduce(m["full"][:, bass.ds(t, 1)], pay[:, b, VAL + 7:VAL + CAND:8], AX, ALU.max)
            if packed:
                ch.wait()
                dve.tensor_tensor(q[:, a, :], q[:, a, :], q[:, a, :], ALU.mult).then_inc(s_q, 1)

        ch.link(dve.memset(zero[:, :], 0.0))
        dve.tensor_copy(pay[:, 0, OWN:OWN + 1], m["own"][:, :])
        ch.link(dve.tensor_copy(pay[:, 1, OWN:OWN + 1], m["own"][:, :]))
        all_steps(dve, step)
        ch.restart()
        dve.wait_ge(s_mask, NT * SEG)
        ch.link(dve.tensor_reduce(sgs[:, :], m["signs"][:, :, :], AX, ALU.add))
        dve.tensor_tensor(bad[:, 0, :], sgs[:, :], m["cnt"][:, :], ALU.not_equal)
        dve.tensor_scalar(bad[:, 1, :], m["cnt"][:, :], float(SLOTS), None, ALU.is_gt)
        dve.tensor_scalar(bad[:, 2, :], m["ends"][:, :], float(EDGES), None, ALU.is_gt)
        ch.link(dve.tensor_scalar(bad[:, 3, :], m["full"][:, :], 0.0, None, ALU.is_gt))
        dve.tensor_reduce(badrow[:, :], bad[:, :, :].rearrange("p a t -> p (a t)"), AX, ALU.add)\
            .then_inc(s_bad, 1)
        dve.wait_ge(s_cntd, 1)
        dve.tensor_scalar(m["flag"][:, :], psB[0:1, 1:2], 1.0, None, ALU.min)

    @block.scalar
    def _(act):
        def signs(t, b, h):
            act.wait_ge(s_off, t + 1)
            act.sem_inc(s_ga, 1)
            act.activation(dsum[:, :], dtmp[:, b, :], ACT.Copy, accum_out=rec[:, b, RECS - 1:RECS])\
                .then_inc(s_diag, 1)
            for g in range(SEG):
                if not (early(t, 1) and g < 2):
                    act.wait_ge(s_turn, SEG * t + g - 1)
                    act.sem_inc(s_ga, 1)
                act.activation(sg[:, g % 2, :], A[:, b, g * SEGW:(g + 1) * SEGW], ACT.Sign,
                               accum_out=m["signs"][:, t, g:g + 1]).then_inc(s_sign, 1)
                if not (early(t, 1) and g < 1):
                    keep(t, g - 1)

        def keep(t, g):
            if g < 0:
                t, g = t - 1, SEG - 1
            act.wait_ge(s_turn, SEG * t + g + 1)
            act.sem_inc(s_ga, 1)
            act.activation(m["maskT"][:, 8 * g:8 * g + 8, bass.ds(t * P, P)],
                           psT[:, g % 2, :].rearrange("p (j i) -> p j i", i=P), ACT.Copy,
                           scale=float(FP8_ONE)).then_inc(s_mask, 1)

        def expo(t, b):
            act.wait_ge(s_q, t + 1)
            act.sem_inc(s_ga, 1)
            act.activation(e[:, b, :], q[:, b, :], ACT.Exp, scale=-2.0).then_inc(s_exp, 1)

        def keep_sum(t, b):
            act.wait_ge(s_sum, t + 1)
            act.sem_inc(s_ga, 1)
            act.activation(m["wsum"][:, bass.ds(t, 1)], psY[:, b, P:P + 1], ACT.Copy)
            act.activation(m["yT"][:, t, :], psY[:, b, 0:P], ACT.Copy).then_inc(s_y, 1)

        def step(t, b, h):
            if not early(t, 2):
                expo(t - 2, b)
            if not over(t, NT):
                signs(t, b, h)
            if over(t, NT) and not over(t, NT + 1):
                keep(NT - 1, SEG - 1)
            if not early(t, 3):
                keep_sum(t - 3, 1 - b)

        all_steps(act, step)
        keep_sum(NT - 1, 1)

    @block.tensor
    def _(pe):
        def turn(t, b, h):
            for g in range(SEG):
                pe.wait_ge(s_sign, SEG * t + g + 1)
                if not (early(t, 1) and g < 2):
                    pe.wait_ge(s_mask, SEG * t + g - 1)
                pe.sem_inc(s_gt, 1)
                for j in range(8):
                    last = pe.transpose(psT[:, g % 2, j * P:(j + 1) * P], sg[:, g % 2, j * P:(j + 1) * P],
                                        m["identb"][:, :])
                last.then_inc(s_turn, 1)
                if g == 2:
                    pe.wait_ge(s_cnt, t + 1)
                    pe.sem_inc(s_gt, 1)
                    pe.matmul(psB[:, 0:1], m["before"][:, :], cnt[:, :], start=True, stop=True)\
                        .then_inc(s_base, 1)

        def hand_over(t, b):
            pe.wait_ge(s_pay, t + 1)
            pe.sem_inc(s_gt, 1)
            for c in range(CHUNKS):
                last = pe.matmul(psE[:, b, c * PAY:(c + 1) * PAY], Q[:, c * P:(c + 1) * P], pay[:, b, :],
                                 start=True, stop=True)
            last.then_inc(s_edge, 1)

        def total(t, b, h):
            pe.wait_ge(s_prod, t + 1)
            pe.wait_ge(s_gath[b], 16 * CHUNKS * (h + 1))
            pe.wait_ge(s_x[b], 16 * (h + 1))
            if not early(t, 2):
                pe.wait_ge(s_y, t - 1)
            pe.sem_inc(s_gt, 1)
            for c in range(CHUNKS + 1):
                rows = G[:, b, c, :] if c < CHUNKS else xt[:, b, :]
                pe.matmul(psY[:, b, 0:P], rows, S[:, b, c, :], start=(c == 0), stop=(c == CHUNKS))
            for c in range(CHUNKS + 1):
                last = pe.matmul(psY[:, b, P:P + 1], S[:, b, c, :], m["ones"][:, 0:1],
                                 start=(c == 0), stop=(c == CHUNKS))
            last.then_inc(s_sum, 1)

        def step(t, b, h):
            if not (early(t, 1) or over(t, NT + 1)):
                hand_over(t - 1, 1 - b)
            if not over(t, NT):
                turn(t, b, h)
            if not early(t, 2):
                total(t - 2, b, h - 1)
        all_steps(pe, step)
        pe.wait_ge(s_bad, 1)
        pe.matmul(psB[0:1, 1:2], badrow[:, :], m["ones"][:, 0:1], start=True, stop=True).then_inc(s_cntd, 1)


def load_weights(nc, root, ctx, sb, ps, sem, m, d):
    w = {}
    w["W0"] = sb("W0", [P, P], F32, root)
    w["B0"] = sb("B0", [P, P], F32, root)
    w["gatW"] = sb("gatW", [P, HEADS, P], F32, root)
    w["ih"] = sb("ihT", [P, 2, 3 * P], F32, root)
    w["hh"] = sb("hhT", [P, 2, 3 * P], F32, root)
    w["bias3"] = sb("bias3", [3, 2, 4 * P], BF16, root)
    w["ones3"] = sb("ones3", [3, P], BF16, root)
    w["WA"] = sb("WA", [P, 2 * HEADS], F32, root)
    w["V"] = sb("V", [P, NT, 2 * HEADS], F32, root)
    w["H"] = sb("H", [P, NT, P], F32, root)
    w["mv"] = sb("mv_all", [P, NT, 2], F32, root)
    w["rstd"] = sb("rstd", [P, NT], F32, root)
    bias = sb("bias", [1, 2, 4 * P], F32, ctx)
    parts = sb("bias_parts", [1, 3, 2, 4 * P], BF16, ctx)
    a6 = sb("a6", [2 * HEADS, P], F32, ctx)
    a6T = sb("a6T", [P, 2 * HEADS], F32, ctx)
    gwT = sb("gwT", [P, HEADS, P], F32, ctx)
    raw = sb("raw", [P, 4, 3, P], F32, ctx)
    bi = sb("bi", [1, 2, 3 * P], F32, ctx)
    bh = sb("bh", [1, 2, 3 * P], F32, ctx)
    pw = ps("pw", [P, 4, 512], F32, ctx)
    pa = ps("pa", [P, 512], F32, ctx)
    pg = ps("pg", [P, 512], F32, ctx)
    pwa = ps("pwa", [P, 512], F32, ctx)
    s_w, s_t, s_c, s_o = sem("s_load", ctx), sem("s_turned", ctx), sem("s_copied", ctx), sem("s_wa", ctx)
    s_b, s_bc, s_bd = sem("s_bias", ctx), sem("s_bias_chain", ctx), sem("s_bias_moved", ctx)
    block = ctx.enter_context(nc.Block())
    names = [("L1_gnn_edge_Wih", "ih", 0), ("L1_gnn_node_Wih", "ih", 1),
             ("L1_gnn_edge_Whh", "hh", 0), ("L1_gnn_node_Whh", "hh", 1)]
    loads = [(w["W0"][:, :], d["L0_gnn_W"]), (w["B0"][:, :], d["L0_gnn_B"].partition_broadcast(P)),
             (w["gatW"][:, :, :], d["L1_gnn_gat_W"].rearrange("k c e -> c k e")),
             (a6[:, :], d["L1_gnn_gat_a"].rearrange("k (g e) o -> (k g) (e o)", g=2)),
             (bi[:, 0, :], d["L1_gnn_edge_bih"].rearrange("(o n) -> o n", o=1)),
             (bi[:, 1, :], d["L1_gnn_node_bih"].rearrange("(o n) -> o n", o=1)),
             (bh[:, 0, :], d["L1_gnn_edge_bhh"].rearrange("(o n) -> o n", o=1)),
             (bh[:, 1, :], d["L1_gnn_node_bhh"].rearrange("(o n) -> o n", o=1))]
    loads += [(raw[:, i, :, :], d[n].rearrange("(g p) c -> p g c", p=P)) for i, (n, _, _) in enumerate(names)]

    @block.sync
    def _(sp):
        for dst, src in loads:
            sp.dma_start(dst, src).then_inc(s_w, 16)
        sp.wait_ge(s_b, 1)
        for j in range(3):
            sp.dma_start(w["bias3"][j:j + 1, :, :], parts[:, j, :, :]).then_inc(s_bd, 16)
        sp.wait_ge(s_bd, 48)

    @block.tensor
    def _(pe):
        pe.wait_ge(s_w, 16 * len(loads))
        for i in range(4):
            for g in range(3):
                pe.transpose(pw[:, i, g * P:(g + 1) * P], raw[:, i, g, :], m["ident"][:, :])
        for k in range(HEADS):
            pe.transpose(pg[:, k * P:(k + 1) * P], w["gatW"][:, k, :], m["ident"][:, :])
        pe.transpose(pa[:, 0:2 * HEADS], a6[:, :], m["ident"][0:2 * HEADS, 0:2 * HEADS]).then_inc(s_t, 1)
        pe.wait_ge(s_c, 1)
        for k in range(HEADS):
            last = pe.matmul(pwa[:, 2 * k:2 * k + 2], gwT[:, k, :], a6T[:, 2 * k:2 * k + 2],
                             start=True, stop=True)
        last.then_inc(s_o, 1)

    @block.vector
    def _(dve):
        dve.wait_ge(s_t, 1)
        dve.tensor_copy(a6T[:, :], pa[:, 0:2 * HEADS])
        dve.tensor_copy(gwT[:, :, :], pg[:, 0:3 * P].rearrange("p (k c) -> p k c", k=HEADS)).then_inc(s_c, 1)
        for i, (_, key, j) in enumerate(names):
            dve.tensor_copy(w[key][:, j, :], pw[:, i, 0:3 * P])
        ch = Chain(dve, s_bc)
        dve.memset(w["ones3"][:, :], 1.0)
        dve.tensor_tensor(bias[:, :, 0:2 * P], bi[:, :, 0:2 * P], bh[:, :, 0:2 * P], ALU.add)
        dve.tensor_copy(bias[:, :, 2 * P:3 * P], bi[:, :, 2 * P:3 * P])
        ch.link(dve.tensor_copy(bias[:, :, 3 * P:4 * P], bh[:, :, 2 * P:3 * P]))
        for j in range(3):
            ch.link(dve.tensor_copy(parts[:, j, :, :], bias[:, :, :]))
            if j < 2:
                ch.link(dve.tensor_tensor(bias[:, :, :], bias[:, :, :], parts[:, j, :, :], ALU.subtract))
        dve.sem_inc(s_b, 1)
        dve.wait_ge(s_o, 1)
        dve.tensor_copy(w["WA"][:, :].rearrange("p (g k) -> p k g", g=2),
                        pwa[:, 0:2 * HEADS].rearrange("p (k g) -> p k g", g=2))
    return w


def finish_stats(dve, act, w, ch, s_var, s_sd):
    ch.link(dve.tensor_scalar(w["rstd"][:, :], w["mv"][:, :, 1], EPS, None, ALU.add))
    dve.sem_inc(s_var, 1)
    dve.wait_ge(s_sd, 1)
    ch.link(dve.reciprocal(w["rstd"][:, :], w["rstd"][:, :]))


def first_norm(nc, ctx, sb, ps, sem, m, w, x_d, table_d):
    hb = sb("h_row", [P, 2, P], F32, ctx)
    yb = sb("yb", [P, 2, P], F32, ctx)
    xb = sb("xb", [P, 2, P], F32, ctx)
    hT = sb("hT", [P, 2, P], F32, ctx)
    st = sb("st", [P, 6], F32, ctx)
    mv = sb("mv", [P, 2], F32, ctx)
    psM = ps("psM", [P, 2, 512], F32, ctx)
    psH = ps("psH", [P, 2, 512], F32, ctx)
    psV = ps("psV", [P, 2, 512], F32, ctx)
    s_x = [sem(f"s_x2{b}", ctx) for b in range(2)]
    s_yb = sem("s_yb", ctx)
    s_mm = sem("s_mm", ctx)
    s_pre = sem("s_pre", ctx)
    s_var, s_sd = sem("s_var", ctx), sem("s_sd", ctx)
    s_h = sem("s_h", ctx)
    s_ht = sem("s_ht", ctx)
    s_htc = sem("s_htc", ctx)
    s_v = sem("s_v2", ctx)
    s_vc = sem("s_vc", ctx)
    s_tab = [sem(f"s_tab{b}", ctx) for b in range(2)]
    s_ch = sem("s_ch2", ctx)
    s_gv, s_gp, s_ga, s_gt, s_gs = m["gates"]
    block = ctx.enter_context(nc.Block())

    @block.sync
    def _(sp):
        def load(t, b, h):
            if not (isinstance(t, int) and t < 2):
                sp.wait_ge(s_pre, t - 1)
                sp.sem_inc(s_gs, 1)
            sp.dma_start(xb[:, b, :], x_d[bass.ds(t * P, P), :]).then_inc(s_x[b], 16)

        def store(t, b, h):
            sp.wait_ge(s_h, t + 1)
            sp.sem_inc(s_gs, 1)
            sp.dma_start(table_d[bass.ds(t * P, P), 0:P], hb[:, b, :]).then_inc(s_tab[b], 16)
        all_tiles(sp, load)
        all_tiles(sp, store)
        for b in range(2):
            sp.wait_ge(s_tab[b], 16 * NT // 2)

    @block.scalar
    def _(act):
        def fetch(t, b, h):
            if not (isinstance(t, int) and t < 2):
                act.wait_ge(s_mm, t - 1)
                act.sem_inc(s_ga, 1)
            act.activation(yb[:, b, :], m["yT"][:, t, :], ACT.Copy).then_inc(s_yb, 1)
        all_tiles(act, fetch)
        act.wait_ge(s_var, 1)
        act.activation(w["rstd"][:, :], w["rstd"][:, :], ACT.Sqrt).then_inc(s_sd, 1)

        def copy(t, b, h):
            act.wait_ge(s_ht, t + 1)
            if not (isinstance(t, int) and t < 2):
                act.wait_ge(s_v, t - 1)
            act.sem_inc(s_ga, 1)
            act.activation(hT[:, b, :], psH[:, b, 0:P], ACT.Copy).then_inc(s_htc, 1)
        all_tiles(act, copy)

    @block.tensor
    def _(pe):
        def product(t, b, h):
            pe.wait_ge(s_yb, t + 1)
            if not (isinstance(t, int) and t < 2):
                pe.wait_ge(s_pre, t - 1)
            pe.sem_inc(s_gt, 1)
            pe.matmul(psM[:, b, 0:P], yb[:, b, :], w["W0"][:, :], start=True, stop=True).then_inc(s_mm, 1)
        all_tiles(pe, product)

        def turn(t, b, h):
            pe.wait_ge(s_h, t + 1)
            if not (isinstance(t, int) and t < 2):
                pe.wait_ge(s_htc, t - 1)
            pe.sem_inc(s_gt, 1)
            pe.transpose(psH[:, b, 0:P], hb[:, b, :], m["ident"][:, :]).then_inc(s_ht, 1)
            pe.wait_ge(s_htc, t + 1)
            if not (isinstance(t, int) and t < 2):
                pe.wait_ge(s_vc, t - 1)
            pe.sem_inc(s_gt, 1)
            pe.matmul(psV[:, b, 0:2 * HEADS], hT[:, b, :], w["WA"][:, :], start=True, stop=True)\
                .then_inc(s_v, 1)
        all_tiles(pe, turn)

    @block.vector
    def _(dve):
        ch = Chain(dve, s_ch)

        def rows(t, b, h):
            ch.restart()
            dve.wait_ge(s_x[b], 16 * (h + 1))
            dve.sem_inc(s_gv, 1)
            ch.link(dve.scalar_tensor_tensor(xb[:, b, :], w["B0"][:, :], m["wsum"][:, bass.ds(t, 1)],
                                             xb[:, b, :], ALU.mult, ALU.add))
            dve.wait_ge(s_mm, t + 1)
            dve.sem_inc(s_gv, 1)
            ch.link(dve.tensor_tensor(w["H"][:, t, :], psM[:, b, 0:P], xb[:, b, :], ALU.add))
            dve.sem_inc(s_pre, 1)
            ch.link(dve.bn_stats(st[:, :], w["H"][:, t, :]))
            ch.link(dve.bn_aggr(mv[:, :], st[:, :]))
            ch.link(dve.tensor_copy(w["mv"][:, t, :], mv[:, :]))
        all_tiles(dve, rows)
        finish_stats(dve, None, w, ch, s_var, s_sd)

        def normalise(t, b, h):
            if not (isinstance(t, int) and t < 2):
                dve.wait_ge(s_tab[b], 16 * h)
                dve.wait_ge(s_ht, t - 1)
                dve.sem_inc(s_gv, 1)
            dve.tensor_scalar(hb[:, b, :], w["H"][:, t, :], w["mv"][:, t, 0:1],
                              w["rstd"][:, bass.ds(t, 1)], ALU.subtract, ALU.mult).then_inc(s_h, 1)

        def values(t, b, h):
            dve.wait_ge(s_v, t + 1)
            dve.sem_inc(s_gv, 1)
            dve.tensor_copy(w["V"][:, t, :], psV[:, b, 0:2 * HEADS]).then_inc(s_vc, 1)
        two_phases(dve, normalise, values)


def logits(nc, ctx, sb, ps, sem, m, w, table_d):
    M9 = 3 * HEADS
    W = 512
    rest = sb("rest", [P, NT, HEADS], F32, ctx)
    parts = sb("parts", [P, NT, M9], BF16, ctx)
    U = sb("U", [M9, N], F32, ctx)
    comb = sb("comb", [M9, HEADS], F32, ctx)
    lg = sb("lg", [P, NT, HEADS], F32, ctx)
    lk = sb("lk", [P, NT, HEADS], F32, ctx)
    psU = ps("psU", [P, 2, W], F32, ctx)
    psL = ps("psL", [P, NT, HEADS], F32, ctx)
    s_comb, s_c3 = sem("s_comb", ctx), sem("s_ch3", ctx)
    s_parts, s_u, s_uc, s_l, s_e, s_out = (sem(n, ctx) for n in
                                           ("s_parts", "s_u", "s_uc", "s_l", "s_e", "s_logit"))
    block = ctx.enter_context(nc.Block())

    @block.gpsimd
    def _(pool):
        pool.memset(comb[:, :], 0.0).then_inc(s_comb, 1)
        for j in range(3):
            pool.wait_ge(s_comb, j + 1)
            pool.affine_select(out=comb[:, :], in_=comb[:, :], compare_op=ALU.not_equal, fill=1.0,
                               base=-HEADS * j, pattern=[[-1, HEADS]], channel_multiplier=1).then_inc(s_comb, 1)

    @block.vector
    def _(dve):
        ch = Chain(dve, s_c3)
        ch.link(dve.tensor_copy(rest[:, :, :], w["V"][:, :, 0:HEADS]))
        for j in range(3):
            part = parts[:, :, j * HEADS:(j + 1) * HEADS]
            ch.link(dve.tensor_copy(part, rest[:, :, :]))
            if j < 2:
                ch.link(dve.tensor_tensor(rest[:, :, :], rest[:, :, :], part, ALU.subtract))
        dve.sem_inc(s_parts, 1)
        dve.wait_ge(s_l, 1)
        ch.link(dve.tensor_copy(lg[:, :, :], psL[:, :, :]))
        dve.scalar_tensor_tensor(lk[:, :, :], lg[:, :, :], 0.2, lg[:, :, :], ALU.mult, ALU.max).then_inc(s_e, 1)

    @block.tensor
    def _(pe):
        pe.wait_ge(s_parts, 1)
        for c in range(N // W):
            if c >= 2:
                pe.wait_ge(s_uc, c - 1)
            for j in range(NT):
                last = pe.matmul(psU[0:M9, c % 2, :], parts[:, j, :],
                                 m["maskT"][:, j, c * W:(c + 1) * W].bitcast(FP8),
                                 start=(j == 0), stop=(j == NT - 1))
            last.then_inc(s_u, 1)
        pe.wait_ge(s_comb, 4)
        pe.wait_ge(s_uc, N // W)
        for t in range(NT):
            last = pe.matmul(psL[:, t, :], U[:, t * P:(t + 1) * P], comb[:, :], start=True, stop=True)
        last.then_inc(s_l, 1)

    @block.scalar
    def _(act):
        for c in range(N // W):
            act.wait_ge(s_u, c + 1)
            act.activation(U[:, c * W:(c + 1) * W], psU[0:M9, c % 2, :], ACT.Copy).then_inc(s_uc, 1)

    @block.sync
    def _(sp):
        sp.wait_ge(s_e, 1)
        sp.dma_start(table_d.rearrange("(t p) c -> p t c", p=P)[:, :, P:P + HEADS], lk[:, :, :],
                     allow_slow_non_contiguous=True).then_inc(s_out, 16)
        sp.wait_ge(s_out, 16)


def carve(region):
    at = [0]

    def place(*shape, dt=F32):
        n = 4
        for x in shape:
            n *= x
        ap = region[:, at[0]:at[0] + n].bitcast(dt)
        at[0] += n
        assert at[0] <= region.shape[1]
        if len(shape) == 2:
            return ap.rearrange("p (a b) -> p a b", b=shape[1])
        if len(shape) == 3:
            return ap.rearrange("p (a b c) -> p a b c", b=shape[1], c=shape[2])
        if len(shape) == 4:
            return ap.rearrange("p (a b c e) -> p a b c e", b=shape[1], c=shape[2], e=shape[3])
        return ap
    return place


class Gru:

    def __init__(self, tag, ctx, place, ps, sem, m, w, hb, supT, s_h, s_supc, s_gv, s_ga, s_gt):
        self.m, self.w, self.hb, self.supT = m, w, hb, supT
        self.s_h, self.s_supc, self.s_gv, self.s_ga, self.s_gt = s_h, s_supc, s_gv, s_ga, s_gt
        bufs = 2 if tag == "" else 1
        self.hT = place(bufs, P)
        self.nsT = place(bufs, P)
        self.g1 = place(bufs, 2, 2 * P)
        self.nn = place(bufs, 2, P)
        self.nt = place(bufs, 2, P)
        self.df = place(2, P)
        self.oo = place(P)
        self.st = place(6)
        self.mv = place(2)
        bank = ps("psHN" + tag, [P, 2, P], F32, ctx)
        self.psH, self.psN = bank[:, 0, :], bank[:, 1, :]
        self.psG = ps("psG" + tag, [P, bufs, 2, 4 * P], F32, ctx)
        self.s_ht = sem("s_ht3" + tag, ctx)
        self.s_htc = sem("s_htc3" + tag, ctx)
        self.s_ns = sem("s_ns" + tag, ctx)
        self.s_nsc = sem("s_nsc" + tag, ctx)
        self.s_gru = sem("s_gru" + tag, ctx)
        self.s_g1 = sem("s_g1" + tag, ctx)
        self.s_nn = sem("s_nn" + tag, ctx)
        self.s_nt = sem("s_nt" + tag, ctx)
        self.s_res = sem("s_res" + tag, ctx)

    def turn_h(self, pe, t, b, landed):
        pe.wait_ge(self.s_h[b], landed)
        if not (isinstance(t, int) and t < 1):
            pe.wait_ge(self.s_nsc, t)
        pe.sem_inc(self.s_gt, 1)
        pe.transpose(self.psH, self.hb[:, b, :], self.m["ident"][:, :]).then_inc(self.s_ht, 1)

    def copy_h(self, act, t, b):
        act.wait_ge(self.s_ht, t + 1)
        act.sem_inc(self.s_ga, 1)
        act.activation(self.hT[:, b, :], self.psH, ACT.Copy).then_inc(self.s_htc, 1)

    def support(self, pe, t, b):
        pe.wait_ge(self.s_supc, t + 1)
        pe.wait_ge(self.s_htc, t + 1)
        pe.sem_inc(self.s_gt, 1)
        for k in range(HEADS):
            last = pe.matmul(self.psN, self.w["gatW"][:, k, :], self.supT[:, b, k + 1, :],
                             start=(k == 0), stop=(k == HEADS - 1))
        last.then_inc(self.s_ns, 1)

    def copy_support(self, act, t, b):
        act.wait_ge(self.s_ns, t + 1)
        act.sem_inc(self.s_ga, 1)
        act.activation(self.nsT[:, b, :], self.psN, ACT.Copy, scale=1.0 / HEADS).then_inc(self.s_nsc, 1)

    def from_h(self, pe, t, b, read=None):
        w, psG = self.w, self.psG[:, b]
        if read is not None:
            pe.wait_ge(self.s_nn, read)
        pe.wait_ge(self.s_htc, t + 1)
        pe.sem_inc(self.s_gt, 1)
        for j in range(2):
            pe.matmul(psG[:, j, :], w["ones3"][:, :], w["bias3"][:, j, :], start=True, stop=False)
            pe.matmul(psG[:, j, 0:2 * P], self.hT[:, b, :], w["hh"][:, j, 0:2 * P], start=False, stop=False)
            pe.matmul(psG[:, j, 3 * P:4 * P], self.hT[:, b, :], w["hh"][:, j, 2 * P:3 * P],
                      start=False, stop=False)

    def from_supports(self, pe, t, b):
        pe.wait_ge(self.s_nsc, t + 1)
        pe.sem_inc(self.s_gt, 1)
        for j in range(2):
            last = pe.matmul(self.psG[:, b, j, 0:3 * P], self.nsT[:, b, :] if j else self.supT[:, b, 0, :],
                             self.w["ih"][:, j, :], start=False, stop=True)
        last.then_inc(self.s_gru, 1)

    def tanh_rz(self, act, t, b):
        act.wait_ge(self.s_gru, t + 1)
        act.sem_inc(self.s_ga, 1)
        act.activation(self.g1[:, b, :, :], self.psG[:, b, :, 0:2 * P], ACT.Tanh, scale=0.5).then_inc(self.s_g1, 1)

    def tanh_n(self, act, t, b):
        act.wait_ge(self.s_nn, t + 1)
        act.sem_inc(self.s_ga, 1)
        act.activation(self.nt[:, b, :, :], self.nn[:, b, :, :], ACT.Tanh).then_inc(self.s_nt, 1)

    def n_input(self, dve, ch, t, b):
        nn, psG = self.nn[:, b], self.psG[:, b]
        dve.wait_ge(self.s_g1, t + 1)
        dve.sem_inc(self.s_gv, 1)
        ch.link(dve.scalar_tensor_tensor(nn[:, :, :], self.g1[:, b, :, 0:P], 1.0, psG[:, :, 3 * P:4 * P],
                                         ALU.add, ALU.mult))
        ch.link(dve.scalar_tensor_tensor(nn[:, :, :], nn[:, :, :], 0.5, psG[:, :, 2 * P:3 * P],
                                         ALU.mult, ALU.add))
        dve.sem_inc(self.s_nn, 1)

    def blend(self, dve, ch, t, b, landed):
        m, w, hb = self.m, self.w, self.hb
        g1, nt, df, oo, st, mv = self.g1[:, b], self.nt[:, b], self.df, self.oo, self.st, self.mv
        dve.wait_ge(self.s_nt, t + 1)
        dve.wait_ge(self.s_h[b], landed)
        dve.sem_inc(self.s_gv, 1)
        ch.link(dve.tensor_tensor(df[:, :, :], spread(hb[:, b, :], 1, [P, 2, P]), nt[:, :, :], ALU.subtract))
        ch.link(dve.scalar_tensor_tensor(df[:, :, :], g1[:, :, P:2 * P], 1.0, df[:, :, :], ALU.add, ALU.mult))
        ch.link(dve.scalar_tensor_tensor(df[:, :, :], df[:, :, :], 0.5, nt[:, :, :], ALU.mult, ALU.add))
        ch.link(dve.tensor_tensor(oo[:, :], df[:, 0, :], df[:, 1, :], ALU.add))
        ch.link(dve.scalar_tensor_tensor(w["H"][:, t, :], oo[:, :], m["rec_all"][:, t, RECS - 1:RECS], hb[:, b, :],
                                         ALU.mult, ALU.add))
        dve.sem_inc(self.s_res, 1)
        ch.link(dve.bn_stats(st[:, :], w["H"][:, t, :]))
        ch.link(dve.bn_aggr(mv[:, :], st[:, :]))
        ch.link(dve.tensor_copy(w["mv"][:, t, :], mv[:, :]))


def attention(nc, ctx, sb, ps, sem, m, w, table_d):
    place = carve(m["maskT"][:, :, :].rearrange("p a b -> p (a b)"))
    K4 = HEADS + 1
    C = CHUNKS
    G = place(4, C, ROW)
    R = place(4, C, P)
    Q = place(2, EDGES)
    S = place(2, C, K4 * P)
    recs = place(4, RECS)
    rec = recs[:, :, 0:REC * C].rearrange("p b (g c) -> p b g c", c=C)
    idx = place(4, C, dt=U32)
    rows = place(2, 3)
    slot = place(2, C, SLOTS)
    EO = place(C, HEADS * SLOTS)
    PS = place(C, HEADS * SLOTS)
    pe3 = place(C, HEADS)
    coef = place(C, HEADS)
    nb = place(2, SLOTS)
    L = place(2, HEADS, SLOTS)
    E = place(2, HEADS, SLOTS)
    mx = place(HEADS)
    den = place(HEADS)
    hb = place(2, P)
    supT = place(2, K4, P)
    psS = ps("psS", [P, K4 * P], F32, ctx)
    psL = ps("psL3", [P, HEADS * SLOTS], F32, ctx)
    psP = ps("psP3", [P, C * HEADS * SLOTS], F32, ctx)

    s_h = [sem(f"s_h3{b}", ctx) for b in range(2)]
    s_gath = [sem(f"s_gath3{q}", ctx) for q in range(4)]
    names = ("s_rec3", "s_onehot", "s_eo", "s_l3", "s_lgt", "s_p", "s_pn", "s_pe3", "s_coef", "s_sup", "s_supc",
             "s_s0", "s_ch4")
    (s_rec, s_hot, s_eo, s_l, s_lgt, s_p, s_pn, s_pe, s_coef, s_sup, s_supc,
     s_s0, s_ch) = (sem(n, ctx) for n in names)
    s_gv, s_gp, s_ga, s_gt, s_gs = m["gates"]
    gru = Gru("", ctx, place, ps, sem, m, w, hb, supT, s_h, s_supc, s_gv, s_ga, s_gt)
    s_res = gru.s_res
    block = ctx.enter_context(nc.Block())

    @block.sync
    def _(sp):
        def load(t, b, h):
            if not (isinstance(t, int) and t < 2):
                sp.wait_ge(s_res, t - 1)
                sp.sem_inc(s_gs, 1)
            sp.dma_start(hb[:, b, :], table_d[bass.ds(t * P, P), 0:P]).then_inc(s_h[b], 16)
        all_tiles(sp, load)

    @block.gpsimd
    def _(pool):
        def gather(t, q, h):
            if over(t, NT):
                return
            pool.wait_ge(s_rec, t + 1)
            pool.sem_inc(s_gp, 1)
            for c in range(C):
                last = pool.tensor_scalar(R[:, q, c, :], m["iota"][:, 0:P], rec[:, q, RROW, c:c + 1], None,
                                          ALU.is_equal)
            last.then_inc(s_hot, 1)
            if not early(t, 4):
                pool.wait_ge(s_sup, t - 3)
                pool.sem_inc(s_gp, 1)
            for c in range(C):
                pool.indirect_dma_start(G[:, q, c, :], None, table_d[:, :],
                                        bass.IndirectOffsetOnAxis(ap=idx[:, q, c:c + 1], axis=0))\
                    .then_inc(s_gath[q], 16)
        all_steps_of_four(pool, gather)

    @block.vector
    def _(dve):
        ch = Chain(dve, s_ch)

        def list_edges(t, q):
            if not early(t, 4):
                dve.wait_ge(s_s0, t - 3)
                dve.sem_inc(s_gv, 1)
            ch.link(dve.tensor_copy(recs[:, q, :], m["rec_all"][:, t, :]))
            dve.tensor_scalar(idx[:, q, :], rec[:, q, RKEY, :], -1.0, 0.0, ALU.add, ALU.max).then_inc(s_rec, 1)

        def list_rows(t, q, b):
            dve.tensor_copy(rows[:, b, 1:2], m["ends"][:, bass.ds(t, 1)])
            ch.link(dve.tensor_copy(rows[:, b, 2:3], m["cnt"][:, bass.ds(t, 1)]))
            ch.mark(dve.tensor_tensor(rows[:, b, 0:1], rows[:, b, 1:2], rows[:, b, 2:3], ALU.subtract))
            dve.tensor_scalar(nb[:, b, :], m["iota"][:, 0:SLOTS], rows[:, b, 2:3], None, ALU.is_lt)
            ch.wait()
            ch.mark(dve.tensor_scalar(Q[:, b, :], m["iota"][:, :], rows[:, b, 0:1], None, ALU.is_ge))
            dve.tensor_tensor(slot[:, b, :, :], spread(m["iota"][:, 1:SLOTS + 1], 1, [P, C, SLOTS]),
                              spread(rec[:, q, RSLOT, :], 2, [P, C, SLOTS]), ALU.is_equal)
            ch.wait()
            dve.tensor_scalar(nb[:, b, :], nb[:, b, :], -1.0, BIG, ALU.add, ALU.mult)
            ch.link(dve.scalar_tensor_tensor(Q[:, b, :], m["iota"][:, :], rows[:, b, 1:2], Q[:, b, :],
                                             ALU.is_lt, ALU.mult))

        def edge_logits(t, q, h, b):
            dve.wait_ge(s_gath[q], 16 * C * (h + 1))
            if not early(t, 1):
                dve.wait_ge(s_l, t)
            dve.sem_inc(s_gv, 1)
            for k in range(HEADS):
                last = dve.tensor_tensor(EO[:, :, k * SLOTS:(k + 1) * SLOTS], slot[:, b, :, :],
                                         G[:, q, :, P + k:P + k + 1].broadcast_to([P, C, SLOTS]), ALU.mult)
            last.then_inc(s_eo, 1)

        def row_max(t, b):
            shape = [P, HEADS, SLOTS]
            dve.wait_ge(s_l, t + 1)
            dve.sem_inc(s_gv, 1)
            ch.link(dve.tensor_tensor(L[:, b, :, :], psL[:, :].rearrange("p (k s) -> p k s", s=SLOTS), spread(nb[:, b, :], 1, shape), ALU.add))
            ch.link(dve.tensor_reduce(mx[:, :], L[:, b, :, :], AX, ALU.max))
            dve.tensor_tensor(L[:, b, :, :], L[:, b, :, :], spread(mx[:, :], 2, shape), ALU.subtract)\
                .then_inc(s_lgt, 1)

        def row_sum(t, b):
            dve.wait_ge(s_p, t + 1)
            dve.sem_inc(s_gv, 1)
            ch.link(dve.tensor_reduce(den[:, :], E[:, b, :, :], AX, ALU.add))
            ch.link(dve.reciprocal(den[:, :], den[:, :]))
            dve.tensor_tensor(E[:, b, :, :], E[:, b, :, :], spread(den[:, :], 2, [P, HEADS, SLOTS]), ALU.mult)\
                .then_inc(s_pn, 1)

        def coefficients(t, q, b):
            dve.wait_ge(s_pe, t + 1)
            if not (isinstance(t, int) and t < 2):
                dve.wait_ge(s_sup, t - 1)
            dve.wait_ge(s_hot, t + 1)
            dve.sem_inc(s_gv, 1)
            pp = psP[:, :].rearrange("p (c y) -> p c y", y=HEADS * SLOTS)
            for k in range(HEADS):
                last = dve.tensor_tensor(PS[:, :, k * SLOTS:(k + 1) * SLOTS], pp[:, :, k * SLOTS:(k + 1) * SLOTS],
                                         slot[:, b, :, :], ALU.mult)
            ch.link(last)
            ch.link(dve.tensor_reduce(pe3[:, :, :], PS[:, :, :].rearrange("p c (k s) -> p c k s", s=SLOTS),
                                      AX, ALU.add))
            ch.link(dve.tensor_tensor(coef[:, :, :], pe3[:, :, :], spread(rec[:, q, RVAL, :], 2, [P, C, HEADS]),
                                      ALU.mult))
            for c in range(C):
                last = dve.tensor_tensor(S[:, b, c, P:K4 * P].rearrange("p (k i) -> p k i", i=P),
                                         spread(R[:, q, c, :], 1, [P, HEADS, P]),
                                         spread(coef[:, c, :], 2, [P, HEADS, P]), ALU.mult)
            last.then_inc(s_coef, 1)

        def step(t, q, h):
            b = q % 2
            ch.restart()
            if not over(t, NT):
                row_max(t, b)
            if not early(t, 2):
                gru.n_input(dve, ch, t - 2, b)
            if not over(t, NT):
                row_sum(t, b)
            if not over(t, NT - 1):
                list_rows(t + 1, (q + 1) % 4, 1 - b)
                edge_logits(t + 1, (q + 1) % 4, h + (q + 1) // 4, 1 - b)
            if not early(t, 2):
                gru.blend(dve, ch, t - 2, b, 16 * (2 * h + q // 2))
            if not over(t, NT):
                coefficients(t, q, b)
            if not over(t, NT - 3):
                list_edges(t + 3, (q + 3) % 4)

        for t in range(3):
            list_edges(t, t)
        list_rows(0, 0, 0)
        edge_logits(0, 0, 0, 0)
        all_steps_of_four(dve, step, 4)

    @block.scalar
    def _(act):
        def node_sum(t, q, b):
            act.wait_ge(s_hot, t + 1)
            if not early(t, 2):
                act.wait_ge(s_sup, t - 1)
            act.sem_inc(s_ga, 1)
            for c in range(C):
                last = act.activation(S[:, b, c, 0:P], R[:, q, c, :], ACT.Copy, scale=rec[:, q, RVAL, c:c + 1])
            last.then_inc(s_s0, 1)

        def step(t, q, h):
            b = q % 2
            if not over(t, NT):
                act.wait_ge(s_lgt, t + 1)
                act.sem_inc(s_ga, 1)
                act.activation(E[:, b, :, :], L[:, b, :, :], ACT.Exp).then_inc(s_p, 1)
            if not early(t, 2):
                gru.tanh_n(act, t - 2, b)
            if not over(t, NT):
                node_sum(t, q, b)
            if not (early(t, 1) or over(t, NT + 1)):
                act.wait_ge(s_sup, t)
                act.sem_inc(s_ga, 1)
                act.activation(supT[:, 1 - b, :, :].rearrange("p k i -> p (k i)"), psS[:, :], ACT.Copy)\
                    .then_inc(s_supc, 1)
                gru.copy_h(act, t - 1, 1 - b)
                gru.copy_support(act, t - 1, 1 - b)
                gru.tanh_rz(act, t - 1, 1 - b)
        all_steps_of_four(act, step)

    @block.tensor
    def _(pe):
        def step(t, q, h):
            b = q % 2
            a = 1 - b
            second = not (early(t, 1) or over(t, NT + 1))
            if not over(t, NT):
                pe.wait_ge(s_eo, t + 1)
                pe.wait_ge(s_hot, t + 1)
                pe.sem_inc(s_gt, 1)
                for c in range(C):
                    last = pe.matmul(psL[:, :], R[:, q, c, :], EO[:, c, :],
                                     start=(c == 0), stop=(c == C - 1))
                last.then_inc(s_l, 1)
            if second:
                pe.wait_ge(s_s0, t)
                pe.wait_ge(s_coef, t)
                if not early(t, 2):
                    pe.wait_ge(s_supc, t - 1)
                pe.sem_inc(s_gt, 1)
                for c in range(C):
                    last = pe.matmul(psS[:, :], G[:, (q + 3) % 4, c, 0:P], S[:, a, c, :], start=(c == 0), stop=(c == C - 1))
                last.then_inc(s_sup, 1)
                gru.turn_h(pe, t - 1, a, 16 * (2 * h + q // 2 + b))
            if not over(t, NT):
                pe.wait_ge(s_pn, t + 1)
                pe.sem_inc(s_gt, 1)
                for c in range(C):
                    last = pe.matmul(psP[:, c * HEADS * SLOTS:(c + 1) * HEADS * SLOTS], Q[:, b, c * P:(c + 1) * P],
                                     E[:, b, :, :].rearrange("p k s -> p (k s)"), start=True, stop=True)
                last.then_inc(s_pe, 1)
            if second:
                gru.support(pe, t - 1, a)
                gru.from_h(pe, t - 1, a, None if early(t, 3) else t - 2)
                gru.from_supports(pe, t - 1, a)
        all_steps_of_four(pe, step)


def tile_by_tile(eng, step):
    step(0)
    with eng.Fori(1, NT) as t:
        step(t)


class DenseSum:

    def __init__(self, tag, ctx, place, ps, sem, m, s_ga, s_gt):
        self.m, self.s_ga, self.s_gt = m, s_ga, s_gt
        self.T = place(4, P)
        self.psT = ps("psT_" + tag, [P, 4, P], F32, ctx)
        self.s_turned = sem("s_turned_" + tag, ctx)
        self.s_copied = sem("s_copied_" + tag, ctx)

    def turn(self, pe, src, n, multiply):
        for c in range(NT // 4):
            for j in range(4):
                at = (4 * c + j) * P
                last = pe.transpose(self.psT[:, j, :], src[:, at:at + P], self.m["ident"][:, :])
            last.then_inc(self.s_turned, 1)
            pe.wait_ge(self.s_copied, n * (NT // 4) + c + 1)
            pe.sem_inc(self.s_gt, 1)
            for j in range(4):
                last = multiply(4 * c + j, self.T[:, j, :], c + j == 0, 4 * c + j == NT - 1)
        return last

    def copy(self, act, n):
        for c in range(NT // 4):
            act.wait_ge(self.s_turned, n * (NT // 4) + c + 1)
            act.sem_inc(self.s_ga, 1)
            act.activation(self.T[:, :, :], self.psT[:, :, :], ACT.Copy).then_inc(self.s_copied, 1)


def weights_dense(nc, ctx, sb, ps, sem, m, x_d, adj_d):
    place = carve(m["maskT"][:, :, :].rearrange("p a b -> p (a b)"))
    A, B, X = place(N), place(N), place(NT, P)
    s_x, s_a, s_q, s_e, s_wt, s_sum, s_y, s_ch = (
        sem(n + "_wd", ctx) for n in ("x", "a", "q", "e", "wt", "sum", "y", "ch"))
    s_gv, s_gp, s_ga, s_gt, s_gs = m["gates"]
    ds = DenseSum("wd", ctx, place, ps, sem, m, s_ga, s_gt)
    psY = ps("psY_d", [P, 512], F32, ctx)
    block = ctx.enter_context(nc.Block())

    @block.gpsimd
    def _(pool):
        pool.dma_start(X[:, :, :], x_d.rearrange("(t p) c -> p t c", p=P)).then_inc(s_x, 16)

    @block.sync
    def _(sp):
        def load(t):
            if not isinstance(t, int):
                sp.wait_ge(s_y, t)
                sp.sem_inc(s_gs, 1)
            sp.dma_start(A[:, :], adj_d[bass.ds(t * P, P), :]).then_inc(s_a, 16)
        tile_by_tile(sp, load)

    @block.vector
    def _(dve):
        ch = Chain(dve, s_ch)

        def weigh(t):
            ch.restart()
            dve.wait_ge(s_a, 16 * (t + 1))
            dve.sem_inc(s_gv, 1)
            ch.link(dve.tensor_scalar(B[:, :], A[:, :], 0.0, 2.0, ALU.is_equal, ALU.mult))
            ch.link(dve.tensor_tensor(A[:, :], A[:, :], B[:, :], ALU.add))
            ch.link(dve.reciprocal(B[:, :], A[:, :]))
            ch.link(dve.tensor_scalar(B[:, :], B[:, :], -1.0, None, ALU.add))
            dve.tensor_tensor(B[:, :], B[:, :], B[:, :], ALU.mult).then_inc(s_q, 1)
            dve.wait_ge(s_e, t + 1)
            dve.sem_inc(s_gv, 1)
            ch.link(dve.scalar_tensor_tensor(A[:, :], A[:, :], 1.0, B[:, :], ALU.is_lt, ALU.mult))
            ch.link(dve.tensor_reduce(m["wsum"][:, bass.ds(t, 1)], A[:, :], AX, ALU.add))
            dve.sem_inc(s_wt, 1)
        tile_by_tile(dve, weigh)

    @block.scalar
    def _(act):
        def step(t):
            act.wait_ge(s_q, t + 1)
            act.sem_inc(s_ga, 1)
            act.activation(B[:, :], B[:, :], ACT.Exp, scale=-2.0).then_inc(s_e, 1)
            ds.copy(act, t)
            act.wait_ge(s_sum, t + 1)
            act.sem_inc(s_ga, 1)
            act.activation(m["yT"][:, t, :], psY[:, 0:P], ACT.Copy).then_inc(s_y, 1)
        tile_by_tile(act, step)

    @block.tensor
    def _(pe):
        pe.wait_ge(s_x, 16)

        def step(t):
            pe.wait_ge(s_wt, t + 1)
            if not isinstance(t, int):
                pe.wait_ge(s_y, t)
            pe.sem_inc(s_gt, 1)
            ds.turn(pe, A, t, lambda j, block_t, first, last: pe.matmul(
                psY[:, 0:P], X[:, j, :], block_t, start=first, stop=last)).then_inc(s_sum, 1)
        tile_by_tile(pe, step)


def logits_dense(nc, ctx, sb, ps, sem, m, w, adj_d, logit_d):
    place = carve(m["maskT"][:, :, :].rearrange("p a b -> p (a b)"))
    A, Mp, Mm = place(N), place(N), place(N)
    K2 = 2 * HEADS
    up, e6, l6 = place(2, K2), place(K2), place(K2)
    rows = place(N)
    s_a, s_m, s_u, s_e6, s_t, s_tc, s_out, s_ch = (
        sem(n + "_ld", ctx) for n in ("a", "m", "u", "e6", "t", "tc", "out", "ch"))
    s_gv, s_gp, s_ga, s_gt, s_gs = m["gates"]
    ds = DenseSum("ld", ctx, place, ps, sem, m, s_ga, s_gt)
    psU = ps("psU_d", [P, 2, 512], F32, ctx)
    psR = ps("psR_d", [P, 512], F32, ctx)
    block = ctx.enter_context(nc.Block())

    @block.sync
    def _(sp):
        def load(t):
            if not isinstance(t, int):
                sp.wait_ge(s_tc, t)
                sp.sem_inc(s_gs, 1)
            sp.dma_start(A[:, :], adj_d[bass.ds(t * P, P), :]).then_inc(s_a, 16)
        tile_by_tile(sp, load)
        sp.wait_ge(s_tc, NT)
        sp.dma_start(logit_d, rows[0:K2, :]).then_inc(s_out, 16)
        sp.wait_ge(s_out, 16)

    @block.vector
    def _(dve):
        ch = Chain(dve, s_ch)

        def step(t):
            ch.restart()
            dve.wait_ge(s_a, 16 * (t + 1))
            dve.sem_inc(s_gv, 1)
            blk = A[:, bass.ds(t * P, P)]
            ch.link(dve.tensor_tensor(blk, blk, m["offdiag"][:, :], ALU.mult))
            dve.tensor_scalar(Mp[:, :], A[:, :], 0.0, None, ALU.is_gt)
            dve.tensor_scalar(Mm[:, :], A[:, :], 0.0, None, ALU.is_lt).then_inc(s_m, 1)
            dve.wait_ge(s_u, t + 1)
            dve.sem_inc(s_gv, 1)
            ch.link(dve.tensor_copy(up[:, :, :], psU[:, :, 0:K2]))
            ch.link(dve.tensor_tensor(e6[:, 0:HEADS], up[:, 0, 0:HEADS], up[:, 1, HEADS:K2], ALU.add))
            ch.link(dve.tensor_tensor(e6[:, HEADS:K2], up[:, 1, 0:HEADS], up[:, 0, HEADS:K2], ALU.add))
            dve.scalar_tensor_tensor(l6[:, :], e6[:, :], 0.2, e6[:, :], ALU.mult, ALU.max).then_inc(s_e6, 1)
        tile_by_tile(dve, step)

    @block.scalar
    def _(act):
        def step(t):
            ds.copy(act, 2 * t)
            ds.copy(act, 2 * t + 1)
            act.wait_ge(s_t, t + 1)
            act.sem_inc(s_ga, 1)
            act.activation(rows[0:K2, bass.ds(t * P, P)], psR[0:K2, 0:P], ACT.Copy).then_inc(s_tc, 1)
        tile_by_tile(act, step)

    @block.tensor
    def _(pe):
        def step(t):
            pe.wait_ge(s_m, t + 1)
            pe.sem_inc(s_gt, 1)
            for n, mask in ((0, Mp), (1, Mm)):
                last = ds.turn(pe, mask, 2 * t + n, lambda j, block_t, first, last, n=n: pe.matmul(
                    psU[:, n, 0:K2], block_t, w["V"][:, j, :], start=first, stop=last))
            last.then_inc(s_u, 1)
            pe.wait_ge(s_e6, t + 1)
            if not isinstance(t, int):
                pe.wait_ge(s_tc, t)
            pe.sem_inc(s_gt, 1)
            pe.transpose(psR[0:K2, 0:P], l6[:, :], m["ident"][:, :]).then_inc(s_t, 1)
        tile_by_tile(pe, step)


def attention_dense(nc, ctx, sb, ps, sem, m, w, adj_d, table_d, logit_d):
    place = carve(m["maskT"][:, :, :].rearrange("p a b -> p (a b)"))
    K4 = HEADS + 1
    A, Mp, L, Ep, Em = (place(N) for _ in range(5))
    Mm = place(N)
    hall = place(NT, P)
    place = carve(m["yT"][:, :, :].rearrange("p a b -> p (a b)").bitcast(U8))
    hb = place(1, P)
    supT = place(1, K4, P)
    mx, den = place(1), place(1)
    psS = ps("psS_d", [P, K4, P], F32, ctx)
    s_all, s_h0, s_a, s_el, s_m, s_lk, s_lg, s_ex, s_s, s_sum, s_supc, s_ch = (
        sem(n + "_ad", ctx) for n in ("all", "h0", "a", "el", "m", "lk", "lg", "ex", "s", "sum", "supc", "ch"))
    s_gv, s_gp, s_ga, s_gt, s_gs = m["gates"]
    ds = DenseSum("ad", ctx, place, ps, sem, m, s_ga, s_gt)
    gru = Gru("d", ctx, place, ps, sem, m, w, hb, supT, [s_h0], s_supc, s_gv, s_ga, s_gt)
    block = ctx.enter_context(nc.Block())

    @block.sync
    def _(sp):
        sp.dma_start(hall[:, :, :], table_d.rearrange("(t p) c -> p t c", p=P)[:, :, 0:P]).then_inc(s_all, 16)

        def load(t):
            if not isinstance(t, int):
                sp.wait_ge(gru.s_res, t)
                sp.sem_inc(s_gs, 1)
            sp.dma_start(A[:, :], adj_d[bass.ds(t * P, P), :]).then_inc(s_a, 16)
            sp.dma_start(hb[:, 0, :], table_d[bass.ds(t * P, P), 0:P]).then_inc(s_h0, 16)
            for k in range(HEADS):
                if not (isinstance(t, int) and k == 0):
                    sp.wait_ge(s_lk, HEADS * t + k)
                    sp.sem_inc(s_gs, 1)
                sp.dma_start(Ep[:, :], logit_d[k, :].partition_broadcast(P)).then_inc(s_el, 16)
                sp.dma_start(Em[:, :], logit_d[HEADS + k, :].partition_broadcast(P)).then_inc(s_el, 16)
        tile_by_tile(sp, load)

    @block.vector
    def _(dve):
        ch = Chain(dve, s_ch)

        def step(t):
            ch.restart()
            dve.wait_ge(s_a, 16 * (t + 1))
            dve.sem_inc(s_gv, 1)
            blk = A[:, bass.ds(t * P, P)]
            ch.link(dve.tensor_tensor(blk, blk, m["offdiag"][:, :], ALU.mult))
            dve.tensor_scalar(Mp[:, :], A[:, :], 0.0, None, ALU.is_gt)
            ch.link(dve.tensor_scalar(Mm[:, :], A[:, :], 0.0, None, ALU.is_lt))
            dve.sem_inc(s_m, 1)
            for k in range(HEADS):
                if k:
                    dve.wait_ge(s_sum, K4 * t + k + 1)
                dve.wait_ge(s_el, 32 * (HEADS * t + k + 1))
                dve.sem_inc(s_gv, 1)
                ch.link(dve.memset(L[:, :], -BIG))
                ch.link(dve.copy_predicated(L[:, :], Mp[:, :].bitcast(I32), Ep[:, :]))
                ch.link(dve.copy_predicated(L[:, :], Mm[:, :].bitcast(I32), Em[:, :]))
                dve.sem_inc(s_lk, 1)
                ch.link(dve.tensor_reduce(mx[:, :], L[:, :], AX, ALU.max))
                ch.link(dve.tensor_scalar(L[:, :], L[:, :], mx[:, :], None, ALU.subtract))
                dve.sem_inc(s_lg, 1)
                dve.wait_ge(s_ex, HEADS * t + k + 1)
                dve.sem_inc(s_gv, 1)
                ch.link(dve.reciprocal(den[:, :], den[:, :]))
                ch.link(dve.scalar_tensor_tensor(L[:, :], L[:, :], den[:, :], A[:, :], ALU.mult, ALU.mult))
                dve.sem_inc(s_s, 1)
            gru.n_input(dve, ch, t, 0)
            gru.blend(dve, ch, t, 0, 16 * (t + 1))
        tile_by_tile(dve, step)

    @block.scalar
    def _(act):
        def step(t):
            gru.copy_h(act, t, 0)
            ds.copy(act, K4 * t)
            for k in range(HEADS):
                act.wait_ge(s_lg, HEADS * t + k + 1)
                act.sem_inc(s_ga, 1)
                act.activation(L[:, :], L[:, :], ACT.Exp, accum_out=den[:, :]).then_inc(s_ex, 1)
                ds.copy(act, K4 * t + k + 1)
            act.wait_ge(s_sum, K4 * (t + 1))
            act.sem_inc(s_ga, 1)
            act.activation(supT[:, 0, :, :], psS[:, :, :], ACT.Copy).then_inc(s_supc, 1)
            gru.copy_support(act, t, 0)
            gru.tanh_rz(act, t, 0)
            gru.tanh_n(act, t, 0)
        tile_by_tile(act, step)

    @block.tensor
    def _(pe):
        pe.wait_ge(s_all, 16)

        def step(t):
            gru.turn_h(pe, t, 0, 16 * (t + 1))
            for k in range(K4):
                if k == 0:
                    pe.wait_ge(s_m, t + 1)
                else:
                    pe.wait_ge(s_s, HEADS * t + k)
                pe.sem_inc(s_gt, 1)
                ds.turn(pe, L if k else A, K4 * t + k, lambda j, block_t, first, last, k=k: pe.matmul(
                    psS[:, k, :], hall[:, j, :], block_t, start=first, stop=last)).then_inc(s_sum, 1)
            gru.support(pe, t, 0)
            gru.from_h(pe, t, 0, None if isinstance(t, int) else t)
            gru.from_supports(pe, t, 0)
        tile_by_tile(pe, step)


def last_norm(nc, ctx, sb, ps, sem, m, w, out):
    s_ch, s_var, s_sd, s_n, s_out = (sem(n, ctx) for n in ("s_ch5", "s_var5", "s_sd5", "s_n5", "s_out"))
    CH = 8
    block = ctx.enter_context(nc.Block())

    @block.scalar
    def _(act):
        act.wait_ge(s_var, 1)
        act.activation(w["rstd"][:, :], w["rstd"][:, :], ACT.Sqrt).then_inc(s_sd, 1)

    @block.vector
    def _(dve):
        ch = Chain(dve, s_ch)
        finish_stats(dve, None, w, ch, s_var, s_sd)
        with dve.Fori(0, NT) as t:
            dve.tensor_scalar(w["H"][:, t, :], w["H"][:, t, :], w["mv"][:, t, 0:1],
                              w["rstd"][:, bass.ds(t, 1)], ALU.subtract, ALU.mult).then_inc(s_n, 1)

    @block.sync
    def _(sp):
        rows = out.rearrange("(t p) c -> p t c", p=P)
        for g in range(NT // CH):
            sp.wait_ge(s_n, CH * (g + 1))
            sp.dma_start(rows[:, CH * g:CH * (g + 1), :], w["H"][:, CH * g:CH * (g + 1), :]).then_inc(s_out, 16)
        sp.wait_ge(s_out, 16 * (NT // CH))


NAMES = ["x", "adj", "L0_gnn_W", "L0_gnn_B", "L1_gnn_gat_W", "L1_gnn_gat_a", "L1_gnn_edge_Wih", "L1_gnn_edge_Whh",
         "L1_gnn_edge_bih", "L1_gnn_edge_bhh", "L1_gnn_node_Wih", "L1_gnn_node_Whh", "L1_gnn_node_bih",
         "L1_gnn_node_bhh"]


def kernel(**inputs):
    import numpy as _np
    import concourse.bacc as _bacc
    from concourse.bass_utils import run_bass_kernel_spmd as _run

    nc = _bacc.Bacc("TRN2", target_bir_lowering=False, num_devices=1)
    arrays, tensors = {}, {}
    for name in NAMES:
        a = _np.ascontiguousarray(inputs[name])
        arrays[f"in_{name}"] = a
        tensors[name] = nc.dram_tensor(f"in_{name}", a.shape, mybir.dt.from_np(a.dtype), kind="ExternalInput").ap()
    out = nc.dram_tensor("out", (N, P), F32, kind="ExternalOutput").ap()
    build(nc, tensors, out)
    result = _run(nc, [arrays], core_ids=[0])
    return result.results[0]["out"]
```

```python
from contextlib import ExitStack

import concourse.bass as bass
from concourse import mybir

F32 = mybir.dt.float32
BF16 = mybir.dt.bfloat16
FP8 = mybir.dt.float8e4
U32 = mybir.dt.uint32
I32 = mybir.dt.int32
U8 = mybir.dt.uint8
ALU = mybir.AluOpType
ACT = mybir.ActivationFunctionType
AX = mybir.AxisListType.X

P = 128
N = 4096
NT = N // P
SEG = 4
SEGW = N // SEG
CAND = 8 * SEG
SLOTS = 16
CHUNKS = 5
EDGES = CHUNKS * P
RANK, KEY, VAL, BASE, OWN = 0, CAND, 2 * CAND, 3 * CAND, 3 * CAND + 1
PAY = OWN + 1
RKEY, RROW, RSLOT, RVAL = 0, 1, 2, 3
REC = 4
RECS = REC * CHUNKS + 1
HEADS = 3
ROW = P + 3
EPS = 1e-5
BIG = 9e15
FP8_ONE = 56


class Chain:

    def __init__(self, eng, sem):
        self.eng, self.sem, self.n = eng, sem, 0

    def restart(self):
        self.eng.sem_clear(self.sem)
        self.n = 0

    def mark(self, ins):
        self.n += 1
        ins.then_inc(self.sem, 1)

    def wait(self):
        self.eng.wait_ge(self.sem, self.n)

    def link(self, ins):
        self.mark(ins)
        self.wait()


def early(t, n):
    return isinstance(t, int) and t < n


def over(t, n):
    return isinstance(t, int) and t >= n


def all_steps(eng, step):
    for t in range(4):
        step(t, t % 2, t // 2)
    with eng.Fori(2, NT // 2) as i:
        step(2 * i, 0, i)
        step(2 * i + 1, 1, i)
    step(NT, 0, NT // 2)
    step(NT + 1, 1, NT // 2)


def all_steps_of_four(eng, step, before_last=0):
    for t in range(4):
        step(t, t, 0)
    with eng.Fori(1, (NT - before_last) // 4) as i:
        for j in range(4):
            step(4 * i + j, j, i)
    for t in range(NT - before_last, NT + 2):
        step(t, t % 4, t // 4)


def spread(ap, axis, shape):
    return ap.unsqueeze(axis).broadcast_to(shape)


def build(nc, d, out):
    x_d, adj_d = d["x"], d["adj"]
    table_d = nc.dram_tensor("node_table", (N, ROW), F32).ap()
    logit_d = nc.dram_tensor("logit_rows", (2 * HEADS, N), F32).ap()
    root = ExitStack()

    with root:
        def sb(name, shape, dt, ctx=root):
            return ctx.enter_context(nc.sbuf_tensor(name, shape, dt))

        def ps(name, shape, dt, ctx=root):
            return ctx.enter_context(nc.psum_tensor(name, shape, dt))

        def sem(name, ctx):
            return root.enter_context(nc.semaphore(name))

        m = {}
        m["gates"] = [sem("gate_" + e, root) for e in ("vector", "pool", "scalar", "tensor", "sync")]
        m["ident"] = sb("ident", [P, P], F32)
        m["identb"] = sb("identb", [P, P], BF16)
        m["offdiag"] = sb("offdiag", [P, P], BF16)
        m["ones"] = sb("ones", [P, 1], F32)
        m["segoff"] = sb("segoff", [P, CAND], F32)
        m["iota"] = sb("iota", [P, EDGES], F32)
        m["halves"] = sb("halves", [P, SLOTS], F32)
        m["edge1"] = sb("edge1", [P, CHUNKS], F32)
        m["before"] = sb("before", [P, P], F32)
        m["own"] = sb("own", [P, 1], F32)
        m["rec_all"] = sb("rec_all", [P, NT, RECS], F32)
        m["ends"] = sb("ends", [P, NT], F32)
        m["wsum"] = sb("wsum", [P, NT], F32)
        m["cnt"] = sb("cnt", [P, NT], F32)
        m["full"] = sb("full", [P, NT], F32)
        m["signs"] = sb("signs", [P, NT, SEG], F32)
        m["flag"] = sb("flag", [1, 1], I32)
        m["yT"] = sb("yT", [P, NT, P], F32)
        m["maskT"] = sb("maskT", [P, NT, N], U8)
        with ExitStack() as ctx:
            constants(nc, ctx, sb, sem, m)
        with ExitStack() as ctx:
            extract(nc, ctx, sb, ps, sem, m, x_d, adj_d)
        unfit = nc.values_load(m["flag"][0:1, 0:1], min_val=0, max_val=1)
        with nc.If(unfit != 0):
            with ExitStack() as ctx:
                weights_dense(nc, ctx, sb, ps, sem, m, x_d, adj_d)
        with ExitStack() as ctx:
            w = first_norm(nc, root, ctx, sb, ps, sem, m, d, table_d)
        unfit = nc.values_load(m["flag"][0:1, 0:1], min_val=0, max_val=1)
        with nc.If(unfit != 0):
            with ExitStack() as ctx:
                logits_dense(nc, ctx, sb, ps, sem, m, w, adj_d, logit_d)
            with ExitStack() as ctx:
                attention_dense(nc, ctx, sb, ps, sem, m, w, adj_d, table_d, logit_d, out)
        with nc.Else():
            with ExitStack() as ctx:
                logits(nc, ctx, sb, ps, sem, m, w, table_d)
            with ExitStack() as ctx:
                attention(nc, ctx, sb, ps, sem, m, w, table_d, out)


def constants(nc, ctx, sb, sem, m):
    oi = sb("own_i", [P, 1], I32, ctx)
    si = sb("segoff_i", [P, CAND], I32, ctx)
    ii = sb("iota_i", [P, EDGES], I32, ctx)
    ei = sb("edge_i", [P, CHUNKS], I32, ctx)
    s_iota, s_iotas = sem("s_iota", ctx), sem("s_iotas", ctx)
    s_fill = sem("s_fill", ctx)
    block = ctx.enter_context(nc.Block())

    @block.gpsimd
    def _(pool):
        pool.iota(oi[:, :], pattern=[[0, 1]], base=0, channel_multiplier=1)
        pool.iota(ii[:, :], pattern=[[1, EDGES]], base=0, channel_multiplier=0)
        pool.iota(ei[:, :], pattern=[[P, CHUNKS]], base=1, channel_multiplier=1)
        pool.iota(si[:, :].rearrange("p (g e) -> p g e", e=8), pattern=[[SEGW, SEG], [0, 8]], base=1,
                  channel_multiplier=0).then_inc(s_iota, 1)
        pool.memset(m["ones"][:, :], 1.0)
        pool.memset(m["before"][:, :], 1.0)
        pool.memset(m["offdiag"][:, :], 1.0)
        pool.memset(m["identb"][:, :], 0.0)
        pool.memset(m["ident"][:, :], 0.0).then_inc(s_fill, 1)
        pool.wait_ge(s_fill, 1)
        for t, op, fill in (("ident", ALU.not_equal, 1.0), ("identb", ALU.not_equal, 1.0),
                            ("offdiag", ALU.not_equal, 0.0)):
            pool.affine_select(out=m[t][:, :], in_=m[t][:, :], compare_op=op, fill=fill, base=0,
                               pattern=[[-1, P]], channel_multiplier=1)
        pool.affine_select(out=m["before"][:, :], in_=m["before"][:, :], compare_op=ALU.is_gt, fill=0.0,
                           base=0, pattern=[[1, P]], channel_multiplier=-1)

    @block.vector
    def _(dve):
        dve.wait_ge(s_iota, 1)
        dve.tensor_copy(m["own"][:, :], oi[:, :])
        dve.tensor_copy(m["iota"][:, :], ii[:, :])
        dve.tensor_copy(m["edge1"][:, :], ei[:, :])
        dve.tensor_copy(m["segoff"][:, :], si[:, :]).then_inc(s_iotas, 1)
        dve.wait_ge(s_iotas, 1)
        dve.tensor_scalar(m["halves"][:, :], m["iota"][:, 0:SLOTS], 0.5, None, ALU.mult)


def extract(nc, ctx, sb, ps, sem, m, x_d, adj_d):
    A = sb("A", [P, 2, N], F32, ctx)
    sg = sb("sg", [P, 2, SEGW], BF16, ctx)
    G = sb("G", [P, 2, CHUNKS, P], F32, ctx)
    S = sb("S", [P, 2, CHUNKS + 1, P], F32, ctx)
    xt = sb("xt", [P, 2, P], F32, ctx)
    pos = sb("pos", [P, CAND], U32, ctx)
    posf = sb("posf", [P, CAND], F32, ctx)
    there = sb("there", [P, CAND], F32, ctx)
    zero = sb("zero", [P, CAND], F32, ctx)
    pay = sb("pay", [P, 2, PAY], F32, ctx)
    cnt = sb("cnt1", [P, 1], F32, ctx)
    half = sb("half", [P, 1], F32, ctx)
    less = sb("less", [P, 1], F32, ctx)
    middle = sb("middle", [P, 1], F32, ctx)
    Q = sb("Q", [P, EDGES], F32, ctx)
    dtmp = sb("dtmp", [P, 2, P], F32, ctx)
    eo = sb("eo", [P, CHUNKS, CAND], F32, ctx)
    kv = sb("kv", [P, CHUNKS, 2, CAND], F32, ctx)
    rec = sb("rec", [P, 2, RECS], F32, ctx)
    idx = sb("idx", [P, 2, CHUNKS], U32, ctx)
    z = sb("z", [P, 2, CHUNKS + 1], F32, ctx)
    q = sb("q", [P, 2, CHUNKS + 1], F32, ctx)
    e = sb("e", [P, 2, CHUNKS + 1], F32, ctx)
    wt = sb("wt", [P, 2, CHUNKS + 1], F32, ctx)
    bad = Q[:, 0:4 * NT].rearrange("p (a t) -> p a t", t=NT)
    sgs = Q[:, 4 * NT:5 * NT]
    badrow = sb("badrow", [P, 1], F32, ctx)
    psT = ps("psT", [P, 2, SEGW], BF16, ctx)
    psE = ps("psE", [P, 2, 512], F32, ctx)
    psB = ps("psB", [P, 512], F32, ctx)
    psY = ps("psY", [P, 2, 512], F32, ctx)
    dsum = ps("dsum", [P, P], F32, ctx)

    s_adj = [sem(f"s_adj{b}", ctx) for b in range(2)]
    s_x = [sem(f"s_x{b}", ctx) for b in range(2)]
    s_gath = [sem(f"s_gath{b}", ctx) for b in range(2)]
    s_off = sem("s_off", ctx)
    s_diag = sem("s_diag", ctx)
    s_wt = sem("s_wt", ctx)
    s_mid = sem("s_mid", ctx)
    s_dist = sem("s_dist", ctx)
    s_scan = sem("s_scan", ctx)
    s_sign = sem("s_sign", ctx)
    s_turn = sem("s_turn", ctx)
    s_mask = sem("s_mask", ctx)
    s_cnt = sem("s_cnt", ctx)
    s_base = sem("s_base", ctx)
    s_pay = sem("s_pay", ctx)
    s_edge = sem("s_edge", ctx)
    s_idx = sem("s_idx", ctx)
    s_q = sem("s_q", ctx)
    s_exp = sem("s_exp", ctx)
    s_prod = sem("s_prod", ctx)
    s_sum = sem("s_sum", ctx)
    s_y = sem("s_y", ctx)
    s_v = sem("s_v", ctx)
    s_gv, s_gp, s_ga, s_gt, s_gs = m["gates"]
    s_bad, s_cntd = sem("s_bad", ctx), sem("s_cntd", ctx)
    block = ctx.enter_context(nc.Block())

    @block.sync
    def _(sp):
        def load(t, b, h):
            if not over(t, NT):
                if not early(t, 2):
                    sp.wait_ge(s_scan, t - 1)
                    sp.sem_inc(s_gs, 1)
                    sp.wait_ge(s_sign, SEG * (t - 1))
                    sp.sem_inc(s_gs, 1)
                sp.dma_start(A[:, b, :], adj_d[bass.ds(t * P, P), :]).then_inc(s_adj[b], 16)
            if not early(t, 2):
                if not early(t, 4):
                    sp.wait_ge(s_sum, t - 3)
                    sp.sem_inc(s_gs, 1)
                sp.dma_start(xt[:, b, :], x_d[bass.ds((t - 2) * P, P), :]).then_inc(s_x[b], 16)
        all_steps(sp, load)

    @block.gpsimd
    def _(pool):
        def clear(t, b, h):
            pool.wait_ge(s_adj[b], 16 * (h + 1))
            if not early(t, 2):
                pool.wait_ge(s_diag, t - 1)
            pool.sem_inc(s_gp, 1)
            blk = A[:, b, bass.ds(t * P, P)]
            pool.tensor_tensor(dtmp[:, b, :], blk, m["ident"][:, :], ALU.mult)
            pool.tensor_tensor(blk, blk, m["offdiag"][:, :], ALU.mult).then_inc(s_off, 1)

        def step(t, b, h):
            if not early(t, 2):
                pool.wait_ge(s_wt, t - 1)
                if not early(t, 4):
                    pool.wait_ge(s_sum, t - 3)
                pool.sem_inc(s_gp, 1)
                pool.tensor_scalar(S[:, b, CHUNKS, :], m["ident"][:, :], wt[:, b, CHUNKS:CHUNKS + 1], None, ALU.mult)
                for c in range(CHUNKS):
                    at = RROW * CHUNKS + c
                    last = pool.tensor_scalar(S[:, b, c, :], m["iota"][:, 0:P], rec[:, b, at:at + 1],
                                              wt[:, b, c:c + 1], ALU.is_equal, ALU.mult)
                last.then_inc(s_prod, 1)
            if not over(t, NT - 1):
                clear(t + 1, 1 - b, h + b)
            if not (early(t, 1) or over(t, NT + 1)):
                pool.wait_ge(s_idx, t)
                if not early(t, 3):
                    pool.wait_ge(s_sum, t - 2)
                pool.sem_inc(s_gp, 1)
                for c in range(CHUNKS):
                    pool.indirect_dma_start(G[:, 1 - b, c, :], None, x_d[:, :],
                                            bass.IndirectOffsetOnAxis(ap=idx[:, 1 - b, c:c + 1], axis=0))\
                        .then_inc(s_gath[1 - b], 16)

        clear(0, 0, 0)
        for t in range(4):
            step(t, t % 2, t // 2)
        with pool.Fori(2, NT // 2 - 1) as i:
            step(2 * i, 0, i)
            step(2 * i + 1, 1, i)
        for t in range(NT - 2, NT + 2):
            step(t, t % 2, t // 2)

    @block.vector
    def _(dve):
        ch = Chain(dve, s_v)

        def step(t, b, h):
            a = 1 - b
            scanned, packed, weighed = not over(t, NT), not (early(t, 1) or over(t, NT + 1)), not early(t, 2)
            ch.restart()
            top, key, rank = (pay[:, b, at:at + CAND] for at in (VAL, KEY, RANK))
            ed = psE[:, a, 0:CHUNKS * PAY].rearrange("p (c y) -> p c y", y=PAY)
            recs = rec[:, a, 0:REC * CHUNKS].rearrange("p (g c) -> p g c", c=CHUNKS)
            values = rec[:, a, RVAL * CHUNKS:RECS]
            shape = [P, CHUNKS, CAND]
            seg = lambda g: A[:, b, g * SEGW:(g + 1) * SEGW]
            best = lambda g: pay[:, b, VAL + 8 * g:VAL + 8 * g + 8]
            find = lambda g: dve.max_index(pos[:, 8 * g:8 * g + 8], best(g), seg(g))
            if scanned:
                dve.wait_ge(s_off, t + 1)
                dve.sem_inc(s_gv, 1)
                dve.max(best(0), seg(0))
            if weighed:
                dve.wait_ge(s_exp, t - 1)
                if not early(t, 4):
                    dve.wait_ge(s_prod, t - 3)
                dve.sem_inc(s_gv, 1)
                dve.scalar_tensor_tensor(wt[:, b, :], z[:, b, :], 1.0, e[:, b, :], ALU.is_lt, ALU.mult)\
                    .then_inc(s_wt, 1)
            if scanned:
                dve.max(best(1), seg(1))
                dve.max(best(2), seg(2))
            if packed:
                dve.wait_ge(s_edge, t)
                dve.wait_ge(s_diag, t)
                if not early(t, 3):
                    dve.wait_ge(s_prod, t - 2)
                dve.sem_inc(s_gv, 1)
                ch.mark(dve.tensor_tensor(recs[:, RSLOT, :], m["edge1"][:, :], ed[:, :, BASE], ALU.subtract))
                dve.tensor_copy(recs[:, RROW, :], ed[:, :, OWN])
            if scanned:
                ch.mark(dve.max(best(3), seg(3)))
            if scanned or packed:
                ch.wait()
            if packed:
                ch.mark(dve.tensor_tensor(eo[:, :, :], ed[:, :, RANK:RANK + CAND],
                                          spread(recs[:, RSLOT, :], 2, shape), ALU.is_equal))
            if scanned:
                ch.link(dve.tensor_scalar(there[:, :], top, 0.0, None, ALU.is_gt))
                ch.mark(dve.tensor_reduce(cnt[:, :], there[:, :], AX, ALU.add))
                find(0)
                ch.wait()
                dve.sem_inc(s_cnt, 1)
            if packed:
                ch.wait()
                ch.link(dve.tensor_tensor(kv[:, :, :, :], ed[:, :, KEY:KEY + 2 * CAND].rearrange(
                    "p c (g q) -> p c g q", g=2), spread(eo[:, :, :], 2, [P, CHUNKS, 2, CAND]), ALU.mult))
                ch.mark(dve.tensor_reduce(recs[:, RKEY:RVAL + 1:RVAL, :].rearrange("p g c -> p c g"),
                                          kv[:, :, :, :], AX, ALU.add))
            if scanned:
                find(1)
                ch.mark(dve.tensor_tensor_scan(posf[:, :], there[:, :], zero[:, :], 0.0, ALU.add, ALU.add))
            ch.wait()
            if packed:
                dve.tensor_scalar(idx[:, a, :], recs[:, RKEY, :], -1.0, 0.0, ALU.add, ALU.max).then_inc(s_idx, 1)
                ch.mark(dve.tensor_scalar(z[:, a, :], values, 0.0, 2.0, ALU.is_equal, ALU.mult))
                dve.tensor_copy(m["rec_all"][:, t - 1, :], rec[:, a, :])
            if scanned:
                dve.tensor_tensor(rank, posf[:, :], there[:, :], ALU.mult)
                find(2)
            if packed:
                ch.wait()
                ch.mark(dve.tensor_tensor(z[:, a, :], z[:, a, :], values, ALU.add))
            if scanned:
                dve.tensor_reduce(m["full"][:, bass.ds(t, 1)], pay[:, b, VAL + 7:VAL + CAND:8], AX, ALU.max)
                dve.wait_ge(s_base, t + 1)
                dve.sem_inc(s_gv, 1)
                ch.mark(dve.tensor_copy(pay[:, b, BASE:BASE + 1], psB[:, 0:1]))
                dve.tensor_scalar(less[:, :], psB[:, 0:1], -1.0, 0.5, ALU.mult, ALU.add)
                ch.mark(dve.tensor_scalar(half[:, :], cnt[:, :], 0.5, None, ALU.mult))
                dve.tensor_copy(m["cnt"][:, bass.ds(t, 1)], cnt[:, :])
            ch.wait()
            if packed:
                ch.mark(dve.reciprocal(q[:, a, :], z[:, a, :]))
            if scanned:
                dve.scalar_tensor_tensor(middle[:, :], half[:, :], -1.0, less[:, :], ALU.mult, ALU.add)\
                    .then_inc(s_mid, 1)
                dve.tensor_tensor(m["ends"][:, bass.ds(t, 1)], pay[:, b, BASE:BASE + 1], cnt[:, :], ALU.add)
            if packed:
                ch.wait()
            if scanned:
                ch.mark(find(3))
            if packed:
                ch.mark(dve.tensor_scalar(q[:, a, :], q[:, a, :], -1.0, None, ALU.add))
            ch.wait()
            if scanned:
                dve.sem_inc(s_scan, 1)
                ch.mark(dve.tensor_tensor(posf[:, :], pos[:, :], m["segoff"][:, :], ALU.add))
            if packed:
                dve.tensor_tensor(q[:, a, :], q[:, a, :], q[:, a, :], ALU.mult).then_inc(s_q, 1)
            if scanned:
                dve.wait_ge(s_dist, t + 1)
                dve.sem_inc(s_gv, 1)
                dve.tensor_scalar(Q[:, :], Q[:, :], half[:, :], None, ALU.is_lt)
                ch.wait()
                dve.tensor_tensor(key, posf[:, :], there[:, :], ALU.mult).then_inc(s_pay, 1)

        ch.link(dve.memset(zero[:, :], 0.0))
        dve.tensor_copy(pay[:, 0, OWN:OWN + 1], m["own"][:, :])
        ch.link(dve.tensor_copy(pay[:, 1, OWN:OWN + 1], m["own"][:, :]))
        all_steps(dve, step)
        ch.restart()
        dve.wait_ge(s_mask, NT * SEG)
        dve.wait_ge(s_edge, NT)
        ch.link(dve.tensor_reduce(sgs[:, :], m["signs"][:, :, :], AX, ALU.add))
        dve.tensor_tensor(bad[:, 0, :], sgs[:, :], m["cnt"][:, :], ALU.not_equal)
        dve.tensor_scalar(bad[:, 1, :], m["cnt"][:, :], float(SLOTS), None, ALU.is_gt)
        dve.tensor_scalar(bad[:, 2, :], m["ends"][:, :], float(EDGES), None, ALU.is_gt)
        ch.link(dve.tensor_scalar(bad[:, 3, :], m["full"][:, :], 0.0, None, ALU.is_gt))
        dve.tensor_reduce(badrow[:, :], Q[:, 0:4 * NT], AX, ALU.add)\
            .then_inc(s_bad, 1)
        dve.wait_ge(s_cntd, 1)
        dve.tensor_scalar(m["flag"][:, :], psB[0:1, 1:2], 1.0, None, ALU.min)

    @block.scalar
    def _(act):
        def signs(t, b, h):
            act.wait_ge(s_off, t + 1)
            act.sem_inc(s_ga, 1)
            act.activation(dsum[:, :], dtmp[:, b, :], ACT.Copy, accum_out=rec[:, b, RECS - 1:RECS])\
                .then_inc(s_diag, 1)
            for g in range(SEG):
                if not (early(t, 1) and g < 2):
                    act.wait_ge(s_turn, SEG * t + g - 1)
                    act.sem_inc(s_ga, 1)
                act.activation(sg[:, g % 2, :], A[:, b, g * SEGW:(g + 1) * SEGW], ACT.Sign,
                               accum_out=m["signs"][:, t, g:g + 1]).then_inc(s_sign, 1)
                if not (early(t, 1) and g < 1):
                    keep(t, g - 1)

        def keep(t, g):
            if g < 0:
                t, g = t - 1, SEG - 1
            act.wait_ge(s_turn, SEG * t + g + 1)
            act.sem_inc(s_ga, 1)
            act.activation(m["maskT"][:, 8 * g:8 * g + 8, bass.ds(t * P, P)],
                           psT[:, g % 2, :].rearrange("p (j i) -> p j i", i=P), ACT.Copy,
                           scale=float(FP8_ONE)).then_inc(s_mask, 1)

        def expo(t, b):
            act.wait_ge(s_q, t + 1)
            act.sem_inc(s_ga, 1)
            act.activation(e[:, b, :], q[:, b, :], ACT.Exp, scale=-2.0).then_inc(s_exp, 1)

        def keep_sum(t, b):
            act.wait_ge(s_sum, t + 1)
            act.sem_inc(s_ga, 1)
            act.activation(m["wsum"][:, bass.ds(t, 1)], psY[:, b, P:P + 1], ACT.Copy)
            act.activation(m["yT"][:, t, :], psY[:, b, 0:P], ACT.Copy).then_inc(s_y, 1)

        def step(t, b, h):
            if not early(t, 2):
                expo(t - 2, b)
            if not over(t, NT):
                signs(t, b, h)
            if over(t, NT) and not over(t, NT + 1):
                keep(NT - 1, SEG - 1)
            if not early(t, 3):
                keep_sum(t - 3, 1 - b)
            if not over(t, NT):
                act.wait_ge(s_mid, t + 1)
                act.sem_inc(s_ga, 1)
                act.activation(Q[:, :], m["iota"][:, :], ACT.Abs, bias=middle[:, :]).then_inc(s_dist, 1)

        all_steps(act, step)
        keep_sum(NT - 1, 1)

    @block.tensor
    def _(pe):
        def turn(t, b, h):
            for g in range(SEG):
                pe.wait_ge(s_sign, SEG * t + g + 1)
                if not (early(t, 1) and g < 2):
                    pe.wait_ge(s_mask, SEG * t + g - 1)
                pe.sem_inc(s_gt, 1)
                for j in range(8):
                    last = pe.transpose(psT[:, g % 2, j * P:(j + 1) * P], sg[:, g % 2, j * P:(j + 1) * P],
                                        m["identb"][:, :])
                last.then_inc(s_turn, 1)
                if g == 2:
                    pe.wait_ge(s_cnt, t + 1)
                    pe.sem_inc(s_gt, 1)
                    pe.matmul(psB[:, 0:1], m["before"][:, :], cnt[:, :], start=True, stop=True)\
                        .then_inc(s_base, 1)

        def hand_over(t, b):
            pe.wait_ge(s_pay, t + 1)
            pe.sem_inc(s_gt, 1)
            for c in range(CHUNKS):
                last = pe.matmul(psE[:, b, c * PAY:(c + 1) * PAY], Q[:, c * P:(c + 1) * P], pay[:, b, :],
                                 start=True, stop=True)
            last.then_inc(s_edge, 1)

        def total(t, b, h):
            pe.wait_ge(s_prod, t + 1)
            pe.wait_ge(s_gath[b], 16 * CHUNKS * (h + 1))
            pe.wait_ge(s_x[b], 16 * (h + 1))
            if not early(t, 2):
                pe.wait_ge(s_y, t - 1)
            pe.sem_inc(s_gt, 1)
            for c in range(CHUNKS + 1):
                rows = G[:, b, c, :] if c < CHUNKS else xt[:, b, :]
                pe.matmul(psY[:, b, 0:P], rows, S[:, b, c, :], start=(c == 0), stop=(c == CHUNKS))
            for c in range(CHUNKS + 1):
                last = pe.matmul(psY[:, b, P:P + 1], S[:, b, c, :], m["ones"][:, 0:1],
                                 start=(c == 0), stop=(c == CHUNKS))
            last.then_inc(s_sum, 1)

        def step(t, b, h):
            if not (early(t, 1) or over(t, NT + 1)):
                hand_over(t - 1, 1 - b)
            if not over(t, NT):
                turn(t, b, h)
            if not early(t, 2):
                total(t - 2, b, h - 1)
        all_steps(pe, step)
        pe.wait_ge(s_bad, 1)
        pe.matmul(psB[0:1, 1:2], badrow[:, :], m["ones"][:, 0:1], start=True, stop=True).then_inc(s_cntd, 1)


def first_norm(nc, root, ctx, sb, ps, sem, m, d, table_d):
    FOUR = 4
    NG = NT // FOUR
    w = {}
    w["W0"] = sb("W0", [P, P], F32, root)
    w["gatW"] = sb("gatW", [P, HEADS, P], F32, root)
    w["ih"] = sb("ihT", [P, 2, 3 * P], F32, root)
    w["hh"] = sb("hhT", [P, 2, 3 * P], F32, root)
    w["bias3"] = sb("bias3", [3, 2, 4 * P], BF16, root)
    w["ones3"] = sb("ones3", [3, P], BF16, root)
    w["V"] = sb("V", [P, NT, 2 * HEADS], F32, root)
    w["H"] = sb("H", [P, NT, P], F32, root)
    w["mv"] = sb("mv_all", [P, NT, 2], F32, root)
    w["rstd"] = sb("rstd", [P, NT], F32, root)
    m["power"] = sb("power", [P, FOUR], F32, root)
    s_var = sem("s_var", ctx)
    s_sd = sem("s_sd", ctx)
    s_pow = sem("s_pow", ctx)
    bias_d = nc.dram_tensor("bias_rows", (3, 8 * P), BF16).ap()
    B0 = sb("B0", [P, P], F32, ctx)
    WA = sb("WA", [P, 2 * HEADS], F32, ctx)
    a6 = sb("a6", [2 * HEADS, P], F32, ctx)
    a6T = sb("a6T", [P, 2 * HEADS], F32, ctx)
    gwT = sb("gwT", [P, HEADS, P], F32, ctx)
    raw = sb("raw", [P, 4, 3, P], F32, ctx)
    bi = sb("bi", [8, P], F32, ctx)
    bh = sb("bh", [8, P], F32, ctx)
    parts = sb("bias_parts", [8, 3, P], BF16, ctx)
    H = w["H"]
    hT = sb("hT", [P, 2, FOUR, P], F32, ctx)
    yb = sb("yb", [P, 2, FOUR, P], F32, ctx)
    hb = yb
    st = sb("st", [P, FOUR, 6], F32, ctx)
    mv = sb("mv", [P, FOUR, 2], F32, ctx)
    psM = ps("psM", [P, 2, FOUR, P], F32, ctx)
    pw = ps("pw", [P, 4, 512], F32, ctx)
    pg = ps("pg", [P, 512], F32, ctx)
    small = ps("small", [P, 512], F32, ctx)
    pa, pwa = small[:, 0:2 * HEADS], small[:, 16:16 + 2 * HEADS]
    psV = small[:, 64:64 + NT * 2 * HEADS].rearrange("p (t k) -> p t k", k=2 * HEADS)
    s_w0 = sem("s_load0", ctx)
    s_w = sem("s_load", ctx)
    s_t, s_c, s_o = sem("s_turned", ctx), sem("s_copied", ctx), sem("s_wa", ctx)
    s_wac = sem("s_wac", ctx)
    s_b, s_bc, s_bd = sem("s_bias", ctx), sem("s_bias_chain", ctx), sem("s_bias_moved", ctx)
    s_zero, s_bl = sem("s_zero", ctx), sem("s_bias_loaded", ctx)
    s_x = [sem(f"s_x2{b}", ctx) for b in range(2)]
    s_yb = sem("s_yb", ctx)
    s_mm = sem("s_mm", ctx)
    s_pre = sem("s_pre", ctx)
    s_xb = sem("s_xb", ctx)
    s_h = sem("s_h", ctx)
    s_ht = sem("s_ht", ctx)
    s_htc = sem("s_htc", ctx)
    s_v = sem("s_v2", ctx)
    s_tab = [sem(f"s_tab{b}", ctx) for b in range(2)]
    s_ch = sem("s_ch2", ctx)
    s_gv, s_gp, s_ga, s_gt, s_gs = m["gates"]
    names = [("L1_gnn_edge_Wih", "ih", 0), ("L1_gnn_node_Wih", "ih", 1),
             ("L1_gnn_edge_Whh", "hh", 0), ("L1_gnn_node_Whh", "hh", 1)]
    loads = [(w["gatW"][:, :, :], d["L1_gnn_gat_W"].rearrange("k c e -> c k e")),
             (a6[:, :], d["L1_gnn_gat_a"].rearrange("k (g e) o -> (k g) (e o)", g=2))]
    bias_loads = []
    for j, gru in enumerate(("edge", "node")):
        of_x = d[f"L1_gnn_{gru}_bih"].rearrange("(g p) -> g p", p=P)
        of_h = d[f"L1_gnn_{gru}_bhh"].rearrange("(g p) -> g p", p=P)
        bias_loads += [(bi[4 * j:4 * j + 3, :], of_x), (bh[4 * j:4 * j + 2, :], of_h[0:2, :]),
                       (bh[4 * j + 3:4 * j + 4, :], of_h[2:3, :])]
    loads += [(raw[:, i, :, :], d[n].rearrange("(g p) c -> p g c", p=P)) for i, (n, _, _) in enumerate(names)]
    block = ctx.enter_context(nc.Block())

    def all_groups(eng, step):
        step(0, 0, 0)
        step(1, 1, 0)
        with eng.Fori(1, NG // 2) as i:
            step(2 * i, 0, i)
            step(2 * i + 1, 1, i)

    def rows_of(dram, g):
        return dram[bass.ds(g * (FOUR * P), FOUR * P), 0:P].rearrange("(t p) c -> p t c", p=P)

    @block.sync
    def _(sp):
        sp.dma_start(w["W0"][:, :], d["L0_gnn_W"]).then_inc(s_w0, 16)
        sp.dma_start(B0[:, :], d["L0_gnn_B"].partition_broadcast(P)).then_inc(s_w0, 16)

        def load(g, b, h):
            if not early(g, 2):
                sp.wait_ge(s_x[b], 16 * h)
                sp.sem_inc(s_gs, 1)
            sp.dma_start(H[:, bass.ds(g * FOUR, FOUR), :], rows_of(d["x"], g)).then_inc(s_x[b], 16)
        all_groups(sp, load)

        def store(g, b, h):
            sp.wait_ge(s_h, g + 1)
            sp.sem_inc(s_gs, 1)
            sp.dma_start(rows_of(table_d, g), hb[:, b, :, :]).then_inc(s_tab[b], 16)
        all_groups(sp, store)
        for b in range(2):
            sp.wait_ge(s_tab[b], 16 * NG // 2)

    @block.gpsimd
    def _(pool):
        pool.wait_ge(s_zero, 1)
        for dst, src in bias_loads:
            pool.dma_start(dst, src).then_inc(s_bl, 16)
        for dst, src in loads:
            pool.dma_start(dst, src).then_inc(s_w, 16)
        pool.memset(m["power"][:, :], -0.5).then_inc(s_pow, 1)
        pool.wait_ge(s_pow, 1)

        def power(g, b, h):
            pool.wait_ge(s_var, g + 1)
            pool.sem_inc(s_gp, 1)
            four = w["rstd"][:, bass.ds(g * FOUR, FOUR)]
            pool.tensor_tensor(four, four, m["power"][:, :], ALU.pow).then_inc(s_sd, 1)
        all_groups(pool, power)
        pool.wait_ge(s_b, 1)
        pool.dma_start(bias_d.rearrange("j (q c) -> q j c", c=P), parts[:, :, :]).then_inc(s_bd, 16)
        pool.wait_ge(s_bd, 16)
        pool.dma_start(w["bias3"][:, :, :], bias_d.rearrange("j (g c) -> j g c", g=2)).then_inc(s_bd, 16)
        pool.wait_ge(s_bd, 32)

    @block.scalar
    def _(act):
        def fetch(g, b, h):
            if not early(g, 2):
                act.wait_ge(s_mm, g - 1)
                act.sem_inc(s_ga, 1)
            act.activation(yb[:, b, :, :], m["yT"][:, bass.ds(g * FOUR, FOUR), :], ACT.Copy).then_inc(s_yb, 1)
        all_groups(act, fetch)

        def copy(g, b, h):
            act.wait_ge(s_ht, g + 1)
            if not early(g, 2):
                act.wait_ge(s_v, g - 1)
            act.sem_inc(s_ga, 1)
            act.activation(hT[:, b, :, :], psM[:, b, :, :], ACT.Copy).then_inc(s_htc, 1)
        all_groups(act, copy)

    @block.tensor
    def _(pe):
        pe.wait_ge(s_w0, 32)

        def product(g, b, h):
            pe.wait_ge(s_yb, g + 1)
            if not early(g, 2):
                pe.wait_ge(s_pre, g - 1)
            pe.sem_inc(s_gt, 1)
            for j in range(FOUR):
                last = pe.matmul(psM[:, b, j, :], yb[:, b, j, :], w["W0"][:, :], start=True, stop=True)
            last.then_inc(s_mm, 1)
        all_groups(pe, product)
        pe.wait_ge(s_w, 16 * len(loads))
        for i in range(4):
            for g in range(3):
                pe.transpose(pw[:, i, g * P:(g + 1) * P], raw[:, i, g, :], m["ident"][:, :])
        for k in range(HEADS):
            pe.transpose(pg[:, k * P:(k + 1) * P], w["gatW"][:, k, :], m["ident"][:, :])
        pe.transpose(pa, a6[:, :], m["ident"][0:2 * HEADS, 0:2 * HEADS]).then_inc(s_t, 1)
        pe.wait_ge(s_c, 1)
        for k in range(HEADS):
            last = pe.matmul(pwa[:, 2 * k:2 * k + 2], gwT[:, k, :], a6T[:, 2 * k:2 * k + 2],
                             start=True, stop=True)
        last.then_inc(s_o, 1)
        pe.wait_ge(s_wac, 1)
        pe.wait_ge(s_pre, NG)

        def turn(g, b):
            pe.wait_ge(s_h, g + 1)
            if not early(g, 2):
                pe.wait_ge(s_htc, g - 1)
            pe.sem_inc(s_gt, 1)
            for j in range(FOUR):
                last = pe.transpose(psM[:, b, j, :], hb[:, b, j, :], m["ident"][:, :])
            last.then_inc(s_ht, 1)

        def values(g, b):
            pe.wait_ge(s_htc, g + 1)
            pe.sem_inc(s_gt, 1)
            for j in range(FOUR):
                last = pe.matmul(psV[:, g * FOUR + j, :], hT[:, b, j, :], WA[:, :], start=True, stop=True)
            last.then_inc(s_v, 1)

        def step(g, b, h):
            turn(g, b)
            if not early(g, 1):
                values(g - 1, 1 - b)
        all_groups(pe, step)
        values(NG - 1, 1)

    @block.vector
    def _(dve):
        ch = Chain(dve, s_ch)
        dve.memset(bi[:, :], 0.0)
        dve.memset(bh[:, :], 0.0).then_inc(s_zero, 1)
        dve.memset(w["ones3"][:, :], 1.0)
        dve.wait_ge(s_w0, 32)

        def biased(g, b, h):
            dve.wait_ge(s_x[b], 16 * (h + 1))
            dve.sem_inc(s_gv, 1)
            for j in range(FOUR):
                row = H[:, g * FOUR + j, :]
                last = dve.scalar_tensor_tensor(row, B0[:, :], m["wsum"][:, bass.ds(g * FOUR + j, 1)], row,
                                                ALU.mult, ALU.add)
            last.then_inc(s_xb, 1)

        def rows(g, b, h, last_one=False):
            ch.restart()
            dve.wait_ge(s_xb, g + 1)
            dve.wait_ge(s_mm, g + 1)
            dve.sem_inc(s_gv, 1)
            four = H[:, bass.ds(g * FOUR, FOUR), :]
            ch.mark(dve.tensor_tensor(four, psM[:, b, :, :], four, ALU.add))
            if not last_one:
                biased(g + 1, 1 - b, h + b)
            ch.wait()
            dve.sem_inc(s_pre, 1)
            for j in range(FOUR):
                last = dve.bn_stats(st[:, j, :], w["H"][:, g * FOUR + j, :])
            ch.link(last)
            for j in range(FOUR):
                last = dve.bn_aggr(mv[:, j, :], st[:, j, :])
            ch.link(last)
            dve.tensor_copy(w["mv"][:, bass.ds(g * FOUR, FOUR), :], mv[:, :, :])
            dve.tensor_scalar(w["rstd"][:, bass.ds(g * FOUR, FOUR)], mv[:, :, 1], EPS, None, ALU.add)\
                .then_inc(s_var, 1)
        biased(0, 0, 0)
        rows(0, 0, 0)
        rows(1, 1, 0)
        with dve.Fori(1, NG // 2 - 1) as i:
            rows(2 * i, 0, i)
            rows(2 * i + 1, 1, i)
        rows(NG - 2, 0, NG // 2 - 1)
        rows(NG - 1, 1, NG // 2 - 1, last_one=True)
        dve.wait_ge(s_t, 1)
        dve.tensor_copy(a6T[:, :], pa)
        dve.tensor_copy(gwT[:, :, :], pg[:, 0:3 * P].rearrange("p (k c) -> p k c", k=HEADS)).then_inc(s_c, 1)
        bias = Chain(dve, s_bc)
        dve.wait_ge(s_bl, 16 * len(bias_loads))
        bias.link(dve.tensor_tensor(bi[:, :], bi[:, :], bh[:, :], ALU.add))
        for j in range(3):
            bias.link(dve.tensor_copy(parts[:, j, :], bi[:, :]))
            if j < 2:
                bias.link(dve.tensor_tensor(bi[:, :], bi[:, :], parts[:, j, :], ALU.subtract))
        dve.sem_inc(s_b, 1)
        dve.wait_ge(s_o, 1)
        dve.tensor_copy(WA[:, :].rearrange("p (g k) -> p k g", g=2),
                        pwa.rearrange("p (k g) -> p k g", g=2)).then_inc(s_wac, 1)

        dve.wait_ge(s_sd, NG)

        def normalise(g, b, h):
            if not early(g, 2):
                dve.wait_ge(s_tab[b], 16 * h)
                dve.wait_ge(s_ht, g - 1)
                dve.sem_inc(s_gv, 1)
            for j in range(FOUR):
                t = g * FOUR + j
                last = dve.tensor_scalar(hb[:, b, j, :], w["H"][:, t, :], w["mv"][:, t, 0:1],
                                         w["rstd"][:, bass.ds(t, 1)], ALU.subtract, ALU.mult)
            last.then_inc(s_h, 1)
        all_groups(dve, normalise)
        for i, (_, key, j) in enumerate(names):
            dve.tensor_copy(w[key][:, j, :], pw[:, i, 0:3 * P])
        dve.wait_ge(s_v, NG)
        dve.tensor_copy(w["V"][:, :, :], psV)
    return w


def logits(nc, ctx, sb, ps, sem, m, w, table_d):
    M9 = 3 * HEADS
    W = 512
    rest = sb("rest", [P, NT, HEADS], F32, ctx)
    parts = sb("parts", [P, NT, M9], BF16, ctx)
    U = sb("U", [M9, N], F32, ctx)
    comb = sb("comb", [M9, HEADS], F32, ctx)
    lg = sb("lg", [P, NT, HEADS], F32, ctx)
    lk = sb("lk", [P, NT, HEADS], F32, ctx)
    psU = ps("psU", [P, 2, W], F32, ctx)
    psL = ps("psL", [P, NT, HEADS], F32, ctx)
    s_comb, s_c3 = sem("s_comb", ctx), sem("s_ch3", ctx)
    s_parts, s_u, s_uc, s_l, s_e, s_out = (sem(n, ctx) for n in
                                           ("s_parts", "s_u", "s_uc", "s_l", "s_e", "s_logit"))
    block = ctx.enter_context(nc.Block())

    @block.gpsimd
    def _(pool):
        pool.memset(comb[:, :], 0.0).then_inc(s_comb, 1)
        for j in range(3):
            pool.wait_ge(s_comb, j + 1)
            pool.affine_select(out=comb[:, :], in_=comb[:, :], compare_op=ALU.not_equal, fill=1.0,
                               base=-HEADS * j, pattern=[[-1, HEADS]], channel_multiplier=1).then_inc(s_comb, 1)

    @block.vector
    def _(dve):
        ch = Chain(dve, s_c3)
        ch.link(dve.tensor_copy(rest[:, :, :], w["V"][:, :, 0:HEADS]))
        for j in range(3):
            part = parts[:, :, j * HEADS:(j + 1) * HEADS]
            ch.link(dve.tensor_copy(part, rest[:, :, :]))
            if j < 2:
                ch.link(dve.tensor_tensor(rest[:, :, :], rest[:, :, :], part, ALU.subtract))
        dve.sem_inc(s_parts, 1)
        dve.wait_ge(s_l, 1)
        ch.link(dve.tensor_copy(lg[:, :, :], psL[:, :, :]))
        dve.scalar_tensor_tensor(lk[:, :, :], lg[:, :, :], 0.2, lg[:, :, :], ALU.mult, ALU.max).then_inc(s_e, 1)

    @block.tensor
    def _(pe):
        pe.wait_ge(s_parts, 1)
        for c in range(N // W):
            if c >= 2:
                pe.wait_ge(s_uc, c - 1)
            for j in range(NT):
                last = pe.matmul(psU[0:M9, c % 2, :], parts[:, j, :],
                                 m["maskT"][:, j, c * W:(c + 1) * W].bitcast(FP8),
                                 start=(j == 0), stop=(j == NT - 1))
            last.then_inc(s_u, 1)
        pe.wait_ge(s_comb, 4)
        pe.wait_ge(s_uc, N // W)
        for t in range(NT):
            last = pe.matmul(psL[:, t, :], U[:, t * P:(t + 1) * P], comb[:, :], start=True, stop=True)
        last.then_inc(s_l, 1)

    @block.scalar
    def _(act):
        for c in range(N // W):
            act.wait_ge(s_u, c + 1)
            act.activation(U[:, c * W:(c + 1) * W], psU[0:M9, c % 2, :], ACT.Copy).then_inc(s_uc, 1)

    @block.sync
    def _(sp):
        sp.wait_ge(s_e, 1)
        sp.dma_start(table_d.rearrange("(t p) c -> p t c", p=P)[:, :, P:P + HEADS], lk[:, :, :],
                     allow_slow_non_contiguous=True).then_inc(s_out, 16)
        sp.wait_ge(s_out, 16)


def carve(region):
    at = [0]

    def place(*shape, dt=F32):
        n = 4
        for x in shape:
            n *= x
        ap = region[:, at[0]:at[0] + n].bitcast(dt)
        at[0] += n
        assert at[0] <= region.shape[1]
        if len(shape) == 2:
            return ap.rearrange("p (a b) -> p a b", b=shape[1])
        if len(shape) == 3:
            return ap.rearrange("p (a b c) -> p a b c", b=shape[1], c=shape[2])
        if len(shape) == 4:
            return ap.rearrange("p (a b c e) -> p a b c e", b=shape[1], c=shape[2], e=shape[3])
        return ap
    return place


class Gru:

    def __init__(self, tag, ctx, place, ps, sem, m, w, hb, supT, s_h, s_supc):
        self.m, self.w, self.hb, self.supT = m, w, hb, supT
        self.s_h, self.s_supc = s_h, s_supc
        self.s_gv, self.s_gp, self.s_ga, self.s_gt, self.s_gs = m["gates"]
        bufs = 2 if tag == "" else 1
        self.hT = place(bufs, P)
        self.nsT = place(bufs, P)
        self.g1 = place(bufs, 2, 2 * P)
        self.nn = place(bufs, 2, P)
        self.nt = place(bufs, 2, P)
        self.df = place(2, P)
        self.oo = place(P)
        self.st = place(6)
        self.mv = place(bufs, 2)
        self.root = place(bufs, 1)
        bank = ps("psHN" + tag, [P, 2, P], F32, ctx)
        self.psH, self.psN = bank[:, 0, :], bank[:, 1, :]
        self.psG = ps("psG" + tag, [P, bufs, 2, 4 * P], F32, ctx)
        self.s_ht = sem("s_ht3" + tag, ctx)
        self.s_htc = sem("s_htc3" + tag, ctx)
        self.s_ns = sem("s_ns" + tag, ctx)
        self.s_nsc = sem("s_nsc" + tag, ctx)
        self.s_gru = sem("s_gru" + tag, ctx)
        self.s_g1 = sem("s_g1" + tag, ctx)
        self.s_nn = sem("s_nn" + tag, ctx)
        self.s_nt = sem("s_nt" + tag, ctx)
        self.s_res = sem("s_res" + tag, ctx)
        self.s_var = sem("s_var3" + tag, ctx)
        self.s_root = sem("s_root" + tag, ctx)
        self.s_out = sem("s_rows" + tag, ctx)

    def turn_h(self, pe, t, b, landed):
        pe.wait_ge(self.s_h[b], landed)
        if not early(t, 1):
            pe.wait_ge(self.s_nsc, t)
        pe.sem_inc(self.s_gt, 1)
        pe.transpose(self.psH, self.hb[:, b, :], self.m["ident"][:, :]).then_inc(self.s_ht, 1)

    def copy_h(self, act, t, b):
        act.wait_ge(self.s_ht, t + 1)
        act.sem_inc(self.s_ga, 1)
        act.activation(self.hT[:, b, :], self.psH, ACT.Copy).then_inc(self.s_htc, 1)

    def support(self, pe, t, b):
        pe.wait_ge(self.s_supc, t + 1)
        pe.wait_ge(self.s_htc, t + 1)
        pe.sem_inc(self.s_gt, 1)
        for k in range(HEADS):
            last = pe.matmul(self.psN, self.w["gatW"][:, k, :], self.supT[:, b, k + 1, :],
                             start=(k == 0), stop=(k == HEADS - 1))
        last.then_inc(self.s_ns, 1)

    def copy_support(self, act, t, b):
        act.wait_ge(self.s_ns, t + 1)
        act.sem_inc(self.s_ga, 1)
        act.activation(self.nsT[:, b, :], self.psN, ACT.Copy, scale=1.0 / HEADS).then_inc(self.s_nsc, 1)

    def from_h(self, pe, t, b, read=None):
        w, psG = self.w, self.psG[:, b]
        if read is not None:
            pe.wait_ge(self.s_nn, read)
        pe.wait_ge(self.s_htc, t + 1)
        pe.sem_inc(self.s_gt, 1)
        for j in range(2):
            pe.matmul(psG[:, j, :], w["ones3"][:, :], w["bias3"][:, j, :], start=True, stop=False)
            pe.matmul(psG[:, j, 0:2 * P], self.hT[:, b, :], w["hh"][:, j, 0:2 * P], start=False, stop=False)
            pe.matmul(psG[:, j, 3 * P:4 * P], self.hT[:, b, :], w["hh"][:, j, 2 * P:3 * P],
                      start=False, stop=False)

    def from_supports(self, pe, t, b):
        pe.wait_ge(self.s_nsc, t + 1)
        pe.sem_inc(self.s_gt, 1)
        for j in range(2):
            last = pe.matmul(self.psG[:, b, j, 0:3 * P], self.nsT[:, b, :] if j else self.supT[:, b, 0, :],
                             self.w["ih"][:, j, :], start=False, stop=True)
        last.then_inc(self.s_gru, 1)

    def tanh_rz(self, act, t, b):
        act.wait_ge(self.s_gru, t + 1)
        act.sem_inc(self.s_ga, 1)
        act.activation(self.g1[:, b, :, :], self.psG[:, b, :, 0:2 * P], ACT.Tanh, scale=0.5).then_inc(self.s_g1, 1)

    def tanh_n(self, act, t, b):
        act.wait_ge(self.s_nn, t + 1)
        act.sem_inc(self.s_ga, 1)
        act.activation(self.nt[:, b, :, :], self.nn[:, b, :, :], ACT.Tanh).then_inc(self.s_nt, 1)


    def n_input(self, dve, ch, t, b, part):
        nn, psG = self.nn[:, b], self.psG[:, b]
        if part == 0:
            dve.wait_ge(self.s_g1, t + 1)
            dve.sem_inc(self.s_gv, 1)
            ch.mark(dve.scalar_tensor_tensor(nn[:, :, :], self.g1[:, b, :, 0:P], 1.0, psG[:, :, 3 * P:4 * P],
                                             ALU.add, ALU.mult))
        elif part == 1:
            ch.wait()
            dve.scalar_tensor_tensor(nn[:, :, :], nn[:, :, :], 0.5, psG[:, :, 2 * P:3 * P],
                                     ALU.mult, ALU.add).then_inc(self.s_nn, 1)

    def blend(self, dve, ch, t, b, landed, part):
        m, w, hb = self.m, self.w, self.hb
        g1, nt, df, oo, st, mv = self.g1[:, b], self.nt[:, b], self.df, self.oo, self.st, self.mv[:, b, :]
        if part == 0:
            dve.wait_ge(self.s_nt, t + 1)
            dve.wait_ge(self.s_h[b], landed)
            dve.sem_inc(self.s_gv, 1)
            ch.mark(dve.tensor_tensor(df[:, :, :], spread(hb[:, b, :], 1, [P, 2, P]), nt[:, :, :], ALU.subtract))
            return
        ch.wait()
        if part == 1:
            ch.mark(dve.scalar_tensor_tensor(df[:, :, :], g1[:, :, P:2 * P], 1.0, df[:, :, :], ALU.add, ALU.mult))
        elif part == 2:
            ch.mark(dve.scalar_tensor_tensor(df[:, :, :], df[:, :, :], 0.5, nt[:, :, :], ALU.mult, ALU.add))
        elif part == 3:
            ch.mark(dve.tensor_tensor(oo[:, :], df[:, 0, :], df[:, 1, :], ALU.add))
        elif part == 4:
            ch.mark(dve.scalar_tensor_tensor(w["H"][:, t, :], oo[:, :], m["rec_all"][:, t, RECS - 1:RECS],
                                             hb[:, b, :], ALU.mult, ALU.add))
        elif part == 5:
            dve.sem_inc(self.s_res, 1)
            ch.mark(dve.bn_stats(st[:, :], w["H"][:, t, :]))
        elif part == 6:
            ch.mark(dve.bn_aggr(mv, st[:, :]))
        elif part == 7:
            dve.tensor_scalar(self.root[:, b, :], mv[:, 1:2], EPS, None, ALU.add).then_inc(self.s_var, 1)

    def power(self, pool, t, b):
        pool.wait_ge(self.s_var, t + 1)
        pool.sem_inc(self.s_gp, 1)
        pool.tensor_tensor(self.root[:, b, :], self.root[:, b, :], self.m["power"][:, 0:1], ALU.pow)\
            .then_inc(self.s_root, 1)

    def normalise(self, dve, t, b):
        dve.wait_ge(self.s_root, t + 1)
        dve.sem_inc(self.s_gv, 1)
        dve.tensor_scalar(self.w["H"][:, t, :], self.w["H"][:, t, :], self.mv[:, b, 0:1], self.root[:, b, :],
                          ALU.subtract, ALU.mult).then_inc(self.s_out, 1)


def attention(nc, ctx, sb, ps, sem, m, w, table_d, out):
    place = carve(m["maskT"][:, :, :].rearrange("p a b -> p (a b)"))
    K4 = HEADS + 1
    C = CHUNKS
    G = place(4, C, ROW)
    R = place(4, C, P)
    Q = place(2, EDGES)
    S = place(2, C, K4 * P)
    recs = place(4, RECS)
    rec = recs[:, :, 0:REC * C].rearrange("p b (g c) -> p b g c", c=C)
    idx = place(4, C, dt=U32)
    rows = place(2, 3)
    slot = place(2, C, SLOTS)
    EO = place(C, HEADS * SLOTS)
    PS = place(C, HEADS * SLOTS)
    pe3 = place(C, HEADS)
    coef = place(2, C, HEADS)
    nb = place(2, SLOTS)
    L = place(2, HEADS, SLOTS)
    E = place(2, HEADS, SLOTS)
    mx = place(HEADS)
    den = place(HEADS)
    hb = place(2, P)
    supT = place(2, K4, P)
    psS = ps("psS", [P, K4 * P], F32, ctx)
    psL = ps("psL3", [P, HEADS * SLOTS], F32, ctx)
    psP = ps("psP3", [P, C * HEADS * SLOTS], F32, ctx)

    s_h = [sem(f"s_h3{b}", ctx) for b in range(2)]
    s_gath = [sem(f"s_gath3{q}", ctx) for q in range(4)]
    names = ("s_rec3", "s_onehot", "s_eo", "s_l3", "s_lgt", "s_p", "s_pn", "s_pe3", "s_coef", "s_sup", "s_supc",
             "s_s3", "s_cf", "s_stored", "s_mid3", "s_dist3", "s_near", "s_ch4")
    (s_rec, s_hot, s_eo, s_l, s_lgt, s_p, s_pn, s_pe, s_coef, s_sup, s_supc,
     s_s3, s_cf, s_stored, s_mid, s_dist, s_near, s_ch) = (sem(n, ctx) for n in names)
    s_gv, s_gp, s_ga, s_gt, s_gs = m["gates"]
    gru = Gru("", ctx, place, ps, sem, m, w, hb, supT, s_h, s_supc)
    s_res = gru.s_res
    block = ctx.enter_context(nc.Block())

    @block.sync
    def _(sp):
        def store(g):
            sp.wait_ge(gru.s_out, 4 * g + 4)
            sp.sem_inc(s_gs, 1)
            sp.dma_start(out[bass.ds(g * (4 * P), 4 * P), :].rearrange("(t p) c -> p t c", p=P),
                         w["H"][:, bass.ds(g * 4, 4), :]).then_inc(s_stored, 16)

        def step(t, q, h):
            if not over(t, NT):
                if not early(t, 2):
                    sp.wait_ge(s_res, t - 1)
                    sp.sem_inc(s_gs, 1)
                sp.dma_start(hb[:, q % 2, :], table_d[bass.ds(t * P, P), 0:P]).then_inc(s_h[q % 2], 16)
            if q == 2 and not early(t, 4):
                store(h - 1)
        all_steps_of_four(sp, step)
        store(NT // 4 - 1)
        sp.wait_ge(s_stored, 16 * (NT // 4))

    @block.gpsimd
    def _(pool):
        def gather(t, q, h):
            if over(t, NT):
                return
            pool.wait_ge(s_rec, t + 1)
            pool.sem_inc(s_gp, 1)
            for c in range(C):
                last = pool.tensor_scalar(R[:, q, c, :], m["iota"][:, 0:P], rec[:, q, RROW, c:c + 1], None,
                                          ALU.is_equal)
            last.then_inc(s_hot, 1)
            if not early(t, 4):
                pool.wait_ge(s_sup, t - 3)
                pool.sem_inc(s_gp, 1)
            for c in range(C):
                pool.indirect_dma_start(G[:, q, c, :], None, table_d[:, :],
                                        bass.IndirectOffsetOnAxis(ap=idx[:, q, c:c + 1], axis=0))\
                    .then_inc(s_gath[q], 16)
            if not early(t, 4):
                gru.power(pool, t - 4, q % 2)
        all_steps_of_four(pool, gather)
        for t in range(NT - 4, NT):
            gru.power(pool, t, t % 2)

    @block.vector
    def _(dve):
        ch = Chain(dve, s_ch)

        def list_edges(t, q):
            if not early(t, 4):
                dve.wait_ge(s_s3, t - 3)
                dve.sem_inc(s_gv, 1)
            ch.link(dve.tensor_copy(recs[:, q, :], m["rec_all"][:, t, :]))
            dve.tensor_scalar(idx[:, q, :], rec[:, q, RKEY, :], -1.0, 0.0, ALU.add, ALU.max).then_inc(s_rec, 1)

        def list_rows(t, q, b, part):
            if part == 0:
                dve.tensor_copy(rows[:, b, 1:2], m["ends"][:, bass.ds(t, 1)])
                ch.mark(dve.tensor_scalar(rows[:, b, 2:3], m["cnt"][:, bass.ds(t, 1)], 0.5, None, ALU.mult))
                return
            ch.wait()
            if part == 1:
                dve.scalar_tensor_tensor(rows[:, b, 0:1], rows[:, b, 2:3], 0.5, rows[:, b, 1:2],
                                         ALU.add, ALU.subtract).then_inc(s_mid, 1)
                dve.tensor_scalar(nb[:, b, :], m["halves"][:, :], rows[:, b, 2:3], None, ALU.is_lt)
                ch.mark(dve.tensor_tensor(slot[:, b, :, :], spread(m["iota"][:, 1:SLOTS + 1], 1, [P, C, SLOTS]),
                                          spread(rec[:, q, RSLOT, :], 2, [P, C, SLOTS]), ALU.is_equal))
            elif part == 2:
                ch.mark(dve.tensor_scalar(nb[:, b, :], nb[:, b, :], -1.0, BIG, ALU.add, ALU.mult))

        def near_edges(t, b):
            dve.wait_ge(s_dist, t + 1)
            dve.sem_inc(s_gv, 1)
            dve.tensor_scalar(Q[:, b, :], Q[:, b, :], rows[:, b, 2:3], None, ALU.is_lt).then_inc(s_near, 1)

        def edge_logits(t, q, h, b, k):
            if k == 0:
                dve.wait_ge(s_gath[q], 16 * C * (h + 1))
                if not early(t, 1):
                    dve.wait_ge(s_l, t)
                dve.sem_inc(s_gv, 1)
            last = dve.tensor_tensor(EO[:, :, k * SLOTS:(k + 1) * SLOTS], slot[:, b, :, :],
                                     G[:, q, :, P + k:P + k + 1].broadcast_to([P, C, SLOTS]), ALU.mult)
            if k == HEADS - 1:
                last.then_inc(s_eo, 1)

        def row_max(t, b, part):
            shape = [P, HEADS, SLOTS]
            if part == 0:
                dve.wait_ge(s_l, t + 1)
                dve.sem_inc(s_gv, 1)
                ch.mark(dve.tensor_tensor(L[:, b, :, :], psL[:, :].rearrange("p (k s) -> p k s", s=SLOTS),
                                          spread(nb[:, b, :], 1, shape), ALU.add))
                return
            ch.wait()
            if part == 1:
                ch.mark(dve.tensor_reduce(mx[:, :], L[:, b, :, :], AX, ALU.max))
            elif part == 2:
                dve.tensor_tensor(L[:, b, :, :], L[:, b, :, :], spread(mx[:, :], 2, shape), ALU.subtract)\
                    .then_inc(s_lgt, 1)

        def row_sum(t, b, part):
            if part == 0:
                dve.wait_ge(s_p, t + 1)
                dve.sem_inc(s_gv, 1)
                ch.mark(dve.tensor_reduce(den[:, :], E[:, b, :, :], AX, ALU.add))
                return
            ch.wait()
            if part == 1:
                ch.mark(dve.reciprocal(den[:, :], den[:, :]))
            elif part == 2:
                dve.tensor_tensor(E[:, b, :, :], E[:, b, :, :], spread(den[:, :], 2, [P, HEADS, SLOTS]), ALU.mult)\
                    .then_inc(s_pn, 1)

        def coefficients(t, q, b, part):
            if part == 0:
                dve.wait_ge(s_pe, t + 1)
                if not early(t, 2):
                    dve.wait_ge(s_sup, t - 1)
                    dve.wait_ge(s_s3, t - 1)
                dve.wait_ge(s_hot, t + 1)
                dve.sem_inc(s_gv, 1)
                pp = psP[:, :].rearrange("p (c y) -> p c y", y=HEADS * SLOTS)
                for k in range(HEADS):
                    last = dve.tensor_tensor(PS[:, :, k * SLOTS:(k + 1) * SLOTS],
                                             pp[:, :, k * SLOTS:(k + 1) * SLOTS], slot[:, b, :, :], ALU.mult)
                ch.mark(last)
                return
            ch.wait()
            if part == 1:
                ch.mark(dve.tensor_reduce(pe3[:, :, :], PS[:, :, :].rearrange("p c (k s) -> p c k s", s=SLOTS),
                                          AX, ALU.add))
            elif part == 2:
                ch.mark(dve.tensor_tensor(coef[:, b, :, :], pe3[:, :, :],
                                          spread(rec[:, q, RVAL, :], 2, [P, C, HEADS]), ALU.mult))
            elif part == 3:
                dve.sem_inc(s_cf, 1)
                for c in range(C):
                    last = dve.tensor_tensor(S[:, b, c, P:HEADS * P].rearrange("p (k i) -> p k i", i=P),
                                             spread(R[:, q, c, :], 1, [P, HEADS - 1, P]),
                                             spread(coef[:, b, c, 0:HEADS - 1], 2, [P, HEADS - 1, P]), ALU.mult)
                last.then_inc(s_coef, 1)

        def step(t, q, h):
            b = q % 2
            a = 1 - b
            now, after, before = not over(t, NT), not over(t, NT - 1), not early(t, 2)
            nq, nh = (q + 1) % 4, h + (q + 1) // 4
            landed = 16 * (2 * h + q // 2)
            ch.restart()
            for part in range(3):
                if now:
                    row_max(t, b, part)
                if before and part < 2:
                    gru.n_input(dve, ch, t - 2, b, part)
            if after:
                list_rows(t + 1, nq, a, 0)
                list_rows(t + 1, nq, a, 1)
            for part in range(3):
                if now:
                    row_sum(t, b, part)
                if after and part == 0:
                    list_rows(t + 1, nq, a, 2)
            for part in range(3):
                if before:
                    gru.blend(dve, ch, t - 2, b, landed, part)
                if after:
                    edge_logits(t + 1, nq, nh, a, part)
            if before:
                gru.blend(dve, ch, t - 2, b, landed, 3)
            if not early(t, 3):
                gru.normalise(dve, t - 3, a)
            if before:
                gru.blend(dve, ch, t - 2, b, landed, 4)
            for part in range(3):
                if now:
                    coefficients(t, q, b, part)
                if before:
                    gru.blend(dve, ch, t - 2, b, landed, 5 + part)
            if now:
                coefficients(t, q, b, 3)
            if after:
                near_edges(t + 1, a)
            if not over(t, NT - 3):
                list_edges(t + 3, (q + 3) % 4)

        for t in range(3):
            list_edges(t, t)
        for part in range(3):
            list_rows(0, 0, 0, part)
        near_edges(0, 0)
        ch.wait()
        for k in range(HEADS):
            edge_logits(0, 0, 0, 0, k)
        all_steps_of_four(dve, step, 4)
        gru.normalise(dve, NT - 1, 1)

    @block.scalar
    def _(act):
        def node_sum(t, q, b):
            act.wait_ge(s_hot, t + 1)
            if not early(t, 2):
                act.wait_ge(s_sup, t - 1)
            act.sem_inc(s_ga, 1)
            for c in range(C):
                act.activation(S[:, b, c, 0:P], R[:, q, c, :], ACT.Copy, scale=rec[:, q, RVAL, c:c + 1])

        def last_head(t, q, b):
            act.wait_ge(s_cf, t + 1)
            act.sem_inc(s_ga, 1)
            for c in range(C):
                last = act.activation(S[:, b, c, HEADS * P:K4 * P], R[:, q, c, :], ACT.Copy,
                                      scale=coef[:, b, c, HEADS - 1:HEADS])
            last.then_inc(s_s3, 1)

        def distances(t, b):
            act.wait_ge(s_mid, t + 1)
            act.sem_inc(s_ga, 1)
            act.activation(Q[:, b, :], m["iota"][:, :], ACT.Abs, bias=rows[:, b, 0:1]).then_inc(s_dist, 1)

        def step(t, q, h):
            b = q % 2
            if not over(t, NT):
                act.wait_ge(s_lgt, t + 1)
                act.sem_inc(s_ga, 1)
                act.activation(E[:, b, :, :], L[:, b, :, :], ACT.Exp).then_inc(s_p, 1)
            if not early(t, 2):
                gru.tanh_n(act, t - 2, b)
            if not over(t, NT):
                node_sum(t, q, b)
            if not over(t, NT - 1):
                distances(t + 1, 1 - b)
            if not (early(t, 1) or over(t, NT + 1)):
                act.wait_ge(s_sup, t)
                act.sem_inc(s_ga, 1)
                act.activation(supT[:, 1 - b, :, :].rearrange("p k i -> p (k i)"), psS[:, :], ACT.Copy)\
                    .then_inc(s_supc, 1)
                gru.copy_h(act, t - 1, 1 - b)
                gru.copy_support(act, t - 1, 1 - b)
            if not over(t, NT):
                last_head(t, q, b)
            if not (early(t, 1) or over(t, NT + 1)):
                gru.tanh_rz(act, t - 1, 1 - b)
        distances(0, 0)
        all_steps_of_four(act, step, 4)

    @block.tensor
    def _(pe):
        def step(t, q, h):
            b = q % 2
            a = 1 - b
            second = not (early(t, 1) or over(t, NT + 1))
            if not over(t, NT):
                pe.wait_ge(s_eo, t + 1)
                pe.wait_ge(s_hot, t + 1)
                pe.sem_inc(s_gt, 1)
                for c in range(C):
                    last = pe.matmul(psL[:, :], R[:, q, c, :], EO[:, c, :],
                                     start=(c == 0), stop=(c == C - 1))
                last.then_inc(s_l, 1)
            if second:
                pe.wait_ge(s_s3, t)
                pe.wait_ge(s_coef, t)
                if not early(t, 2):
                    pe.wait_ge(s_supc, t - 1)
                pe.sem_inc(s_gt, 1)
                for c in range(C):
                    last = pe.matmul(psS[:, :], G[:, (q + 3) % 4, c, 0:P], S[:, a, c, :],
                                     start=(c == 0), stop=(c == C - 1))
                last.then_inc(s_sup, 1)
                gru.turn_h(pe, t - 1, a, 16 * (2 * h + q // 2 + b))
            if not over(t, NT):
                pe.wait_ge(s_pn, t + 1)
                pe.wait_ge(s_near, t + 1)
                pe.sem_inc(s_gt, 1)
                for c in range(C):
                    last = pe.matmul(psP[:, c * HEADS * SLOTS:(c + 1) * HEADS * SLOTS], Q[:, b, c * P:(c + 1) * P],
                                     E[:, b, :, :].rearrange("p k s -> p (k s)"), start=True, stop=True)
                last.then_inc(s_pe, 1)
            if second:
                gru.support(pe, t - 1, a)
                gru.from_h(pe, t - 1, a, None if early(t, 3) else t - 2)
                gru.from_supports(pe, t - 1, a)
        all_steps_of_four(pe, step)


def tile_by_tile(eng, step):
    step(0)
    with eng.Fori(1, NT) as t:
        step(t)


class DenseSum:

    def __init__(self, tag, ctx, place, ps, sem, m, s_ga, s_gt):
        self.m, self.s_ga, self.s_gt = m, s_ga, s_gt
        self.T = place(4, P)
        self.psT = ps("psT_" + tag, [P, 4, P], F32, ctx)
        self.s_turned = sem("s_turned_" + tag, ctx)
        self.s_copied = sem("s_copied_" + tag, ctx)

    def turn(self, pe, src, n, multiply):
        for c in range(NT // 4):
            for j in range(4):
                at = (4 * c + j) * P
                last = pe.transpose(self.psT[:, j, :], src[:, at:at + P], self.m["ident"][:, :])
            last.then_inc(self.s_turned, 1)
            pe.wait_ge(self.s_copied, n * (NT // 4) + c + 1)
            pe.sem_inc(self.s_gt, 1)
            for j in range(4):
                last = multiply(4 * c + j, self.T[:, j, :], c + j == 0, 4 * c + j == NT - 1)
        return last

    def copy(self, act, n):
        for c in range(NT // 4):
            act.wait_ge(self.s_turned, n * (NT // 4) + c + 1)
            act.sem_inc(self.s_ga, 1)
            act.activation(self.T[:, :, :], self.psT[:, :, :], ACT.Copy).then_inc(self.s_copied, 1)


def weights_dense(nc, ctx, sb, ps, sem, m, x_d, adj_d):
    place = carve(m["maskT"][:, :, :].rearrange("p a b -> p (a b)"))
    A, B, X = place(N), place(N), place(NT, P)
    s_x, s_a, s_q, s_e, s_wt, s_sum, s_y, s_ch = (
        sem(n + "_wd", ctx) for n in ("x", "a", "q", "e", "wt", "sum", "y", "ch"))
    s_gv, s_gp, s_ga, s_gt, s_gs = m["gates"]
    ds = DenseSum("wd", ctx, place, ps, sem, m, s_ga, s_gt)
    psY = ps("psY_d", [P, 512], F32, ctx)
    block = ctx.enter_context(nc.Block())

    @block.gpsimd
    def _(pool):
        pool.dma_start(X[:, :, :], x_d.rearrange("(t p) c -> p t c", p=P)).then_inc(s_x, 16)

    @block.sync
    def _(sp):
        def load(t):
            if not early(t, 1):
                sp.wait_ge(s_y, t)
                sp.sem_inc(s_gs, 1)
            sp.dma_start(A[:, :], adj_d[bass.ds(t * P, P), :]).then_inc(s_a, 16)
        tile_by_tile(sp, load)

    @block.vector
    def _(dve):
        ch = Chain(dve, s_ch)

        def weigh(t):
            ch.restart()
            dve.wait_ge(s_a, 16 * (t + 1))
            dve.sem_inc(s_gv, 1)
            ch.link(dve.tensor_scalar(B[:, :], A[:, :], 0.0, 2.0, ALU.is_equal, ALU.mult))
            ch.link(dve.tensor_tensor(A[:, :], A[:, :], B[:, :], ALU.add))
            ch.link(dve.reciprocal(B[:, :], A[:, :]))
            ch.link(dve.tensor_scalar(B[:, :], B[:, :], -1.0, None, ALU.add))
            dve.tensor_tensor(B[:, :], B[:, :], B[:, :], ALU.mult).then_inc(s_q, 1)
            dve.wait_ge(s_e, t + 1)
            dve.sem_inc(s_gv, 1)
            ch.link(dve.scalar_tensor_tensor(A[:, :], A[:, :], 1.0, B[:, :], ALU.is_lt, ALU.mult))
            ch.link(dve.tensor_reduce(m["wsum"][:, bass.ds(t, 1)], A[:, :], AX, ALU.add))
            dve.sem_inc(s_wt, 1)
        tile_by_tile(dve, weigh)

    @block.scalar
    def _(act):
        def step(t):
            act.wait_ge(s_q, t + 1)
            act.sem_inc(s_ga, 1)
            act.activation(B[:, :], B[:, :], ACT.Exp, scale=-2.0).then_inc(s_e, 1)
            ds.copy(act, t)
            act.wait_ge(s_sum, t + 1)
            act.sem_inc(s_ga, 1)
            act.activation(m["yT"][:, t, :], psY[:, 0:P], ACT.Copy).then_inc(s_y, 1)
        tile_by_tile(act, step)

    @block.tensor
    def _(pe):
        pe.wait_ge(s_x, 16)

        def step(t):
            pe.wait_ge(s_wt, t + 1)
            if not early(t, 1):
                pe.wait_ge(s_y, t)
            pe.sem_inc(s_gt, 1)
            ds.turn(pe, A, t, lambda j, block_t, first, last: pe.matmul(
                psY[:, 0:P], X[:, j, :], block_t, start=first, stop=last)).then_inc(s_sum, 1)
        tile_by_tile(pe, step)


def logits_dense(nc, ctx, sb, ps, sem, m, w, adj_d, logit_d):
    place = carve(m["maskT"][:, :, :].rearrange("p a b -> p (a b)"))
    A, Mp, Mm = place(N), place(N), place(N)
    K2 = 2 * HEADS
    up, e6, l6 = place(2, K2), place(K2), place(K2)
    rows = place(N)
    s_a, s_m, s_u, s_e6, s_t, s_tc, s_out, s_ch = (
        sem(n + "_ld", ctx) for n in ("a", "m", "u", "e6", "t", "tc", "out", "ch"))
    s_gv, s_gp, s_ga, s_gt, s_gs = m["gates"]
    ds = DenseSum("ld", ctx, place, ps, sem, m, s_ga, s_gt)
    psU = ps("psU_d", [P, 2, 512], F32, ctx)
    psR = ps("psR_d", [P, 512], F32, ctx)
    block = ctx.enter_context(nc.Block())

    @block.sync
    def _(sp):
        def load(t):
            if not early(t, 1):
                sp.wait_ge(s_tc, t)
                sp.sem_inc(s_gs, 1)
            sp.dma_start(A[:, :], adj_d[bass.ds(t * P, P), :]).then_inc(s_a, 16)
        tile_by_tile(sp, load)
        sp.wait_ge(s_tc, NT)
        sp.dma_start(logit_d, rows[0:K2, :]).then_inc(s_out, 16)
        sp.wait_ge(s_out, 16)

    @block.vector
    def _(dve):
        ch = Chain(dve, s_ch)

        def step(t):
            ch.restart()
            dve.wait_ge(s_a, 16 * (t + 1))
            dve.sem_inc(s_gv, 1)
            blk = A[:, bass.ds(t * P, P)]
            ch.link(dve.tensor_tensor(blk, blk, m["offdiag"][:, :], ALU.mult))
            dve.tensor_scalar(Mp[:, :], A[:, :], 0.0, None, ALU.is_gt)
            dve.tensor_scalar(Mm[:, :], A[:, :], 0.0, None, ALU.is_lt).then_inc(s_m, 1)
            dve.wait_ge(s_u, t + 1)
            dve.sem_inc(s_gv, 1)
            ch.link(dve.tensor_copy(up[:, :, :], psU[:, :, 0:K2]))
            ch.link(dve.tensor_tensor(e6[:, 0:HEADS], up[:, 0, 0:HEADS], up[:, 1, HEADS:K2], ALU.add))
            ch.link(dve.tensor_tensor(e6[:, HEADS:K2], up[:, 1, 0:HEADS], up[:, 0, HEADS:K2], ALU.add))
            dve.scalar_tensor_tensor(l6[:, :], e6[:, :], 0.2, e6[:, :], ALU.mult, ALU.max).then_inc(s_e6, 1)
        tile_by_tile(dve, step)

    @block.scalar
    def _(act):
        def step(t):
            ds.copy(act, 2 * t)
            ds.copy(act, 2 * t + 1)
            act.wait_ge(s_t, t + 1)
            act.sem_inc(s_ga, 1)
            act.activation(rows[0:K2, bass.ds(t * P, P)], psR[0:K2, 0:P], ACT.Copy).then_inc(s_tc, 1)
        tile_by_tile(act, step)

    @block.tensor
    def _(pe):
        def step(t):
            pe.wait_ge(s_m, t + 1)
            pe.sem_inc(s_gt, 1)
            for n, mask in ((0, Mp), (1, Mm)):
                last = ds.turn(pe, mask, 2 * t + n, lambda j, block_t, first, last, n=n: pe.matmul(
                    psU[:, n, 0:K2], block_t, w["V"][:, j, :], start=first, stop=last))
            last.then_inc(s_u, 1)
            pe.wait_ge(s_e6, t + 1)
            if not early(t, 1):
                pe.wait_ge(s_tc, t)
            pe.sem_inc(s_gt, 1)
            pe.transpose(psR[0:K2, 0:P], l6[:, :], m["ident"][:, :]).then_inc(s_t, 1)
        tile_by_tile(pe, step)


def attention_dense(nc, ctx, sb, ps, sem, m, w, adj_d, table_d, logit_d, out):
    place = carve(m["maskT"][:, :, :].rearrange("p a b -> p (a b)"))
    K4 = HEADS + 1
    A, Mp, L, Ep, Em = (place(N) for _ in range(5))
    Mm = place(N)
    hall = place(NT, P)
    place = carve(m["yT"][:, :, :].rearrange("p a b -> p (a b)").bitcast(U8))
    hb = place(1, P)
    supT = place(1, K4, P)
    mx, den = place(1), place(1)
    psS = ps("psS_d", [P, K4, P], F32, ctx)
    s_all, s_h0, s_a, s_el, s_m, s_lk, s_lg, s_ex, s_s, s_sum, s_supc, s_stored, s_ch = (
        sem(n + "_ad", ctx) for n in ("all", "h0", "a", "el", "m", "lk", "lg", "ex", "s", "sum", "supc", "st", "ch"))
    s_gv, s_gp, s_ga, s_gt, s_gs = m["gates"]
    ds = DenseSum("ad", ctx, place, ps, sem, m, s_ga, s_gt)
    gru = Gru("d", ctx, place, ps, sem, m, w, hb, supT, [s_h0], s_supc)
    block = ctx.enter_context(nc.Block())

    @block.sync
    def _(sp):
        sp.dma_start(hall[:, :, :], table_d.rearrange("(t p) c -> p t c", p=P)[:, :, 0:P]).then_inc(s_all, 16)

        def load(t):
            if not early(t, 1):
                sp.wait_ge(gru.s_res, t)
                sp.sem_inc(s_gs, 1)
            sp.dma_start(A[:, :], adj_d[bass.ds(t * P, P), :]).then_inc(s_a, 16)
            sp.dma_start(hb[:, 0, :], table_d[bass.ds(t * P, P), 0:P]).then_inc(s_h0, 16)
            for k in range(HEADS):
                if not (isinstance(t, int) and k == 0):
                    sp.wait_ge(s_lk, HEADS * t + k)
                    sp.sem_inc(s_gs, 1)
                sp.dma_start(Ep[:, :], logit_d[k, :].partition_broadcast(P)).then_inc(s_el, 16)
                sp.dma_start(Em[:, :], logit_d[HEADS + k, :].partition_broadcast(P)).then_inc(s_el, 16)
        tile_by_tile(sp, load)
        sp.wait_ge(gru.s_out, NT)
        sp.dma_start(out.rearrange("(t p) c -> p t c", p=P), w["H"][:, :, :]).then_inc(s_stored, 16)
        sp.wait_ge(s_stored, 16)

    @block.gpsimd
    def _(pool):
        tile_by_tile(pool, lambda t: gru.power(pool, t, 0))

    @block.vector
    def _(dve):
        ch = Chain(dve, s_ch)

        def step(t):
            ch.restart()
            dve.wait_ge(s_a, 16 * (t + 1))
            dve.sem_inc(s_gv, 1)
            blk = A[:, bass.ds(t * P, P)]
            ch.link(dve.tensor_tensor(blk, blk, m["offdiag"][:, :], ALU.mult))
            dve.tensor_scalar(Mp[:, :], A[:, :], 0.0, None, ALU.is_gt)
            ch.link(dve.tensor_scalar(Mm[:, :], A[:, :], 0.0, None, ALU.is_lt))
            dve.sem_inc(s_m, 1)
            for k in range(HEADS):
                if k:
                    dve.wait_ge(s_sum, K4 * t + k + 1)
                dve.wait_ge(s_el, 32 * (HEADS * t + k + 1))
                dve.sem_inc(s_gv, 1)
                ch.link(dve.memset(L[:, :], -BIG))
                ch.link(dve.copy_predicated(L[:, :], Mp[:, :].bitcast(I32), Ep[:, :]))
                ch.link(dve.copy_predicated(L[:, :], Mm[:, :].bitcast(I32), Em[:, :]))
                dve.sem_inc(s_lk, 1)
                ch.link(dve.tensor_reduce(mx[:, :], L[:, :], AX, ALU.max))
                ch.link(dve.tensor_scalar(L[:, :], L[:, :], mx[:, :], None, ALU.subtract))
                dve.sem_inc(s_lg, 1)
                dve.wait_ge(s_ex, HEADS * t + k + 1)
                dve.sem_inc(s_gv, 1)
                ch.link(dve.reciprocal(den[:, :], den[:, :]))
                ch.link(dve.scalar_tensor_tensor(L[:, :], L[:, :], den[:, :], A[:, :], ALU.mult, ALU.mult))
                dve.sem_inc(s_s, 1)
            for part in range(2):
                gru.n_input(dve, ch, t, 0, part)
            for part in range(8):
                gru.blend(dve, ch, t, 0, 16 * (t + 1), part)
            gru.normalise(dve, t, 0)
        tile_by_tile(dve, step)

    @block.scalar
    def _(act):
        def step(t):
            gru.copy_h(act, t, 0)
            ds.copy(act, K4 * t)
            for k in range(HEADS):
                act.wait_ge(s_lg, HEADS * t + k + 1)
                act.sem_inc(s_ga, 1)
                act.activation(L[:, :], L[:, :], ACT.Exp, accum_out=den[:, :]).then_inc(s_ex, 1)
                ds.copy(act, K4 * t + k + 1)
            act.wait_ge(s_sum, K4 * (t + 1))
            act.sem_inc(s_ga, 1)
            act.activation(supT[:, 0, :, :], psS[:, :, :], ACT.Copy).then_inc(s_supc, 1)
            gru.copy_support(act, t, 0)
            gru.tanh_rz(act, t, 0)
            gru.tanh_n(act, t, 0)
        tile_by_tile(act, step)

    @block.tensor
    def _(pe):
        pe.wait_ge(s_all, 16)

        def step(t):
            gru.turn_h(pe, t, 0, 16 * (t + 1))
            for k in range(K4):
                if k == 0:
                    pe.wait_ge(s_m, t + 1)
                else:
                    pe.wait_ge(s_s, HEADS * t + k)
                pe.sem_inc(s_gt, 1)
                ds.turn(pe, L if k else A, K4 * t + k, lambda j, block_t, first, last, k=k: pe.matmul(
                    psS[:, k, :], hall[:, j, :], block_t, start=first, stop=last)).then_inc(s_sum, 1)
            gru.support(pe, t, 0)
            gru.from_h(pe, t, 0, None if early(t, 1) else t)
            gru.from_supports(pe, t, 0)
        tile_by_tile(pe, step)


NAMES = ["x", "adj", "L0_gnn_W", "L0_gnn_B", "L1_gnn_gat_W", "L1_gnn_gat_a", "L1_gnn_edge_Wih", "L1_gnn_edge_Whh",
         "L1_gnn_edge_bih", "L1_gnn_edge_bhh", "L1_gnn_node_Wih", "L1_gnn_node_Whh", "L1_gnn_node_bih",
         "L1_gnn_node_bhh"]


def kernel(**inputs):
    import numpy as _np
    import concourse.bacc as _bacc
    from concourse.bass_utils import run_bass_kernel_spmd as _run

    nc = _bacc.Bacc("TRN2", target_bir_lowering=False, num_devices=1)
    arrays, tensors = {}, {}
    for name in NAMES:
        a = _np.ascontiguousarray(inputs[name])
        arrays[f"in_{name}"] = a
        tensors[name] = nc.dram_tensor(f"in_{name}", a.shape, mybir.dt.from_np(a.dtype), kind="ExternalInput").ap()
    out = nc.dram_tensor("out", (N, P), F32, kind="ExternalOutput").ap()
    build(nc, tensors, out)
    result = _run(nc, [arrays], core_ids=[0])
    return result.results[0]["out"]
```
